# Optimizing a Trainium2 kernel written in Bass

```python
import numpy as np
import jax
import jax.numpy as jnp

def _softmax(x, axis=-1):
    return jax.nn.softmax(x, axis=axis)

def _gelu(x):
    return jax.nn.gelu(x, approximate=True)

def _silu(x):
    return jax.nn.silu(x)

def _sigmoid(x):
    return jax.nn.sigmoid(x)

def _layernorm(x, axis=-1, eps=1e-05):
    m = jnp.mean(x, axis=axis, keepdims=True)
    v = jnp.var(x, axis=axis, keepdims=True)
    return (x - m) / jnp.sqrt(v + eps)

def _scatter_add(tgt, idx, src, axis=0):
    return tgt.at[idx].add(src)

def _segment_sum(src, seg, n):
    return jax.ops.segment_sum(src, seg, n)
kernel_name = 'mk_gnn_resnorm_d4_gnn_r8_a7221d'

def setup_inputs(seed: int=0):
    np.random.seed(seed)
    _w = jnp.asarray

    def _rec_inputs():
        import jax
        import jax.numpy as jnp
        _gk = jax.random.key(seed)
        x = -0.0003713 + 1 * jax.random.normal(jax.random.fold_in(_gk, 1), (6250, 128), jnp.float32)
        _s = jax.random.randint(jax.random.fold_in(_gk, 2), (50000,), 0, 6250, jnp.int32)
        _d = jax.random.randint(jax.random.fold_in(_gk, 3), (50000,), 0, 6250, jnp.int32)
        _loop = jnp.arange(6250, dtype=jnp.int32)
        src = jnp.concatenate([_s, _d, _loop])
        dst = jnp.concatenate([_d, _s, _loop])
        _o = jnp.argsort(dst, stable=True)
        src = src[_o]
        dst = dst[_o]
        edge_attr_128 = -2.25437e-05 + 0.999858 * jax.random.normal(jax.random.fold_in(_gk, 12), (106250, 128), jnp.float32)
        edge_attr_32 = 0.000283511 + 1.00007 * jax.random.normal(jax.random.fold_in(_gk, 13), (106250, 32), jnp.float32)
        edge_type_2 = jax.random.randint(jax.random.fold_in(_gk, 16), (106250,), 0, 2, jnp.int32)
        edge_weight = jax.random.uniform(jax.random.fold_in(_gk, 17), (106250,), jnp.float32, 0.0, 0.999998)
        return (x, src, dst, edge_attr_128, edge_attr_32, edge_type_2, edge_weight)
    x, src, dst, edge_attr_128, edge_attr_32, edge_type_2, edge_weight = _rec_inputs()

    def _L0_gnn_setup():
        import jax, jax.numpy as jnp
        import numpy as np
        N_NODES = 12500
        N_EDGES = 400000
        D = 128
        key = jax.random.key(seed)
        k1, k2, k3 = jax.random.split(key, 3)
        x = jax.random.normal(k1, (N_NODES, D), dtype=jnp.float32)
        edge_index = jax.random.randint(k2, (2, N_EDGES), 0, N_NODES, dtype=jnp.int64)
        W = jax.random.normal(k3, (D, D), dtype=jnp.float32) / np.sqrt(D)
        b = jnp.zeros((D,), dtype=jnp.float32)
        return {'x': x, 'edge_index': edge_index, 'W': W, 'b': b}
    _L0_gnn_all = _L0_gnn_setup()
    _L0_gnn_in = {k: v for k, v in _L0_gnn_all.items() if k in ('W', 'b')}
    del _L0_gnn_all

    def _L1_gnn_setup():
        import jax, jax.numpy as jnp
        import numpy as np
        N_NODES = 6250
        N_EDGES = 62500
        D_FEAT = 128
        key = jax.random.key(seed)
        k1, k2, k3 = jax.random.split(key, 3)
        r = jax.random.normal(k1, (N_NODES, D_FEAT), dtype=jnp.float32)
        e = jax.random.normal(k2, (N_EDGES, D_FEAT), dtype=jnp.float32)
        a = jax.random.randint(k3, (N_EDGES, 2), 0, N_NODES, dtype=jnp.int64)
        return {'r': r, 'e': e, 'a': a}
    _L1_gnn_all = _L1_gnn_setup()
    _L1_gnn_in = {k: v for k, v in _L1_gnn_all.items() if k in ()}
    del _L1_gnn_all

    def _L2_gnn_setup():
        import jax, jax.numpy as jnp
        import numpy as np
        N, E = (6250, 100000)
        D, H = (128, 8)
        DH = D // H
        DFF = 2 * D
        EPS_BN = 1e-05

        def _batch_norm(x, g, b):
            mu = jnp.mean(x, axis=0)
            var = jnp.mean((x - mu) ** 2, axis=0)
            return (x - mu) * jax.lax.rsqrt(var + EPS_BN) * g + b
        key = jax.random.key(seed)
        ks = jax.random.split(key, 12)
        s = 1.0 / np.sqrt(D)
        inp = {'h': jax.random.normal(ks[0], (N, D), dtype=jnp.float32), 'src': jax.random.randint(ks[1], (E,), 0, N, dtype=jnp.int32), 'dst': jax.random.randint(ks[2], (E,), 0, N, dtype=jnp.int32), 'Wq': jax.random.normal(ks[3], (D, D), dtype=jnp.float32) * s, 'Wk': jax.random.normal(ks[4], (D, D), dtype=jnp.float32) * s, 'Wv': jax.random.normal(ks[5], (D, D), dtype=jnp.float32) * s, 'Wo': jax.random.normal(ks[6], (D, D), dtype=jnp.float32) * s, 'bo': jnp.zeros((D,), dtype=jnp.float32), 'W1': jax.random.normal(ks[7], (D, DFF), dtype=jnp.float32) * s, 'b1': jnp.zeros((DFF,), dtype=jnp.float32), 'W2': jax.random.normal(ks[8], (DFF, D), dtype=jnp.float32) * (1.0 / np.sqrt(DFF)), 'b2': jnp.zeros((D,), dtype=jnp.float32), 'bn1_g': jnp.ones((D,), dtype=jnp.float32), 'bn1_b': jnp.zeros((D,), dtype=jnp.float32), 'bn2_g': jnp.ones((D,), dtype=jnp.float32), 'bn2_b': jnp.zeros((D,), dtype=jnp.float32)}
        return inp
    _L2_gnn_all = _L2_gnn_setup()
    _L2_gnn_in = {k: v for k, v in _L2_gnn_all.items() if k in ('Wq', 'Wk', 'Wv', 'Wo', 'bo', 'W1', 'b1', 'W2', 'b2', 'bn1_g', 'bn1_b', 'bn2_g', 'bn2_b')}
    del _L2_gnn_all

    def _L3_gnn_setup():
        import jax, jax.numpy as jnp
        import numpy as np
        N = 12500
        E = 75000
        D = 128
        H = 8
        DH = D // H
        T = 32
        NET = 2

        def _ln(x, g, b, eps=1e-05):
            mu = jnp.mean(x, axis=-1, keepdims=True)
            var = jnp.mean((x - mu) ** 2, axis=-1, keepdims=True)
            return (x - mu) * jax.lax.rsqrt(var + eps) * g + b

        def _expmap(e, c):
            abs_c = jnp.maximum(jnp.abs(c), 1e-15)
            sq = jnp.sqrt(abs_c)
            n = jnp.maximum(jnp.linalg.norm(e, axis=-1, keepdims=True), 1e-15)
            tanh_p = jnp.tanh(sq * n) * e / (sq * n)
            tan_p = jnp.tan(sq * n) * e / (sq * n)
            return jnp.where(c < 0, tanh_p, tan_p)

        def _proj(x, c, eps=1e-05):
            abs_c = jnp.maximum(jnp.abs(c), 1e-15)
            maxnorm = (1.0 - eps) / jnp.sqrt(abs_c)
            norm = jnp.linalg.norm(x, axis=-1, keepdims=True)
            scale = jnp.where(norm > maxnorm, maxnorm / norm, jnp.ones_like(norm))
            return x * scale

        def _forward(x, time_emb, edge_time, Wq, Wk, Wv, rel_q, rel_k, rel_v, Wt, bt, Wd1, bd1, Wd2, bd2, decay_scale, c_mag, hyp_beta, logit_alpha, Wo, bo, g1, be1, g2, be2, Wf1, bf1, Wf2, bf2, src, dst, edge_type):
            n = x.shape[0]
            Q = (x @ Wq).reshape(n, H, DH)
            K = (x @ Wk).reshape(n, H, DH)
            V = (x @ Wv).reshape(n, H, DH)
            q_dst = Q[dst] + rel_q[edge_type].reshape(-1, H, DH)
            k_src = K[src] + rel_k[edge_type].reshape(-1, H, DH)
            v_src = V[src] + rel_v[edge_type].reshape(-1, H, DH)
            k_src = k_src + (time_emb @ Wt + bt).reshape(-1, H, DH)
            euclid = jnp.sum(q_dst * k_src, axis=-1) / np.float32(np.sqrt(DH))
            denom_t = jnp.maximum(1.0, edge_type.max().astype(jnp.float32) + 1.0)
            et = edge_type.astype(jnp.float32)[:, None] / denom_t
            dec_in = jnp.concatenate([edge_time[:, None], et], axis=-1)
            decay_raw = jnp.tanh(jax.nn.relu(dec_in @ Wd1 + bd1) @ Wd2 + bd2)
            decay = jnp.exp(decay_scale[None, :] * decay_raw)
            euclid = euclid * decay
            c = -jnp.abs(c_mag)
            m = _proj(_expmap(x, c), c)
            man_dist = jnp.linalg.norm(m[src] - m[dst], axis=-1)[:, None]
            hyp = -hyp_beta[None, :] * man_dist * decay
            alpha = jax.nn.sigmoid(logit_alpha)[None, :]
            logits = alpha * euclid + (1.0 - alpha) * hyp
            seg_max = jax.ops.segment_max(logits, dst, num_segments=n)
            ex = jnp.exp(logits - seg_max[dst])
            denom = jax.ops.segment_sum(ex, dst, num_segments=n)
            attn = ex / denom[dst]
            agg = jax.ops.segment_sum(v_src * attn[..., None], dst, num_segments=n).reshape(n, D)
            out = agg @ Wo + bo
            x = _ln(x + out, g1, be1)
            ffn = jax.nn.gelu(x @ Wf1 + bf1, approximate=False) @ Wf2 + bf2
            x = _ln(x + ffn, g2, be2)
            return x
        key = jax.random.key(seed)
        ks = jax.random.split(key, 20)

        def lin(k, fi, fo):
            return jax.random.normal(k, (fi, fo), jnp.float32) / np.float32(np.sqrt(fi))
        return {'x': jax.random.normal(ks[0], (N, D), jnp.float32), 'edge_index': jax.random.randint(ks[1], (2, E), 0, N), 'time_emb': jax.random.normal(ks[2], (E, T), jnp.float32), 'edge_type': jax.random.randint(ks[3], (E,), 0, NET), 'edge_time': jax.random.uniform(ks[4], (E,), jnp.float32), 'Wq': lin(ks[5], D, D), 'Wk': lin(ks[6], D, D), 'Wv': lin(ks[7], D, D), 'rel_q': jax.random.normal(ks[8], (NET, D), jnp.float32) * 0.1, 'rel_k': jax.random.normal(ks[9], (NET, D), jnp.float32) * 0.1, 'rel_v': jax.random.normal(ks[10], (NET, D), jnp.float32) * 0.1, 'Wt': lin(ks[11], T, D), 'bt': jnp.zeros((D,), jnp.float32), 'Wd1': lin(ks[12], 2, 64), 'bd1': jnp.zeros((64,), jnp.float32), 'Wd2': lin(ks[13], 64, H), 'bd2': jnp.zeros((H,), jnp.float32), 'decay_scale': jnp.full((H,), 0.5, jnp.float32), 'c_mag': jnp.asarray(1.0, jnp.float32), 'hyp_beta': jnp.ones((H,), jnp.float32), 'logit_alpha': jnp.zeros((H,), jnp.float32), 'Wo': lin(ks[14], D, D), 'bo': jnp.zeros((D,), jnp.float32), 'g1': jnp.ones((D,), jnp.float32), 'be1': jnp.zeros((D,), jnp.float32), 'g2': jnp.ones((D,), jnp.float32), 'be2': jnp.zeros((D,), jnp.float32), 'Wf1': lin(ks[15], D, 4 * D), 'bf1': jnp.zeros((4 * D,), jnp.float32), 'Wf2': lin(ks[16], 4 * D, D), 'bf2': jnp.zeros((D,), jnp.float32)}
    _L3_gnn_all = _L3_gnn_setup()
    _L3_gnn_in = {k: v for k, v in _L3_gnn_all.items() if k in ('Wq', 'Wk', 'Wv', 'rel_q', 'rel_k', 'rel_v', 'Wt', 'bt', 'Wd1', 'bd1', 'Wd2', 'bd2', 'decay_scale', 'c_mag', 'hyp_beta', 'logit_alpha', 'Wo', 'bo', 'g1', 'be1', 'g2', 'be2', 'Wf1', 'bf1', 'Wf2', 'bf2')}
    del _L3_gnn_all
    return {'x': x, 'src': src, 'dst': dst, 'edge_attr_128': edge_attr_128, 'edge_attr_32': edge_attr_32, 'edge_type_2': edge_type_2, 'edge_weight': edge_weight, 'L0_gnn_W': _L0_gnn_in['W'], 'L0_gnn_b': _L0_gnn_in['b'], 'L2_gnn_Wq': _L2_gnn_in['Wq'], 'L2_gnn_Wk': _L2_gnn_in['Wk'], 'L2_gnn_Wv': _L2_gnn_in['Wv'], 'L2_gnn_Wo': _L2_gnn_in['Wo'], 'L2_gnn_bo': _L2_gnn_in['bo'], 'L2_gnn_W1': _L2_gnn_in['W1'], 'L2_gnn_b1': _L2_gnn_in['b1'], 'L2_gnn_W2': _L2_gnn_in['W2'], 'L2_gnn_b2': _L2_gnn_in['b2'], 'L2_gnn_bn1_g': _L2_gnn_in['bn1_g'], 'L2_gnn_bn1_b': _L2_gnn_in['bn1_b'], 'L2_gnn_bn2_g': _L2_gnn_in['bn2_g'], 'L2_gnn_bn2_b': _L2_gnn_in['bn2_b'], 'L3_gnn_Wq': _L3_gnn_in['Wq'], 'L3_gnn_Wk': _L3_gnn_in['Wk'], 'L3_gnn_Wv': _L3_gnn_in['Wv'], 'L3_gnn_rel_q': _L3_gnn_in['rel_q'], 'L3_gnn_rel_k': _L3_gnn_in['rel_k'], 'L3_gnn_rel_v': _L3_gnn_in['rel_v'], 'L3_gnn_Wt': _L3_gnn_in['Wt'], 'L3_gnn_bt': _L3_gnn_in['bt'], 'L3_gnn_Wd1': _L3_gnn_in['Wd1'], 'L3_gnn_bd1': _L3_gnn_in['bd1'], 'L3_gnn_Wd2': _L3_gnn_in['Wd2'], 'L3_gnn_bd2': _L3_gnn_in['bd2'], 'L3_gnn_decay_scale': _L3_gnn_in['decay_scale'], 'L3_gnn_c_mag': _L3_gnn_in['c_mag'], 'L3_gnn_hyp_beta': _L3_gnn_in['hyp_beta'], 'L3_gnn_logit_alpha': _L3_gnn_in['logit_alpha'], 'L3_gnn_Wo': _L3_gnn_in['Wo'], 'L3_gnn_bo': _L3_gnn_in['bo'], 'L3_gnn_g1': _L3_gnn_in['g1'], 'L3_gnn_be1': _L3_gnn_in['be1'], 'L3_gnn_g2': _L3_gnn_in['g2'], 'L3_gnn_be2': _L3_gnn_in['be2'], 'L3_gnn_Wf1': _L3_gnn_in['Wf1'], 'L3_gnn_bf1': _L3_gnn_in['bf1'], 'L3_gnn_Wf2': _L3_gnn_in['Wf2'], 'L3_gnn_bf2': _L3_gnn_in['bf2']}

def reference(x, src, dst, edge_attr_128, edge_attr_32, edge_type_2, edge_weight, L0_gnn_W, L0_gnn_b, L2_gnn_Wq, L2_gnn_Wk, L2_gnn_Wv, L2_gnn_Wo, L2_gnn_bo, L2_gnn_W1, L2_gnn_b1, L2_gnn_W2, L2_gnn_b2, L2_gnn_bn1_g, L2_gnn_bn1_b, L2_gnn_bn2_g, L2_gnn_bn2_b, L3_gnn_Wq, L3_gnn_Wk, L3_gnn_Wv, L3_gnn_rel_q, L3_gnn_rel_k, L3_gnn_rel_v, L3_gnn_Wt, L3_gnn_bt, L3_gnn_Wd1, L3_gnn_bd1, L3_gnn_Wd2, L3_gnn_bd2, L3_gnn_decay_scale, L3_gnn_c_mag, L3_gnn_hyp_beta, L3_gnn_logit_alpha, L3_gnn_Wo, L3_gnn_bo, L3_gnn_g1, L3_gnn_be1, L3_gnn_g2, L3_gnn_be2, L3_gnn_Wf1, L3_gnn_bf1, L3_gnn_Wf2, L3_gnn_bf2):
    import jax
    import jax.numpy as jnp

    def _L0_gnn_ref(x, edge_index, W, b):
        import jax, jax.numpy as jnp
        import numpy as np
        N_NODES = 12500
        N_EDGES = 400000
        D = 128
        N = x.shape[0]
        loop = jnp.arange(N, dtype=edge_index.dtype)
        src = jnp.concatenate([edge_index[0], loop])
        dst = jnp.concatenate([edge_index[1], loop])
        deg = jax.ops.segment_sum(jnp.ones_like(dst, dtype=x.dtype), dst, num_segments=N)
        dinv = deg ** (-0.5)
        norm = dinv[src] * dinv[dst]
        h = x @ W
        msgs = h[src] * norm[:, None]
        out = jax.ops.segment_sum(msgs, dst, num_segments=N) + b
        return jax.nn.relu(out)

    def _L1_gnn_ref(r, e, a):
        import jax, jax.numpy as jnp
        import numpy as np
        N_NODES = 6250
        N_EDGES = 62500
        D_FEAT = 128
        rij = r[a[:, 0]] * e
        rji = r[a[:, 1]] * e
        out = jax.ops.segment_sum(rij, a[:, 1], num_segments=r.shape[0])
        out = out + jax.ops.segment_sum(rji, a[:, 0], num_segments=r.shape[0])
        return out

    def _L2_gnn_ref(h, src, dst, Wq, Wk, Wv, Wo, bo, W1, b1, W2, b2, bn1_g, bn1_b, bn2_g, bn2_b):
        import jax, jax.numpy as jnp
        import numpy as np
        N, E = (6250, 100000)
        D, H = (128, 8)
        DH = D // H
        DFF = 2 * D
        EPS_BN = 1e-05

        def _batch_norm(x, g, b):
            mu = jnp.mean(x, axis=0)
            var = jnp.mean((x - mu) ** 2, axis=0)
            return (x - mu) * jax.lax.rsqrt(var + EPS_BN) * g + b
        n = h.shape[0]
        Q = (h @ Wq).reshape(n, H, DH)
        K = (h @ Wk).reshape(n, H, DH)
        V = (h @ Wv).reshape(n, H, DH)
        score = K[src] * Q[dst] / np.sqrt(DH)
        s = jnp.exp(jnp.clip(jnp.sum(score, axis=-1), -5.0, 5.0))
        s = s[..., None]
        wV = jax.ops.segment_sum(V[src] * s, dst, num_segments=n)
        z = jax.ops.segment_sum(s, dst, num_segments=n)
        h_attn = (wV / (z + 1e-06)).reshape(n, D)
        hx = h_attn @ Wo + bo
        hx = h + hx
        hx = _batch_norm(hx, bn1_g, bn1_b)
        h2 = jax.nn.relu(hx @ W1 + b1) @ W2 + b2
        hx = _batch_norm(hx + h2, bn2_g, bn2_b)
        return hx

    def _L3_gnn_ref(x, edge_index, time_emb, edge_type, edge_time, Wq, Wk, Wv, rel_q, rel_k, rel_v, Wt, bt, Wd1, bd1, Wd2, bd2, decay_scale, c_mag, hyp_beta, logit_alpha, Wo, bo, g1, be1, g2, be2, Wf1, bf1, Wf2, bf2):
        import jax, jax.numpy as jnp
        import numpy as np
        N = 12500
        E = 75000
        D = 128
        H = 8
        DH = D // H
        T = 32
        NET = 2

        def _ln(x, g, b, eps=1e-05):
            mu = jnp.mean(x, axis=-1, keepdims=True)
            var = jnp.mean((x - mu) ** 2, axis=-1, keepdims=True)
            return (x - mu) * jax.lax.rsqrt(var + eps) * g + b

        def _expmap(e, c):
            abs_c = jnp.maximum(jnp.abs(c), 1e-15)
            sq = jnp.sqrt(abs_c)
            n = jnp.maximum(jnp.linalg.norm(e, axis=-1, keepdims=True), 1e-15)
            tanh_p = jnp.tanh(sq * n) * e / (sq * n)
            tan_p = jnp.tan(sq * n) * e / (sq * n)
            return jnp.where(c < 0, tanh_p, tan_p)

        def _proj(x, c, eps=1e-05):
            abs_c = jnp.maximum(jnp.abs(c), 1e-15)
            maxnorm = (1.0 - eps) / jnp.sqrt(abs_c)
            norm = jnp.linalg.norm(x, axis=-1, keepdims=True)
            scale = jnp.where(norm > maxnorm, maxnorm / norm, jnp.ones_like(norm))
            return x * scale

        def _forward(x, time_emb, edge_time, Wq, Wk, Wv, rel_q, rel_k, rel_v, Wt, bt, Wd1, bd1, Wd2, bd2, decay_scale, c_mag, hyp_beta, logit_alpha, Wo, bo, g1, be1, g2, be2, Wf1, bf1, Wf2, bf2, src, dst, edge_type):
            n = x.shape[0]
            Q = (x @ Wq).reshape(n, H, DH)
            K = (x @ Wk).reshape(n, H, DH)
            V = (x @ Wv).reshape(n, H, DH)
            q_dst = Q[dst] + rel_q[edge_type].reshape(-1, H, DH)
            k_src = K[src] + rel_k[edge_type].reshape(-1, H, DH)
            v_src = V[src] + rel_v[edge_type].reshape(-1, H, DH)
            k_src = k_src + (time_emb @ Wt + bt).reshape(-1, H, DH)
            euclid = jnp.sum(q_dst * k_src, axis=-1) / np.float32(np.sqrt(DH))
            denom_t = jnp.maximum(1.0, edge_type.max().astype(jnp.float32) + 1.0)
            et = edge_type.astype(jnp.float32)[:, None] / denom_t
            dec_in = jnp.concatenate([edge_time[:, None], et], axis=-1)
            decay_raw = jnp.tanh(jax.nn.relu(dec_in @ Wd1 + bd1) @ Wd2 + bd2)
            decay = jnp.exp(decay_scale[None, :] * decay_raw)
            euclid = euclid * decay
            c = -jnp.abs(c_mag)
            m = _proj(_expmap(x, c), c)
            man_dist = jnp.linalg.norm(m[src] - m[dst], axis=-1)[:, None]
            hyp = -hyp_beta[None, :] * man_dist * decay
            alpha = jax.nn.sigmoid(logit_alpha)[None, :]
            logits = alpha * euclid + (1.0 - alpha) * hyp
            seg_max = jax.ops.segment_max(logits, dst, num_segments=n)
            ex = jnp.exp(logits - seg_max[dst])
            denom = jax.ops.segment_sum(ex, dst, num_segments=n)
            attn = ex / denom[dst]
            agg = jax.ops.segment_sum(v_src * attn[..., None], dst, num_segments=n).reshape(n, D)
            out = agg @ Wo + bo
            x = _ln(x + out, g1, be1)
            ffn = jax.nn.gelu(x @ Wf1 + bf1, approximate=False) @ Wf2 + bf2
            x = _ln(x + ffn, g2, be2)
            return x
        src, dst = (edge_index[0], edge_index[1])
        return _forward(x, time_emb, edge_time, Wq, Wk, Wv, rel_q, rel_k, rel_v, Wt, bt, Wd1, bd1, Wd2, bd2, decay_scale, c_mag, hyp_beta, logit_alpha, Wo, bo, g1, be1, g2, be2, Wf1, bf1, Wf2, bf2, src, dst, edge_type)
    edge_index = jnp.stack([src, dst])
    edge_index_t = jnp.stack([src, dst], axis=1)
    x = _layernorm(x + _L0_gnn_ref(x, edge_index, L0_gnn_W, L0_gnn_b), axis=-1)
    x = _layernorm(x + _L1_gnn_ref(x, edge_attr_128, edge_index_t), axis=-1)
    x = _layernorm(x + _L2_gnn_ref(x, src, dst, L2_gnn_Wq, L2_gnn_Wk, L2_gnn_Wv, L2_gnn_Wo, L2_gnn_bo, L2_gnn_W1, L2_gnn_b1, L2_gnn_W2, L2_gnn_b2, L2_gnn_bn1_g, L2_gnn_bn1_b, L2_gnn_bn2_g, L2_gnn_bn2_b), axis=-1)
    x = _layernorm(x + _L3_gnn_ref(x, edge_index, edge_attr_32, edge_type_2, edge_weight, L3_gnn_Wq, L3_gnn_Wk, L3_gnn_Wv, L3_gnn_rel_q, L3_gnn_rel_k, L3_gnn_rel_v, L3_gnn_Wt, L3_gnn_bt, L3_gnn_Wd1, L3_gnn_bd1, L3_gnn_Wd2, L3_gnn_bd2, L3_gnn_decay_scale, L3_gnn_c_mag, L3_gnn_hyp_beta, L3_gnn_logit_alpha, L3_gnn_Wo, L3_gnn_bo, L3_gnn_g1, L3_gnn_be1, L3_gnn_g2, L3_gnn_be2, L3_gnn_Wf1, L3_gnn_bf1, L3_gnn_Wf2, L3_gnn_bf2), axis=-1)
    return x

_drawn_inputs = setup_inputs


def setup_inputs(seed=0):
    import zlib

    import numpy as np

    out = dict(_drawn_inputs(seed))
    spreads = {'L0_gnn_b': (0.0, 0.1),
     'L2_gnn_bo': (0.0, 2.0),
     'L2_gnn_b1': (0.0, 0.373),
     'L2_gnn_b2': (0.0, 2.0),
     'L2_gnn_bn1_g': (1.0, 0.2),
     'L2_gnn_bn1_b': (0.0, 0.354),
     'L2_gnn_bn2_g': (1.0, 0.2),
     'L2_gnn_bn2_b': (0.0, 0.1),
     'L3_gnn_bt': (0.0, 0.8),
     'L3_gnn_bd1': (0.0, 0.8),
     'L3_gnn_bd2': (0.0, 2.0),
     'L3_gnn_decay_scale': (0.5, 0.6),
     'L3_gnn_hyp_beta': (1.0, 0.6),
     'L3_gnn_logit_alpha': (0.0, 0.8),
     'L3_gnn_bo': (0.0, 0.1),
     'L3_gnn_g1': (1.0, 0.2),
     'L3_gnn_be1': (0.0, 0.1),
     'L3_gnn_g2': (1.0, 0.2),
     'L3_gnn_be2': (0.0, 0.1),
     'L3_gnn_bf1': (0.0, 0.272),
     'L3_gnn_bf2': (0.0, 0.1)}
    factors = {'edge_weight': 8.0,
     'L3_gnn_rel_q': 5.817,
     'L3_gnn_rel_k': 8.0,
     'L3_gnn_Wd1': 4.386,
     'L3_gnn_Wd2': 3.546}
    for name, (base, spread) in spreads.items():
        noise = np.random.default_rng([zlib.crc32(name.encode()), seed]).standard_normal(out[name].shape)
        drawn = base * np.exp(spread * noise) if base else spread * noise
        out[name] = jnp.asarray(drawn.astype(out[name].dtype))
    for name, factor in factors.items():
        out[name] = (out[name] * factor).astype(out[name].dtype)
    return out
```

```python
from contextlib import ExitStack

import numpy as np
import concourse.bass as bass
from concourse import mybir

P = 128
D = 128
N = 6250
E = 106250
H = 8
DH = D // H
K4 = 4
UNIT = P * K4
NU = 208
EP = NU * UNIT
NT = 52
NG = NT // 4
GC = 512
NP = NT * P
TR = NP + P
R = 4
NI = NU // R
LASTN = N - (NG - 1) * GC
CH = 16
CU = NU // CH
CE = CU * UNIT
TE = 36
HID = 64
BIG = 1e30

ALU = mybir.AluOpType
ACT = mybir.ActivationFunctionType
AX = mybir.AxisListType.X
F32 = mybir.dt.float32
BF16 = mybir.dt.bfloat16
I32 = mybir.dt.int32

WEIGHTS = {
    "L0_gnn_W": (D, D), "L0_gnn_b": (D,),
    "L2_gnn_Wq": (D, D), "L2_gnn_Wk": (D, D), "L2_gnn_Wv": (D, D), "L2_gnn_Wo": (D, D), "L2_gnn_bo": (D,),
    "L2_gnn_W1": (D, 256), "L2_gnn_b1": (256,), "L2_gnn_W2": (256, D), "L2_gnn_b2": (D,),
    "L2_gnn_bn1_g": (D,), "L2_gnn_bn1_b": (D,), "L2_gnn_bn2_g": (D,), "L2_gnn_bn2_b": (D,),
    "L3_gnn_Wq": (D, D), "L3_gnn_Wk": (D, D), "L3_gnn_Wv": (D, D),
    "L3_gnn_rel_q": (2, D), "L3_gnn_rel_k": (2, D), "L3_gnn_rel_v": (2, D),
    "L3_gnn_Wt": (32, D), "L3_gnn_bt": (D,), "L3_gnn_Wd1": (2, HID), "L3_gnn_bd1": (HID,),
    "L3_gnn_Wd2": (HID, H), "L3_gnn_bd2": (H,), "L3_gnn_decay_scale": (H,), "L3_gnn_c_mag": (1,),
    "L3_gnn_hyp_beta": (H,), "L3_gnn_logit_alpha": (H,), "L3_gnn_Wo": (D, D), "L3_gnn_bo": (D,),
    "L3_gnn_g1": (D,), "L3_gnn_be1": (D,), "L3_gnn_g2": (D,), "L3_gnn_be2": (D,),
    "L3_gnn_Wf1": (D, 512), "L3_gnn_bf1": (512,), "L3_gnn_Wf2": (512, D), "L3_gnn_bf2": (D,),
}


class Steps:

    def __init__(self, eng, sem, turn=0, per=0):
        self.eng, self.sem, self.start, self.n, self.per = eng, sem, turn * per, 0, per

    def done(self, ins):
        ins.then_inc(self.sem, 1)
        self.n += 1

    def settle(self):
        self.eng.wait_ge(self.sem, self.start + self.n)

    def end(self):
        assert not self.per or self.n == self.per, (self.n, self.per)


def turns(eng, n):
    yield 0
    with eng.Fori(1, n) as i:
        yield i


def bc(ap, shape):
    return ap.broadcast_to(shape)


def cols(vec):
    return vec.rearrange("(p o) -> p o", o=1)


def everywhere(vec, n):
    return bc(vec.rearrange("(o n) -> o n", o=1), [P, n])


class Net:
    def __init__(self, nc, stack, dram):
        self.nc, self.stack, self.dram = nc, stack, dram
        self.phase = ""
        self.lasting = stack
        self.semaphores = []

    def scope(self, name):
        scope = Net(self.nc, ExitStack(), self.dram)
        scope.lasting = self.lasting
        scope.phase = name
        scope.semaphores = []
        return scope

    def sb(self, name, shape, dt=F32):
        return self.stack.enter_context(self.nc.sbuf_tensor(f"{self.phase}{name}", shape, dt))

    def ps(self, name, shape, dt=F32):
        return self.stack.enter_context(self.nc.psum_tensor(f"{self.phase}{name}", shape, dt))

    def sem(self, name):
        self.semaphores.append(self.stack.enter_context(self.nc.semaphore(f"{self.phase}{name}")))
        return self.semaphores[-1]

    def __enter__(self):
        return self

    def __exit__(self, *error):
        if error[0] is None and self.semaphores:
            with self.nc.Block() as block:
                @block.gpsimd
                def _(eng):
                    for s in self.semaphores:
                        eng.sem_clear(s)
        self.stack.close()

    def gather_sems(self, name, n):
        return [self.lasting.enter_context(self.nc.semaphore(f"{self.phase}{name}{i}")) for i in range(n)]

    def sems(self, name, n):
        return [self.sem(f"{name}{i}") for i in range(n)]

    def table(self, name, shape, dt=F32):
        return self.nc.dram_tensor(name, shape, dt, kind="Internal").ap()


def layer_norm(eng, steps, y, stats, moments, std, out, sqrt_in, sqrt_done, sqrt_count, eps):
    for j in range(4):
        steps.done(eng.bn_stats(stats[:, j, :], y[:, j, :]))
    steps.settle()
    mark(eng, sqrt_in)
    for j in range(4):
        steps.done(eng.bn_aggr(moments[:, j, :], stats[:, j, :]))
    steps.settle()
    steps.done(eng.tensor_scalar(std[:, :], moments[:, :, 1], eps, None, ALU.add))
    steps.settle()
    mark(eng, sqrt_in)
    eng.wait_ge(sqrt_done, sqrt_count)
    mark(eng, sqrt_in)
    steps.done(eng.reciprocal(std[:, :], std[:, :]))
    steps.settle()
    for j in range(4):
        steps.done(eng.tensor_scalar(out[:, j, :], y[:, j, :], moments[:, j, 0:1], std[:, j:j + 1],
                                     ALU.subtract, ALU.mult))
    steps.settle()


LN_STEPS = 4 + 4 + 1 + 1 + 4


def mark(eng, sem):
    eng.sem_inc(sem, 1)


def setup(net):
    nc, dram = net.nc, net.dram
    net.ident = net.sb("ident", [P, P])
    net.iota = net.sb("iota", [P, P])
    net.lower = net.sb("lower", [P, P])
    net.spare = net.sb("spare", [P, 1])
    net.ones = net.sb("ones", [P, P])
    net.expand = net.sb("expand", [H, P])
    net.dst_local = net.sb("dst_local", [P, NU * K4])
    net.src_f = net.sb("src_f", [P, NU * K4])
    net.base_i = net.sb("base_i", [1, NU], I32)
    net.type_scale = net.sb("type_scale", [P, 1])
    net.dinv = net.sb("dinv", [P, NT])
    net.dst_rows = net.table("dst_rows", (EP,))
    net.type_rows = net.table("types", (2, EP))
    net.base_rows = net.table("base_rows", (NU,))
    HU = NU // 2

    n = net.scope("s0_")
    with n:
        dst_i = n.sb("dst_i", [P, NU * K4], I32)
        src_i = n.sb("src_i", [P, NU * K4], I32)
        dst_f = n.sb("dst_f", [P, NU * K4])
        rows_i = n.sb("rows_i", [HU, 2, UNIT], I32)
        rows_f = n.sb("rows_f", [HU, 2, UNIT])
        types_i = n.sb("types_i", [HU, 2, UNIT], I32)
        types_f = n.sb("types_f", [HU, 2, 2, UNIT])
        least = n.sb("least", [HU, 2])
        most = n.sb("most", [HU, 1])
        base_f = n.sb("base_f", [1, NU])
        base_all = n.sb("base_all", [P, NU])
        hi_i = n.sb("hi_i", [P, NU * K4], I32)
        lo_i = n.sb("lo_i", [P, NU * K4], I32)
        hi = n.sb("hi", [P, NU * K4])
        lo = n.sb("lo", [P, NU * K4])
        row = n.sb("row", [1, 8])
        sel = n.sb("sel", [1, 2, P])
        pm = n.ps("pm", [P, P])
        loaded, pool_built, written = n.sem("loaded"), n.sem("pool_built"), n.sem("written")
        dve, most_turned, scale_spread, base_in = n.sem("dve"), n.sem("most_turned"), n.sem("scale_spread"), n.sem("base_in")
        with nc.Block() as block:
            @block.sync
            def _(eng):
                eng.dma_start(dst_i[:, :], dram["dst_tiles"]).then_inc(loaded, 16)
                eng.dma_start(src_i[:, :], dram["src_tiles"]).then_inc(loaded, 16)
                eng.dma_start(rows_i[:, :, :], dram["dst_row"].rearrange("(p a e) -> p a e", a=2, e=UNIT)).then_inc(loaded, 16)
                eng.dma_start(types_i[:, :, :], dram["type_row"].rearrange("(p a e) -> p a e", a=2, e=UNIT)).then_inc(loaded, 16)
                eng.wait_ge(dve, 7)
                eng.dma_start(net.base_rows.rearrange("(p a) -> p a", a=2), least[:, :]).then_inc(written, 16)
                eng.dma_start(net.dst_rows.rearrange("(p a e) -> p a e", a=2, e=UNIT), rows_f[:, :, :]).then_inc(written, 16)
                for c in range(2):
                    eng.dma_start(net.type_rows[c].rearrange("(p a e) -> p a e", a=2, e=UNIT), types_f[:, c, :, :]).then_inc(written, 16)
                eng.wait_ge(written, 64)
                eng.dma_start(base_f[:, :], net.base_rows.rearrange("(o n) -> o n", o=1)).then_inc(base_in, 16)
                eng.dma_start(base_all[:, :], everywhere(net.base_rows, NU)).then_inc(base_in, 16)
                eng.wait_ge(base_in, 32)

            @block.gpsimd
            def _(eng):
                eng.memset(net.ident[:, :], 0.0).then_inc(pool_built, 1)
                eng.memset(net.lower[:, :], 1.0).then_inc(pool_built, 1)
                eng.memset(net.expand[:, :], 1.0).then_inc(pool_built, 1)
                eng.memset(net.ones[:, :], 1.0).then_inc(pool_built, 1)
                eng.memset(sel[:, 0, :], 0.0).then_inc(pool_built, 1)
                eng.memset(sel[:, 1, :], 1.0).then_inc(pool_built, 1)
                eng.iota(net.iota[:, :], pattern=[[1, P]], base=0, channel_multiplier=0,
                         allow_small_or_imprecise_dtypes=True).then_inc(pool_built, 1)
                eng.iota(net.spare[:, :], pattern=[[1, 1]], base=NP, channel_multiplier=1,
                         allow_small_or_imprecise_dtypes=True).then_inc(pool_built, 1)
                eng.wait_ge(pool_built, 8)
                eng.affine_select(out=net.ident[:, :], in_=net.ident[:, :], compare_op=ALU.not_equal, fill=1.0,
                                  base=0, pattern=[[-1, P]], channel_multiplier=1).then_inc(pool_built, 1)
                eng.affine_select(out=net.lower[:, :], in_=net.lower[:, :], compare_op=ALU.is_gt, fill=0.0,
                                  base=0, pattern=[[-1, P]], channel_multiplier=1).then_inc(pool_built, 1)
                eng.affine_select(out=net.expand[:, :], in_=net.expand[:, :], compare_op=ALU.is_ge, fill=0.0,
                                  base=0, pattern=[[1, P]], channel_multiplier=-DH).then_inc(pool_built, 1)
                eng.wait_ge(pool_built, 11)
                eng.affine_select(out=net.expand[:, :], in_=net.expand[:, :], compare_op=ALU.is_ge, fill=0.0,
                                  base=DH - 1, pattern=[[-1, P]], channel_multiplier=DH).then_inc(pool_built, 1)
                eng.memset(sel[:, 0, TE - 2:TE - 1], 1.0).then_inc(pool_built, 1)
                eng.memset(sel[:, 1, TE - 2:TE - 1], 0.0).then_inc(pool_built, 1)

            @block.vector
            def _(eng):
                eng.wait_ge(loaded, 64)
                steps = Steps(eng, dve)
                steps.done(eng.tensor_copy(dst_f[:, :], dst_i[:, :]))
                steps.done(eng.tensor_copy(net.src_f[:, :], src_i[:, :]))
                steps.done(eng.tensor_copy(rows_f[:, :, :], rows_i[:, :, :]))
                steps.done(eng.tensor_copy(types_f[:, 0, :, :], types_i[:, :, :]))
                steps.settle()
                steps.done(eng.tensor_scalar(types_f[:, 1, :, :], types_f[:, 0, :, :], -1.0, 1.0, ALU.mult, ALU.add))
                steps.done(eng.tensor_reduce(least[:, :], rows_f[:, :, :], AX, ALU.min))
                steps.done(eng.tensor_reduce(most[:, :], types_f[:, 0, :, :].rearrange("p a e -> p (a e)"), AX, ALU.max))
                eng.wait_ge(base_in, 32)
                steps.done(eng.tensor_copy(net.base_i[:, :], base_f[:, :]))
                steps.done(eng.tensor_tensor(net.dst_local[:, :].rearrange("p (u k) -> p u k", k=K4),
                                             dst_f[:, :].rearrange("p (u k) -> p u k", k=K4),
                                             bc(base_all[:, :].unsqueeze(2), [P, NU, K4]), ALU.subtract))
                eng.wait_ge(most_turned, 1)
                steps.done(eng.tensor_reduce(row[:, 0:1], pm[0:1, 0:HU], AX, ALU.max))
                steps.settle()
                steps.done(eng.tensor_scalar(row[:, 1:2], row[:, 0:1], 1.0, 1.0, ALU.add, ALU.max))
                steps.settle()
                steps.done(eng.reciprocal(row[:, 2:3], row[:, 1:2]))
                steps.settle()
                eng.wait_ge(scale_spread, 1)
                steps.done(eng.tensor_copy(net.type_scale[:, :], pm[:, 0:1]))

            @block.tensor
            def _(eng):
                eng.wait_ge(pool_built, 14)
                eng.wait_ge(dve, 7)
                eng.transpose(pm[0:1, 0:HU], most[:, :], net.ident[0:HU, 0:HU]).then_inc(most_turned, 1)
                eng.wait_ge(dve, 12)
                eng.matmul(pm[:, 0:1], sel[:, 0, :], row[:, 2:3], start=True, stop=False)
                eng.matmul(pm[:, 0:1], sel[:, 1, :], net.ones[0:1, 0:1], start=False, stop=True).then_inc(scale_spread, 1)

    n = net.scope("s1_")
    with n:
        dst_i = n.sb("dst_i", [P, NU * K4], I32)
        hi_i = n.sb("hi_i", [P, NU * K4], I32)
        lo_i = n.sb("lo_i", [P, NU * K4], I32)
        hi = n.sb("hi", [P, NU * K4])
        lo = n.sb("lo", [P, NU * K4])
        hot_lo = n.sb("hot_lo", [P, R, K4, P], BF16)
        hot_hi = n.sb("hot_hi", [P, R, K4, NT], BF16)
        deg = n.sb("deg", [P, NT])
        counts = n.ps("counts", [P, NT])
        loaded, dve = n.sem("loaded"), n.sem("dve")
        hot, used = n.sems("hot", R), n.sems("used", R)
        counted, rooted, zeroed = n.sem("counted"), n.sem("rooted"), n.sem("zeroed")
        zero = n.sb("zero", [P, P], BF16)
        with nc.Block() as block:
            @block.sync
            def _(eng):
                eng.dma_start(dst_i[:, :], dram["dst_tiles"]).then_inc(loaded, 16)

            @block.gpsimd
            def _(eng):
                eng.memset(zero[:, :], 0.0).then_inc(zeroed, 1)

            @block.vector
            def _(eng):
                eng.wait_ge(loaded, 16)
                steps = Steps(eng, dve)
                steps.done(eng.tensor_scalar(hi_i[:, :], dst_i[:, :], 7, None, ALU.logical_shift_right))
                steps.done(eng.tensor_scalar(lo_i[:, :], dst_i[:, :], P - 1, None, ALU.bitwise_and))
                steps.settle()
                steps.done(eng.tensor_copy(hi[:, :], hi_i[:, :]))
                steps.done(eng.tensor_copy(lo[:, :], lo_i[:, :]))
                steps.settle()
                for i in turns(eng, NI):
                    for b in range(R):
                        u = i * R + b
                        eng.wait_ge(used[b], i)
                        eng.tensor_tensor(hot_lo[:, b], bc(net.iota[:, :].unsqueeze(1), [P, K4, P]),
                                          bc(lo[:, bass.ds(u * K4, K4)].unsqueeze(2), [P, K4, P]), ALU.is_equal).then_inc(hot[b], 1)
                        eng.tensor_tensor(hot_hi[:, b], bc(net.iota[:, 0:NT].unsqueeze(1), [P, K4, NT]),
                                          bc(hi[:, bass.ds(u * K4, K4)].unsqueeze(2), [P, K4, NT]), ALU.is_equal).then_inc(hot[b], 1)
                eng.wait_ge(counted, 1)
                steps.done(eng.tensor_scalar(deg[:, :], counts[:, :], 1.0, None, ALU.add))
                eng.wait_ge(rooted, 1)
                steps.done(eng.reciprocal(net.dinv[:, :], deg[:, :]))

            @block.scalar
            def _(eng):
                eng.wait_ge(dve, 5)
                eng.activation(deg[:, :], deg[:, :], ACT.Sqrt).then_inc(rooted, 1)

            @block.tensor
            def _(eng):
                eng.wait_ge(zeroed, 1)
                eng.matmul(counts[:, :], zero[:, :], zero[:, 0:NT], start=True, stop=False, skip_group_check=True)
                for i in turns(eng, NI):
                    for b in range(R):
                        eng.wait_ge(hot[b], i * 2 + 2)
                        for k in range(K4):
                            mm = eng.matmul(counts[:, :], hot_lo[:, b, k, :], hot_hi[:, b, k, :], start=False,
                                            stop=False, skip_group_check=True)
                        mm.then_inc(used[b], 1)
                eng.matmul(counts[:, :], zero[:, :], zero[:, 0:NT], start=False, stop=True, skip_group_check=True).then_inc(counted, 1)


def rows_of(table, lo, n=GC):
    return table[bass.ds(lo, n), :].rearrange("(t p) d -> p t d", p=P)


def project(net, name, weights, outs, x_row, x_T=None, scale=None, keep=None, hyper=None):
    nc, dram = net.nc, net.dram
    n = net.scope(name)
    with n:
        F = D * len(weights)
        w = n.sb("w", [D, len(weights), D])
        xt = n.sb("xt", [P, GC])
        prod = n.sb("prod", [P, 4, F])
        turned = n.ps("turned", [P, GC])
        pp = [n.ps(f"pp{j}", [P, F]) for j in range(4)]
        loaded, turned_s, copied, made, kept, stored = (n.sem(s) for s in (
            "loaded", "turned_s", "copied", "made", "kept", "stored"))
        moved = n.sem("moved")
        with nc.Block() as block:
            @block.sync
            def _(eng):
                for c, name_ in enumerate(weights):
                    eng.dma_start(w[:, c, :], dram[name_]).then_inc(loaded, 16)
                for g in turns(eng, NG):
                    eng.wait_ge(kept, g + 1)
                    mark(eng, moved)
                    for table, at, width, to in outs:
                        eng.dma_start(rows_of(table, g * GC)[:, :, to:to + width],
                                      prod[:, :, at:at + width]).then_inc(stored, 16)
                eng.wait_ge(stored, 16 * len(outs) * NG)

            @block.tensor
            def _(eng):
                eng.wait_ge(loaded, 16 * len(weights))
                for g in turns(eng, NG):
                    eng.wait_ge(copied, g * 2 + 1)
                    for j in range(4):
                        mm = eng.transpose(turned[:, j * P:(j + 1) * P], prod[:, j, 0:D], net.ident[:, :])
                    mm.then_inc(turned_s, 1)
                    eng.wait_ge(copied, g * 2 + 2)
                    for j in range(4):
                        mm = eng.matmul(pp[j][:, :], xt[:, j * P:(j + 1) * P], w[:, :, :].rearrange("p c d -> p (c d)"),
                                        start=True, stop=True)
                    mm.then_inc(made, 1)

            @block.vector
            def _(eng):
                for g in turns(eng, NG):
                    eng.wait_ge(stored, g * (16 * len(outs)))
                    mark(eng, moved)
                    eng.tensor_copy(prod[:, :, 0:D], x_row[:, bass.ds(g * 4, 4), :]).then_inc(copied, 1)
                    eng.wait_ge(turned_s, g + 1)
                    eng.tensor_copy(xt[:, :], turned[:, :]).then_inc(copied, 1)
                    if x_T is not None:
                        eng.tensor_copy(x_T[:, bass.ds(g * GC, GC)], turned[:, :])
                    eng.wait_ge(made, g + 1)
                    mark(eng, moved)
                    for j in range(4):
                        if scale is None:
                            cp = eng.tensor_copy(prod[:, j, :], pp[j][:, :])
                        else:
                            cp = eng.tensor_scalar(prod[:, j, :], pp[j][:, :], scale[:, bass.ds(g * 4 + j, 1)], None, ALU.mult)
                            cp = eng.tensor_scalar(keep[:, bass.ds(g * 4 + j, 1), :].rearrange("p a d -> p (a d)"),
                                                   pp[j][:, :], scale[:, bass.ds(g * 4 + j, 1)], None, ALU.mult)
                    cp.then_inc(kept, 1)


def gather(eng, out, table, idx):
    return eng.indirect_dma_start(out=out, out_offset=None, in_=table,
                                  in_offset=bass.IndirectOffsetOnAxis(ap=idx, axis=0))


def index_loads(net, eng, i, b, idx, idx_in, got, per):
    eng.wait_ge(got[b], i * per)
    eng.dma_start(idx[:, b, :], net.dram["idx"][:, bass.ds((i * R + b) * 8, 8)]).then_inc(idx_in[b], 16)


def build_hot(net, eng, hot, i, b):
    return eng.tensor_tensor(hot[:, b], bc(net.iota[:, :].unsqueeze(1), [P, K4, P]),
                             bc(net.dst_local[:, bass.ds((i * R + b) * K4, K4)].unsqueeze(2), [P, K4, P]), ALU.is_equal)


def clear(net, name, acc):
    n = net.scope(name)
    with n, net.nc.Block() as block:
        @block.gpsimd
        def _(eng):
            for a in acc:
                eng.memset(a[:, :], 0.0)


def add_window(net, eng, i, b, adds, sums_free):
    if b:
        eng.wait_ge(sums_free[b - 1], i * len(adds) + len(adds))
    else:
        eng.wait_ge(sums_free[R - 1], i * len(adds))
    base = eng.value_load(net.base_i[0:1, bass.ds(i * R + b, 1)], min_val=0, max_val=NP - P)
    for acc, sums in adds:
        at = acc[:, bass.ds(base, P)]
        eng.tensor_tensor(at, at, sums, ALU.add).then_inc(sums_free[b], 1)


def edges_gcn(net, hs, acc):
    nc, dram = net.nc, net.dram
    n = net.scope("l0_")
    with n:
        idx = n.sb("idx", [P, R, 8], I32)
        msg = n.sb("msg", [P, R, K4, D])
        hot = n.sb("hot", [P, R, K4, P])
        sums = [n.ps(f"sums{b}", [P, P]) for b in range(R)]
        idx_in, hot_in, summed, sums_free = (n.sems(s, R) for s in ("idx_in", "hot_in", "summed", "sums_free"))
        got = n.gather_sems("got", R)
        marks = n.sem("marks")
        with nc.Block() as block:
            @block.sync
            def _(eng):
                for i in turns(eng, NI):
                    for b in range(R):
                        index_loads(net, eng, i, b, idx, idx_in, got, 64)

            @block.gpsimd
            def _(eng):
                for i in turns(eng, NI):
                    for b in range(R):
                        eng.wait_ge(idx_in[b], i * 16 + 16)
                        eng.wait_ge(summed[b], i)
                        mark(eng, marks)
                        for k in range(K4):
                            gather(eng, msg[:, b, k, :], hs, idx[:, b, k:k + 1]).then_inc(got[b], 16)

            @block.vector
            def _(eng):
                for i in turns(eng, NI):
                    for b in range(R):
                        eng.wait_ge(summed[b], i)
                        build_hot(net, eng, hot, i, b).then_inc(hot_in[b], 1)
                    for b in range(R):
                        eng.wait_ge(summed[b], i + 1)
                        add_window(net, eng, i, b, [(acc, sums[b][:, :])], sums_free)

            @block.tensor
            def _(eng):
                for i in turns(eng, NI):
                    for b in range(R):
                        eng.wait_ge(hot_in[b], i + 1)
                        eng.wait_ge(sums_free[b], i)
                        eng.wait_ge(got[b], i * 64 + 64)
                        for k in range(K4):
                            mm = eng.matmul(sums[b][:, :], msg[:, b, k, :], hot[:, b, k, :], start=(k == 0), stop=(k == K4 - 1))
                        mm.then_inc(summed[b], 1)


def nodes_gcn(net, acc, hs_row, x_row, table):
    nc, dram = net.nc, net.dram
    n = net.scope("n0_")
    PER = 1 + 1 + 4 + 1 + 1 + LN_STEPS
    with n:
        bias = n.sb("bias", [P, D])
        st = n.sb("st", [P, GC])
        y = n.sb("y", [P, 4, D])
        z = n.sb("z", [P, 4, D])
        stats, moments, std = n.sb("stats", [P, 4, 6]), n.sb("moments", [P, 4, 2]), n.sb("std", [P, 4])
        turned = n.ps("turned", [P, GC])
        loaded, dve, turned_s, rooted, stored, marks = (n.sem(s) for s in ("loaded", "dve", "turned_s", "rooted", "stored", "marks"))
        with nc.Block() as block:
            @block.sync
            def _(eng):
                eng.dma_start(bias[:, :], everywhere(dram["L0_gnn_b"], D)).then_inc(loaded, 16)
                for g in turns(eng, NG):
                    eng.wait_ge(dve, g * PER + PER)
                    mark(eng, marks)
                    eng.dma_start(rows_of(table, g * GC), x_row[:, bass.ds(g * 4, 4), :]).then_inc(stored, 16)
                eng.wait_ge(stored, 16 * NG)

            @block.tensor
            def _(eng):
                for g in turns(eng, NG):
                    eng.wait_ge(dve, g * PER + 1)
                    for j in range(4):
                        mm = eng.transpose(turned[:, j * P:(j + 1) * P], st[:, j * P:(j + 1) * P], net.ident[:, :])
                    mm.then_inc(turned_s, 1)

            @block.scalar
            def _(eng):
                for g in turns(eng, NG):
                    eng.wait_ge(dve, g * PER + 8 + 9)
                    eng.activation(std[:, :], std[:, :], ACT.Sqrt).then_inc(rooted, 1)

            @block.vector
            def _(eng):
                eng.wait_ge(loaded, 16)
                for g in turns(eng, NG):
                    steps = Steps(eng, dve, g, PER)
                    steps.done(eng.tensor_copy(st[:, :], acc[:, bass.ds(g * GC, GC)]))
                    eng.wait_ge(turned_s, g + 1)
                    steps.done(eng.tensor_tensor(y[:, :, :], turned[:, :].rearrange("p (t d) -> p t d", d=D),
                                                 hs_row[:, bass.ds(g * 4, 4), :], ALU.add))
                    steps.settle()
                    for j in range(4):
                        steps.done(eng.scalar_tensor_tensor(out=z[:, j, :], in0=y[:, j, :], scalar=net.dinv[:, bass.ds(g * 4 + j, 1)],
                                                            in1=bias[:, :], op0=ALU.mult, op1=ALU.add))
                    steps.settle()
                    steps.done(eng.tensor_scalar(y[:, :, :], z[:, :, :], 0.0, None, ALU.max))
                    steps.settle()
                    steps.done(eng.tensor_tensor(z[:, :, :], y[:, :, :], x_row[:, bass.ds(g * 4, 4), :], ALU.add))
                    steps.settle()
                    layer_norm(eng, steps, z, stats, moments, std, x_row[:, bass.ds(g * 4, 4), :], marks, rooted, g + 1, 1e-5)
                    steps.end()


def edges_gated(net, x1, acc, tabs):
    nc, dram = net.nc, net.dram
    n = net.scope("l1_")
    IDX = 6
    with n:
        idx = n.sb("idx", [P, R, 8], I32)
        src_all = n.sb("src_all", [P, R, UNIT], I32)
        xs, xd, ea = (n.sb(s, [P, R, K4, D]) for s in ("xs", "xd", "ea"))
        hot = n.sb("hot", [P, R, K4, P])
        same = n.sb("same", [P, R, K4, P])
        before = n.sb("before", [P, K4, P])
        again = n.sb("again", [P, K4])
        off = n.sb("off", [P, K4])
        to_i = n.sb("to_i", [P, R, K4], I32)
        total = n.sb("total", [P, R, K4, D])
        sums = [n.ps(f"sums{b}", [P, P]) for b in range(R)]
        pres = [n.ps(f"pres{b}", [P, K4, D]) for b in range(2)]
        got = n.gather_sems("got", R)
        idx_in, ea_in, hot_in, gated, summed, sums_free = (n.sems(s, R) for s in (
            "idx_in", "ea_in", "hot_in", "gated", "summed", "sums_free"))
        total_in, to_in, added = (n.sems(s, R) for s in ("total_in", "to_in", "added"))
        pre_in, pre_free = n.sems("pre_in", 2), n.sems("pre_free", 2)
        tab_added = n.gather_sems("tab_added", K4)
        marks, dve = n.sem("marks"), n.sem("dve")
        with nc.Block() as block:
            @block.sync
            def _(eng):
                for i in turns(eng, NI):
                    for b in range(R):
                        index_loads(net, eng, i, b, idx, idx_in, got, 128)
                        eng.wait_ge(summed[b], i)
                        mark(eng, marks)
                        eng.dma_start(ea[:, b], dram["ea"][bass.ds((i * R + b) * UNIT, UNIT), :].rearrange(
                            "(p k) d -> p k d", k=K4)).then_inc(ea_in[b], 16)
                        eng.dma_start(src_all[:, b, :], bc(dram["src_row"][bass.ds((i * R + b) * UNIT, UNIT)].rearrange(
                            "(o e) -> o e", o=1), [P, UNIT])).then_inc(ea_in[b], 16)

            @block.gpsimd
            def _(eng):
                for i in turns(eng, NI):
                    for b in range(R):
                        eng.wait_ge(idx_in[b], i * 16 + 16)
                        eng.wait_ge(summed[b], i)
                        mark(eng, marks)
                        for k in range(K4):
                            gather(eng, xs[:, b, k, :], x1, idx[:, b, k:k + 1]).then_inc(got[b], 16)
                            gather(eng, xd[:, b, k, :], x1, idx[:, b, 4 + k:5 + k]).then_inc(got[b], 16)
                    for b in range(R):
                        eng.wait_ge(total_in[b], i + 1)
                        eng.wait_ge(to_in[b], i + 1)
                        for k in range(K4):
                            eng.wait_ge(tab_added[k], (i * R + b) * 16)
                            mark(eng, marks)
                            eng.indirect_dma_start(out=tabs[k], out_offset=bass.IndirectOffsetOnAxis(ap=to_i[:, b, k:k + 1], axis=0),
                                                   in_=total[:, b, k, :], in_offset=None, compute_op=ALU.add).then_inc(tab_added[k], 16)
                for k in range(K4):
                    eng.wait_ge(tab_added[k], NU * 16)

            @block.vector
            def _(eng):
                for i in turns(eng, NI):
                    for b in range(R):
                        u = i * R + b
                        steps = Steps(eng, dve, u, IDX)
                        eng.wait_ge(ea_in[b], i * 32 + 32)
                        eng.wait_ge(summed[b], i)
                        build_hot(net, eng, hot, i, b).then_inc(hot_in[b], 1)
                        steps.done(eng.tensor_tensor(same[:, b], src_all[:, b, :].rearrange("p (q k) -> p k q", k=K4),
                                                     bc(net.src_f[:, bass.ds(u * K4, K4)].unsqueeze(2), [P, K4, P]), ALU.is_equal))
                        steps.settle()
                        steps.done(eng.tensor_tensor(before[:, :, :], same[:, b], bc(net.lower[:, :].unsqueeze(1), [P, K4, P]), ALU.mult))
                        steps.settle()
                        mark(eng, marks)
                        steps.done(eng.tensor_reduce(again[:, :], before[:, :, :], AX, ALU.max))
                        steps.done(eng.tensor_scalar(off[:, :], net.src_f[:, bass.ds(u * K4, K4)], -1.0, net.spare[:, 0:1], ALU.mult, ALU.add))
                        steps.settle()
                        steps.done(eng.tensor_tensor(off[:, :], off[:, :], again[:, :], ALU.mult))
                        eng.wait_ge(tab_added[K4 - 1], i * (16 * R))
                        for k in range(K4 - 1):
                            eng.wait_ge(tab_added[k], i * (16 * R))
                        steps.settle()
                        mark(eng, marks)
                        steps.done(eng.tensor_tensor(off[:, :], off[:, :], net.src_f[:, bass.ds(u * K4, K4)], ALU.add))
                        steps.settle()
                        mark(eng, marks)
                        eng.tensor_copy(to_i[:, b, :], off[:, :]).then_inc(to_in[b], 1)
                        eng.wait_ge(got[b], i * 128 + 128)
                        eng.tensor_tensor(xs[:, b], xs[:, b], ea[:, b], ALU.mult).then_inc(gated[b], 1)
                        eng.tensor_tensor(xd[:, b], xd[:, b], ea[:, b], ALU.mult).then_inc(gated[b], 1)
                        steps.end()
                    for b in range(R):
                        eng.wait_ge(summed[b], i + 1)
                        add_window(net, eng, i, b, [(acc, sums[b][:, :])], sums_free)

            @block.scalar
            def _(eng):
                for i in turns(eng, NI):
                    for b in range(R):
                        h = b % 2
                        eng.wait_ge(pre_in[h], i * (R // 2) + b // 2 + 1)
                        for k in range(K4):
                            eng.wait_ge(tab_added[k], i * (16 * R))
                        mark(eng, marks)
                        eng.activation(total[:, b], pres[h][:, :, :], ACT.Copy).then_inc(total_in[b], 1)

            @block.tensor
            def _(eng):
                for i in turns(eng, NI):
                    for b in range(R):
                        h = b % 2
                        eng.wait_ge(hot_in[b], i + 1)
                        eng.wait_ge(gated[b], i * 2 + 2)
                        eng.wait_ge(sums_free[b], i)
                        if b >= 2:
                            eng.wait_ge(total_in[b - 2], i + 1)
                        else:
                            eng.wait_ge(total_in[b + 2], i)
                        for k in range(K4):
                            mm = eng.matmul(pres[h][:, k, :], same[:, b, k, :], xd[:, b, k, :], start=True, stop=True)
                        mm.then_inc(pre_in[h], 1)
                        for k in range(K4):
                            mm = eng.matmul(sums[b][:, :], xs[:, b, k, :], hot[:, b, k, :], start=(k == 0), stop=(k == K4 - 1))
                        mm.then_inc(summed[b], 1)


def clear_tables(net, tabs):
    nc = net.nc
    n = net.scope("ct_")
    with n:
        zeros = n.sb("zeros", [P, NT, D])
        zeroed, written = n.sem("zeroed"), n.sem("written")
        with nc.Block() as block:
            @block.gpsimd
            def _(eng):
                eng.memset(zeros[:, :, :], 0.0).then_inc(zeroed, 1)

            @block.sync
            def _(eng):
                eng.wait_ge(zeroed, 1)
                for t in tabs:
                    eng.dma_start(t[0:NP, :].rearrange("(p t) d -> p t d", p=P), zeros[:, :, :]).then_inc(written, 16)
                    eng.dma_start(t[NP:TR, :], zeros[:, 0, :]).then_inc(written, 16)
                eng.wait_ge(written, 32 * len(tabs))


def nodes_gated(net, acc, tabs, x_row):
    nc, dram = net.nc, net.dram
    n = net.scope("n1_")
    PER = 1 + 3 + 2 + LN_STEPS
    with n:
        st = n.sb("st", [P, GC])
        parts = n.sb("parts", [P, K4, 4, D])
        z = n.sb("z", [P, 4, D])
        stats, moments, std = n.sb("stats", [P, 4, 6]), n.sb("moments", [P, 4, 2]), n.sb("std", [P, 4])
        turned = n.ps("turned", [P, GC])
        loaded, dve, turned_s, rooted, marks = (n.sem(s) for s in ("loaded", "dve", "turned_s", "rooted", "marks"))
        with nc.Block() as block:
            @block.sync
            def _(eng):
                for g in turns(eng, NG):
                    eng.wait_ge(dve, g * PER)
                    mark(eng, marks)
                    for k in range(K4):
                        eng.dma_start(parts[:, k], rows_of(tabs[k], g * GC)).then_inc(loaded, 16)

            @block.tensor
            def _(eng):
                for g in turns(eng, NG):
                    eng.wait_ge(dve, g * PER + 1)
                    for j in range(4):
                        mm = eng.transpose(turned[:, j * P:(j + 1) * P], st[:, j * P:(j + 1) * P], net.ident[:, :])
                    mm.then_inc(turned_s, 1)

            @block.scalar
            def _(eng):
                for g in turns(eng, NG):
                    eng.wait_ge(dve, g * PER + 6 + 9)
                    eng.activation(std[:, :], std[:, :], ACT.Sqrt).then_inc(rooted, 1)

            @block.vector
            def _(eng):
                for g in turns(eng, NG):
                    steps = Steps(eng, dve, g, PER)
                    steps.done(eng.tensor_copy(st[:, :], acc[:, bass.ds(g * GC, GC)]))
                    eng.wait_ge(loaded, g * (16 * K4) + 16 * K4)
                    steps.done(eng.tensor_tensor(parts[:, 0], parts[:, 0], parts[:, 1], ALU.add))
                    steps.done(eng.tensor_tensor(parts[:, 2], parts[:, 2], parts[:, 3], ALU.add))
                    steps.settle()
                    steps.done(eng.tensor_tensor(z[:, :, :], parts[:, 0], parts[:, 2], ALU.add))
                    steps.settle()
                    eng.wait_ge(turned_s, g + 1)
                    steps.done(eng.tensor_tensor(z[:, :, :], turned[:, :].rearrange("p (t d) -> p t d", d=D), z[:, :, :], ALU.add))
                    steps.settle()
                    steps.done(eng.tensor_tensor(z[:, :, :], z[:, :, :], x_row[:, bass.ds(g * 4, 4), :], ALU.add))
                    steps.settle()
                    layer_norm(eng, steps, z, stats, moments, std, x_row[:, bass.ds(g * 4, 4), :], marks, rooted, g + 1, 1e-5)
                    steps.end()


def edges_attention(net, kv, q, acc, acc_z):
    nc, dram = net.nc, net.dram
    n = net.scope("l2_")
    PER = 3
    with n:
        idx = n.sb("idx", [P, R, 8], I32)
        kvs = n.sb("kvs", [P, R, K4, 2 * D])
        qd = n.sb("qd", [P, R, K4, D])
        hot = n.sb("hot", [P, R, K4, P])
        s = n.sb("s", [P, R, K4, H])
        msg = n.sb("msg", [P, R, K4, D])
        sums = [n.ps(f"sums{b}", [P, P]) for b in range(R)]
        zs = [n.ps(f"zs{b}", [H, P]) for b in range(R)]
        got = n.gather_sems("got", R)
        idx_in, hot_in, scored, weighed, ready, summed, sums_free = (n.sems(x, R) for x in (
            "idx_in", "hot_in", "scored", "weighed", "ready", "summed", "sums_free"))
        marks, dve = n.sem("marks"), n.sem("dve")
        with nc.Block() as block:
            @block.sync
            def _(eng):
                for i in turns(eng, NI):
                    for b in range(R):
                        index_loads(net, eng, i, b, idx, idx_in, got, 128)

            @block.gpsimd
            def _(eng):
                for i in turns(eng, NI):
                    for b in range(R):
                        eng.wait_ge(idx_in[b], i * 16 + 16)
                        eng.wait_ge(ready[b], i)
                        mark(eng, marks)
                        for k in range(K4):
                            gather(eng, kvs[:, b, k, :], kv, idx[:, b, k:k + 1]).then_inc(got[b], 16)
                            gather(eng, qd[:, b, k, :], q, idx[:, b, 4 + k:5 + k]).then_inc(got[b], 16)

            @block.vector
            def _(eng):
                for i in turns(eng, NI):
                    for b in range(R):
                        u = i * R + b
                        steps = Steps(eng, dve, u, PER)
                        eng.wait_ge(summed[b], i)
                        build_hot(net, eng, hot, i, b).then_inc(hot_in[b], 1)
                        eng.wait_ge(got[b], i * 128 + 128)
                        steps.done(eng.tensor_tensor(qd[:, b], qd[:, b], kvs[:, b, :, 0:D], ALU.mult))
                        steps.settle()
                        mark(eng, marks)
                        steps.done(eng.tensor_reduce(s[:, b], qd[:, b].rearrange("p k (h c) -> p k h c", h=H), AX, ALU.add))
                        steps.settle()
                        steps.done(eng.tensor_scalar(s[:, b], s[:, b], 1.0 / DH ** 0.5, 5.0, ALU.mult, ALU.min))
                        steps.settle()
                        eng.tensor_scalar(s[:, b], s[:, b], -5.0, None, ALU.max).then_inc(scored[b], 1)
                        eng.wait_ge(weighed[b], i + 1)
                        eng.tensor_tensor(msg[:, b].rearrange("p k (h c) -> p k h c", h=H),
                                          kvs[:, b, :, D:2 * D].rearrange("p k (h c) -> p k h c", h=H),
                                          bc(s[:, b].unsqueeze(3), [P, K4, H, DH]), ALU.mult).then_inc(ready[b], 1)
                        steps.end()
                    for b in range(R):
                        eng.wait_ge(summed[b], i + 1)
                        add_window(net, eng, i, b, [(acc, sums[b][:, :]), (acc_z, zs[b][:, :])], sums_free)

            @block.scalar
            def _(eng):
                for i in turns(eng, NI):
                    for b in range(R):
                        eng.wait_ge(scored[b], i + 1)
                        eng.activation(s[:, b], s[:, b], ACT.Exp).then_inc(weighed[b], 1)

            @block.tensor
            def _(eng):
                for i in turns(eng, NI):
                    for b in range(R):
                        eng.wait_ge(hot_in[b], i + 1)
                        eng.wait_ge(sums_free[b], i * 2)
                        eng.wait_ge(weighed[b], i + 1)
                        mark(eng, marks)
                        for k in range(K4):
                            eng.matmul(zs[b][:, :], s[:, b, k, :], hot[:, b, k, :], start=(k == 0), stop=(k == K4 - 1))
                        eng.wait_ge(ready[b], i + 1)
                        for k in range(K4):
                            mm = eng.matmul(sums[b][:, :], msg[:, b, k, :], hot[:, b, k, :], start=(k == 0), stop=(k == K4 - 1))
                        mm.then_inc(summed[b], 1)


def nodes_attention(net, acc, acc_z, x_row, x_T):
    nc, dram = net.nc, net.dram
    n = net.scope("n2_")
    with n:
        hx = n.sb("hx", [P, NP])
        wo, w1, w2 = n.sb("wo", [D, D]), n.sb("w1", [D, 2, P]), n.sb("w2", [P, 2, D])
        bo, b1, b2 = n.sb("bo", [P, 1]), n.sb("b1", [P, 2]), n.sb("b2", [P, 1])
        bn = n.sb("bn", [P, 4])
        z = n.sb("z", [H, GC])
        h, h1 = n.sb("h", [P, GC]), n.sb("h1", [P, 2, GC])
        stats, mv, coef, std = n.sb("stats", [P, NG, 6]), n.sb("mv", [P, 2]), n.sb("coef", [P, 2]), n.sb("std", [P, 1])
        pz, po = n.ps("pz", [P, GC]), n.ps("po", [P, GC])
        p1 = [n.ps(f"p1{f}", [P, GC]) for f in range(2)]
        marks = n.sem("marks")

        def batch_coefficients(name, gain, bias):
            dve, rooted = n.sem(name + "dve"), n.sem(name + "rooted")
            with nc.Block() as block:
                @block.scalar
                def _(eng):
                    eng.wait_ge(dve, 2)
                    eng.activation(std[:, :], std[:, :], ACT.Sqrt).then_inc(rooted, 1)

                @block.vector
                def _(eng):
                    steps = Steps(eng, dve)
                    steps.done(eng.bn_aggr(mv[:, :], stats[:, :, :]))
                    steps.settle()
                    steps.done(eng.tensor_scalar(std[:, :], mv[:, 1:2], 1e-5, None, ALU.add))
                    eng.wait_ge(rooted, 1)
                    steps.done(eng.reciprocal(std[:, :], std[:, :]))
                    steps.settle()
                    steps.done(eng.tensor_tensor(coef[:, 0:1], std[:, :], gain, ALU.mult))
                    steps.settle()
                    steps.done(eng.tensor_tensor(std[:, :], mv[:, 0:1], coef[:, 0:1], ALU.mult))
                    steps.settle()
                    steps.done(eng.tensor_tensor(coef[:, 1:2], bias, std[:, :], ALU.subtract))

        loaded, dve, spread, made = n.sem("loaded"), n.sem("dve"), n.sem("spread"), n.sem("made")
        with nc.Block() as block:
            @block.sync
            def _(eng):
                eng.dma_start(wo[:, :], dram["L2_gnn_Wo"]).then_inc(loaded, 16)
                eng.dma_start(w1[:, :, :], dram["L2_gnn_W1"].rearrange("d (f o) -> d f o", f=2)).then_inc(loaded, 16)
                eng.dma_start(w2[:, :, :], dram["L2_gnn_W2"].rearrange("(f o) d -> o f d", f=2)).then_inc(loaded, 16)
                eng.dma_start(bo[:, :], cols(dram["L2_gnn_bo"])).then_inc(loaded, 16)
                for f in range(2):
                    eng.dma_start(b1[:, f:f + 1], cols(dram["L2_gnn_b1"][f * P:(f + 1) * P])).then_inc(loaded, 16)
                eng.dma_start(b2[:, :], cols(dram["L2_gnn_b2"])).then_inc(loaded, 16)
                for c, name in enumerate(("bn1_g", "bn1_b", "bn2_g", "bn2_b")):
                    eng.dma_start(bn[:, c:c + 1], cols(dram["L2_gnn_" + name])).then_inc(loaded, 16)
                eng.wait_ge(loaded, 16 * 11)

            @block.vector
            def _(eng):
                eng.wait_ge(loaded, 16 * 11)

                def group(g, width):
                    steps = Steps(eng, dve, g, 5)
                    steps.done(eng.tensor_scalar(z[:, :], acc_z[:, bass.ds(g * GC, GC)], 1e-6, None, ALU.add))
                    steps.settle()
                    steps.done(eng.reciprocal(z[:, :], z[:, :]))
                    eng.wait_ge(spread, g + 1)
                    steps.done(eng.tensor_tensor(h[:, :], acc[:, bass.ds(g * GC, GC)], pz[:, :], ALU.mult))
                    eng.wait_ge(made, g + 1)
                    steps.done(eng.scalar_tensor_tensor(out=hx[:, bass.ds(g * GC, GC)], in0=po[:, :], scalar=bo[:, 0:1],
                                                        in1=x_T[:, bass.ds(g * GC, GC)], op0=ALU.add, op1=ALU.add))
                    steps.settle()
                    mark(eng, marks)
                    steps.done(eng.bn_stats(stats[:, bass.ds(g, 1), :].rearrange("p a s -> p (a s)"), hx[:, bass.ds(g * GC, width)]))
                    steps.end()

                for g in turns(eng, NG - 1):
                    group(g, GC)
                group(NG - 1, LASTN)

            @block.tensor
            def _(eng):
                for g in turns(eng, NG):
                    eng.wait_ge(dve, g * 5 + 2)
                    eng.matmul(pz[:, :], net.expand[:, :], z[:, :], start=True, stop=True).then_inc(spread, 1)
                    eng.wait_ge(dve, g * 5 + 3)
                    eng.matmul(po[:, :], wo[:, :], h[:, :], start=True, stop=True).then_inc(made, 1)
        batch_coefficients("a_", bn[:, 0:1], bn[:, 1:2])

        dve, hid, relu, made2 = n.sem("dve2"), n.sem("hid"), n.sem("relu"), n.sem("made2")
        with nc.Block() as block:
            @block.vector
            def _(eng):
                def group(g, width):
                    steps = Steps(eng, dve, g, 3)
                    steps.done(eng.tensor_scalar(h[:, :], hx[:, bass.ds(g * GC, GC)], coef[:, 0:1], coef[:, 1:2], ALU.mult, ALU.add))
                    steps.settle()
                    eng.wait_ge(made2, g + 1)
                    steps.done(eng.scalar_tensor_tensor(out=hx[:, bass.ds(g * GC, GC)], in0=po[:, :], scalar=b2[:, 0:1],
                                                        in1=h[:, :], op0=ALU.add, op1=ALU.add))
                    steps.settle()
                    mark(eng, marks)
                    steps.done(eng.bn_stats(stats[:, bass.ds(g, 1), :].rearrange("p a s -> p (a s)"), hx[:, bass.ds(g * GC, width)]))
                    steps.end()

                for g in turns(eng, NG - 1):
                    group(g, GC)
                group(NG - 1, LASTN)

            @block.scalar
            def _(eng):
                for g in turns(eng, NG):
                    for f in range(2):
                        eng.wait_ge(hid, g * 2 + f + 1)
                        eng.activation(h1[:, f, :], p1[f][:, :], ACT.Relu, bias=b1[:, f:f + 1]).then_inc(relu, 1)

            @block.tensor
            def _(eng):
                for g in turns(eng, NG):
                    eng.wait_ge(dve, g * 3 + 1)
                    for f in range(2):
                        eng.matmul(p1[f][:, :], w1[:, f, :], h[:, :], start=True, stop=True).then_inc(hid, 1)
                    for f in range(2):
                        eng.wait_ge(relu, g * 2 + f + 1)
                        mm = eng.matmul(po[:, :], w2[:, f, :], h1[:, f, :], start=(f == 0), stop=(f == 1))
                    mm.then_inc(made2, 1)
        batch_coefficients("b_", bn[:, 2:3], bn[:, 3:4])

        PER = 2 + LN_STEPS
        y = h1[:, 0, :].rearrange("p (t d) -> p t d", d=D)
        rs, rm, rstd = n.sb("rs", [P, 4, 6]), n.sb("rm", [P, 4, 2]), n.sb("rstd", [P, 4])
        dve, turned, rooted = n.sem("dve3"), n.sem("turned"), n.sem("rooted")
        with nc.Block() as block:
            @block.vector
            def _(eng):
                for g in turns(eng, NG):
                    steps = Steps(eng, dve, g, PER)
                    steps.done(eng.tensor_scalar(h[:, :], hx[:, bass.ds(g * GC, GC)], coef[:, 0:1], coef[:, 1:2], ALU.mult, ALU.add))
                    eng.wait_ge(turned, g + 1)
                    steps.done(eng.tensor_tensor(y, po[:, :].rearrange("p (t d) -> p t d", d=D), x_row[:, bass.ds(g * 4, 4), :], ALU.add))
                    steps.settle()
                    layer_norm(eng, steps, y, rs, rm, rstd, x_row[:, bass.ds(g * 4, 4), :], marks, rooted, g + 1, 1e-5)
                    steps.end()

            @block.scalar
            def _(eng):
                for g in turns(eng, NG):
                    eng.wait_ge(dve, g * PER + 2 + 9)
                    eng.activation(rstd[:, :], rstd[:, :], ACT.Sqrt).then_inc(rooted, 1)

            @block.tensor
            def _(eng):
                for g in turns(eng, NG):
                    eng.wait_ge(dve, g * PER + 1)
                    for j in range(4):
                        mm = eng.transpose(po[:, j * P:(j + 1) * P], h[:, j * P:(j + 1) * P], net.ident[:, :])
                    mm.then_inc(turned, 1)


def hyperbolic(net, x_row, kvm, qm):
    nc, dram = net.nc, net.dram
    n = net.scope("hy_")
    with n:
        xx = n.sb("xx", [P, 4, D])
        m = n.sb("m", [P, 2, 4, D])
        norm, y, th, f = (n.sb(s, [P, NT]) for s in ("norm", "y", "th", "f"))
        c, most = n.sb("c", [P, 2]), n.sb("most", [P, 1])
        loaded, squared, dve, act, made, stored, marks = (n.sem(s) for s in ("loaded", "squared", "dve", "act", "made", "stored", "marks"))
        with nc.Block() as block:
            @block.sync
            def _(eng):
                eng.dma_start(c[:, 0:1], everywhere(dram["L3_gnn_c_mag"], 1)).then_inc(loaded, 16)
                for g in turns(eng, NG):
                    eng.wait_ge(made, g * 4 + 4)
                    mark(eng, marks)
                    eng.dma_start(rows_of(kvm, g * GC)[:, :, 2 * D:3 * D], m[:, 0]).then_inc(stored, 16)
                    eng.dma_start(rows_of(qm, g * GC)[:, :, D:2 * D], m[:, 0]).then_inc(stored, 16)
                eng.wait_ge(stored, 32 * NG)

            @block.scalar
            def _(eng):
                eng.wait_ge(dve, 4)
                eng.activation(norm[:, :], norm[:, :], ACT.Sqrt).then_inc(act, 1)
                eng.activation(c[:, 1:2], c[:, 0:1], ACT.Sqrt).then_inc(act, 1)
                eng.wait_ge(dve, 5)
                eng.activation(th[:, :], y[:, :], ACT.Tanh).then_inc(act, 1)

            @block.vector
            def _(eng):
                for g in turns(eng, NG):
                    eng.wait_ge(squared, g * 2)
                    mark(eng, marks)
                    eng.tensor_tensor(xx[:, :, :], x_row[:, bass.ds(g * 4, 4), :], x_row[:, bass.ds(g * 4, 4), :], ALU.mult).then_inc(squared, 1)
                    eng.wait_ge(squared, g * 2 + 1)
                    mark(eng, marks)
                    eng.tensor_reduce(norm[:, bass.ds(g * 4, 4)], xx[:, :, :], AX, ALU.add).then_inc(squared, 1)
                eng.wait_ge(squared, 2 * NG)
                eng.wait_ge(loaded, 16)
                steps = Steps(eng, dve)
                steps.done(eng.tensor_scalar(norm[:, :], norm[:, :], 1e-30, None, ALU.max))
                steps.done(eng.tensor_scalar(c[:, 1:2], c[:, 0:1], -1.0, None, ALU.mult))
                steps.settle()
                steps.done(eng.tensor_tensor(c[:, 0:1], c[:, 0:1], c[:, 1:2], ALU.max))
                steps.settle()
                steps.done(eng.tensor_scalar(c[:, 0:1], c[:, 0:1], 1e-15, None, ALU.max))
                eng.wait_ge(act, 2)
                steps.done(eng.tensor_scalar(y[:, :], norm[:, :], c[:, 1:2], None, ALU.mult))
                steps.settle()
                eng.wait_ge(act, 3)
                steps.done(eng.reciprocal(f[:, :], y[:, :]))
                steps.done(eng.reciprocal(most[:, :], c[:, 1:2]))
                steps.settle()
                steps.done(eng.tensor_tensor(f[:, :], f[:, :], th[:, :], ALU.mult))
                steps.done(eng.tensor_scalar(most[:, :], most[:, :], 1.0 - 1e-5, None, ALU.mult))
                steps.settle()
                steps.done(eng.tensor_tensor(norm[:, :], norm[:, :], f[:, :], ALU.mult))
                steps.settle()
                steps.done(eng.reciprocal(norm[:, :], norm[:, :]))
                steps.settle()
                steps.done(eng.tensor_scalar(norm[:, :], norm[:, :], most[:, 0:1], 1.0, ALU.mult, ALU.min))
                steps.settle()
                steps.done(eng.tensor_tensor(f[:, :], f[:, :], norm[:, :], ALU.mult))
                steps.settle()
                for g in turns(eng, NG):
                    eng.wait_ge(stored, g * 32)
                    mark(eng, marks)
                    for j in range(4):
                        eng.tensor_scalar(m[:, 0, j, :], x_row[:, bass.ds(g * 4 + j, 1), :].rearrange("p a d -> p (a d)"),
                                          f[:, bass.ds(g * 4 + j, 1)], None, ALU.mult).then_inc(made, 1)


def edges_relational(net, kvm, qm, dot, dec, dist2, v_rows):
    nc, dram = net.nc, net.dram
    n = net.scope("l3_")
    with n:
        idx = n.sb("idx", [P, R, 8], I32)
        ks = n.sb("ks", [P, R, K4, 3 * D])
        qd = n.sb("qd", [P, R, K4, 2 * D])
        te = n.sb("te", [TE, R, UNIT])
        wadd = n.sb("wadd", [TE, 3, D])
        wd1 = n.sb("wd1", [TE, P])
        wd2 = n.sb("wd2", [P, H])
        hid = n.sb("hid", [P, UNIT])
        adds = n.ps("adds", [P, K4, GC])
        ph, pd = n.ps("ph", [P, UNIT]), n.ps("pd", [P, K4, H])
        got = n.gather_sems("got", R)
        idx_in, te_in, v_out, dotted, vs_in = (n.sems(x, R) for x in ("idx_in", "te_in", "v_out", "dotted", "vs_in"))
        zeroed, loaded, marks, dve, hid_in, relu, pd_in, added, squared = (n.sem(x) for x in (
            "zeroed", "loaded", "marks", "dve", "hid_in", "relu", "pd_in", "added", "squared"))
        adds_free, dec_out, scaled = n.sem("adds_free"), n.sem("dec_out"), n.sem("scaled")
        PER = 5
        with nc.Block() as block:
            @block.sync
            def _(eng):
                eng.wait_ge(zeroed, 3)
                eng.dma_start(wadd[0:32, 0, :], dram["L3_gnn_Wt"]).then_inc(loaded, 16)
                eng.dma_start(wadd[33:34, 0, :], dram["L3_gnn_bt"].rearrange("(o d) -> o d", o=1)).then_inc(loaded, 16)
                for c, name in enumerate(("rel_k", "rel_q", "rel_v")):
                    for t in range(2):
                        eng.dma_start(wadd[35 - t:36 - t, c, :], dram["L3_gnn_" + name][t:t + 1, :]).then_inc(loaded, 16)
                eng.dma_start(wd1[32:33, 0:HID], dram["L3_gnn_Wd1"][0:1, :]).then_inc(loaded, 16)
                eng.dma_start(wd1[34:35, 0:HID], dram["L3_gnn_Wd1"][1:2, :]).then_inc(loaded, 16)
                eng.dma_start(wd1[33:34, 0:HID], dram["L3_gnn_bd1"].rearrange("(o d) -> o d", o=1)).then_inc(loaded, 16)
                eng.dma_start(wd1[33:34, HID:HID + 1], dram["one"].rearrange("(o d) -> o d", o=1)).then_inc(loaded, 16)
                eng.dma_start(wd2[0:HID, :], dram["L3_gnn_Wd2"]).then_inc(loaded, 16)
                eng.dma_start(wd2[HID:HID + 1, :], dram["L3_gnn_bd2"].rearrange("(o d) -> o d", o=1)).then_inc(loaded, 16)
                for i in turns(eng, NI):
                    for b in range(R):
                        u = i * R + b
                        index_loads(net, eng, i, b, idx, idx_in, got, 128)
                        eng.wait_ge(vs_in[b], i)
                        mark(eng, marks)
                        eng.dma_start(te[0:34, b, :], dram["te"][:, bass.ds(u * UNIT, UNIT)]).then_inc(te_in[b], 16)
                        eng.dma_start(te[34:36, b, :], net.type_rows[:, bass.ds(u * UNIT, UNIT)]).then_inc(te_in[b], 16)

            @block.gpsimd
            def _(eng):
                for w in (wd1, wd2):
                    eng.memset(w[:, :], 0.0).then_inc(zeroed, 1)
                eng.memset(wadd[:, :, :], 0.0).then_inc(zeroed, 1)
                for i in turns(eng, NI):
                    for b in range(R):
                        eng.wait_ge(idx_in[b], i * 16 + 16)
                        eng.wait_ge(dotted[b], i * 2)
                        eng.wait_ge(v_out[b], i * 16)
                        mark(eng, marks)
                        for k in range(K4):
                            gather(eng, ks[:, b, k, :], kvm, idx[:, b, k:k + 1]).then_inc(got[b], 16)
                            gather(eng, qd[:, b, k, :], qm, idx[:, b, 4 + k:5 + k]).then_inc(got[b], 16)

            @block.vector
            def _(eng):
                eng.wait_ge(loaded, 16 * 14)
                eng.tensor_scalar(wd1[:, :], wd1[:, :], net.type_scale[0:TE, 0:1], None, ALU.mult).then_inc(scaled, 1)
                for i in turns(eng, NI):
                    for b in range(R):
                        u = i * R + b
                        steps = Steps(eng, dve, u, PER)
                        eng.wait_ge(got[b], i * 128 + 128)
                        mk = ks[:, b, :, 2 * D:3 * D]
                        steps.done(eng.tensor_tensor(mk, mk, qd[:, b, :, D:2 * D], ALU.subtract))
                        eng.wait_ge(added, u + 1)
                        steps.done(eng.tensor_tensor(ks[:, b, :, 0:D], ks[:, b, :, 0:D], adds[:, :, 0:D], ALU.add))
                        steps.done(eng.tensor_tensor(qd[:, b, :, 0:D], qd[:, b, :, 0:D], adds[:, :, D:2 * D], ALU.add))
                        eng.tensor_tensor(ks[:, b, :, D:2 * D], ks[:, b, :, D:2 * D], adds[:, :, 2 * D:3 * D], ALU.add).then_inc(vs_in[b], 1)
                        steps.settle()
                        steps.done(eng.tensor_tensor(qd[:, b, :, 0:D], qd[:, b, :, 0:D], ks[:, b, :, 0:D], ALU.mult))
                        steps.settle()
                        mark(eng, marks)
                        eng.tensor_reduce(dot[:, bass.ds(u * K4, K4), :], qd[:, b, :, 0:D].rearrange("p k (h c) -> p k h c", h=H),
                                          AX, ALU.add).then_inc(dotted[b], 1)
                        eng.wait_ge(squared, u + 1)
                        mark(eng, marks)
                        eng.tensor_reduce(dist2[:, bass.ds(u * K4, K4)], mk, AX, ALU.add).then_inc(dotted[b], 1)
                        eng.wait_ge(pd_in, u + 1)
                        mark(eng, marks)
                        steps.done(eng.tensor_copy(dec[:, bass.ds(u * K4, K4), :], pd[:, :, :]))
                        steps.end()

            @block.scalar
            def _(eng):
                for i in turns(eng, NI):
                    for b in range(R):
                        u = i * R + b
                        eng.wait_ge(hid_in, u + 1)
                        eng.activation(hid[:, :], ph[:, :], ACT.Relu).then_inc(relu, 1)
                        eng.wait_ge(dve, u * PER + 1)
                        mk = ks[:, b, :, 2 * D:3 * D]
                        eng.activation(mk, mk, ACT.Square).then_inc(squared, 1)
                        eng.wait_ge(vs_in[b], i + 1)
                        mark(eng, marks)
                        eng.dma_start(v_rows[bass.ds(u * UNIT, UNIT), :].rearrange("(p k) d -> p k d", k=K4),
                                      ks[:, b, :, D:2 * D]).then_inc(v_out[b], 16)
                for b in range(R):
                    eng.wait_ge(v_out[b], NI * 16)

            @block.tensor
            def _(eng):
                eng.wait_ge(scaled, 1)
                for i in turns(eng, NI):
                    for b in range(R):
                        u = i * R + b
                        eng.wait_ge(te_in[b], i * 32 + 32)
                        eng.wait_ge(relu, u)
                        eng.matmul(ph[:, :], wd1[:, :], te[:, b, :], start=True, stop=True).then_inc(hid_in, 1)
                        eng.wait_ge(dve, u * PER)
                        if b:
                            eng.wait_ge(vs_in[b - 1], i + 1)
                        else:
                            eng.wait_ge(vs_in[R - 1], i)
                        for k in range(K4):
                            mm = eng.matmul(adds[:, k, 0:3 * D], te[:, b, k * P:(k + 1) * P], wadd[:, :, :].rearrange("t c d -> t (c d)"),
                                            start=True, stop=True)
                        mm.then_inc(added, 1)
                        eng.wait_ge(relu, u + 1)
                        for k in range(K4):
                            mm = eng.matmul(pd[:, k, :], hid[:, k * P:(k + 1) * P], wd2[:, :], start=True, stop=True)
                        mm.then_inc(pd_in, 1)


def logits(net, dot, dec, dist2):
    nc, dram = net.nc, net.dram
    n = net.scope("lg_")
    with n:
        small = n.sb("small", [P, 6, H])
        far = n.sb("far", [P, NU * K4, H])
        loaded, dve, act = n.sem("loaded"), n.sem("dve"), n.sem("act")
        every = [P, NU * K4, H]
        with nc.Block() as block:
            @block.sync
            def _(eng):
                for c, name in enumerate(("decay_scale", "logit_alpha", "hyp_beta")):
                    eng.dma_start(small[:, c, :], everywhere(dram["L3_gnn_" + name], H)).then_inc(loaded, 16)
                eng.wait_ge(loaded, 48)

            @block.scalar
            def _(eng):
                eng.activation(dec[:, :, :], dec[:, :, :], ACT.Tanh).then_inc(act, 1)
                eng.wait_ge(loaded, 48)
                eng.activation(small[:, 3, :], small[:, 1, :], ACT.Exp, scale=-1.0).then_inc(act, 1)
                eng.wait_ge(dve, 1)
                eng.activation(dec[:, :, :], dec[:, :, :], ACT.Exp).then_inc(act, 1)
                eng.activation(dist2[:, :], dist2[:, :], ACT.Sqrt).then_inc(act, 1)

            @block.vector
            def _(eng):
                steps = Steps(eng, dve)
                eng.wait_ge(loaded, 48)
                eng.wait_ge(act, 2)
                steps.done(eng.tensor_tensor(dec[:, :, :], dec[:, :, :], bc(small[:, 0, :].unsqueeze(1), every), ALU.mult))
                steps.done(eng.tensor_scalar(small[:, 3, :], small[:, 3, :], 1.0, None, ALU.add))
                steps.settle()
                steps.done(eng.reciprocal(small[:, 4, :], small[:, 3, :]))
                steps.settle()
                steps.done(eng.tensor_scalar(small[:, 5, :], small[:, 4, :], -1.0, 1.0, ALU.mult, ALU.add))
                steps.done(eng.tensor_scalar(small[:, 3, :], small[:, 4, :], 1.0 / DH ** 0.5, None, ALU.mult))
                steps.settle()
                steps.done(eng.tensor_tensor(small[:, 5, :], small[:, 5, :], small[:, 2, :], ALU.mult))
                steps.done(eng.tensor_tensor(dot[:, :, :], dot[:, :, :], bc(small[:, 3, :].unsqueeze(1), every), ALU.mult))
                steps.settle()
                eng.wait_ge(act, 4)
                steps.done(eng.tensor_tensor(far[:, :, :], bc(dist2[:, :].unsqueeze(2), every), bc(small[:, 5, :].unsqueeze(1), every), ALU.mult))
                steps.settle()
                steps.done(eng.tensor_tensor(dot[:, :, :], dot[:, :, :], far[:, :, :], ALU.subtract))
                steps.settle()
                steps.done(eng.tensor_tensor(dot[:, :, :], dot[:, :, :], dec[:, :, :], ALU.mult))


def segment_softmax(net, dot):
    nc, dram = net.nc, net.dram
    n = net.scope("sm_")
    last = CE - 1
    with n:
        lt = n.sb("lt", [P, CE])
        pen = n.sb("pen", [P, CE + 1])
        run = n.sb("run", [P, CE])
        best = n.sb("best", [P, CE])
        stage = n.sb("stage", [P, K4, P])
        edge_dst = n.sb("edge_dst", [P, 2])
        pair = n.sb("pair", [P, 2])
        carry = n.sb("carry", [H, 3, CH])
        start = n.sb("start", [P, 1])
        turned = n.ps("turned", [P, K4, P])
        loaded, staged, turned_s, placed, marks, dve = (n.sem(s) for s in ("loaded", "staged", "turned_s", "placed", "marks", "dve"))
        cells = net.table("cells", (2, P, 2))
        carried = net.table("carried", (2, CH, H))
        chunks = net.dst_rows.rearrange("(c e) -> c e", c=CH)
        view = dot[:, :, :].rearrange("p (c j k) h -> p c j k h", c=CH, k=K4)
        with nc.Block() as block:
            @block.gpsimd
            def _(eng):
                eng.memset(edge_dst[:, :], -1.0).then_inc(marks, 1)

            @block.sync
            def _(eng):
                for c in range(CH):
                    eng.dma_start(best[c * H:(c + 1) * H, :], bc(chunks[c:c + 1, :], [H, CE])).then_inc(loaded, 16)
                eng.wait_ge(marks, 1)
                for c in range(1, CH):
                    eng.dma_start(edge_dst[c * H:(c + 1) * H, 0:1], bc(chunks[c - 1:c, last:CE], [H, 1])).then_inc(loaded, 16)
                for c in range(CH - 1):
                    eng.dma_start(edge_dst[c * H:(c + 1) * H, 1:2], bc(chunks[c + 1:c + 2, 0:1], [H, 1])).then_inc(loaded, 16)
                eng.wait_ge(loaded, 16 * (3 * CH - 2))

            @block.vector
            def _(eng):
                for j in turns(eng, CU):
                    eng.wait_ge(turned_s, j)
                    mark(eng, staged)
                    for k in range(K4):
                        eng.tensor_copy(stage[:, k, :].rearrange("p (c a h) -> p c a h", a=1, h=H),
                                        view[:, :, bass.ds(j, 1), k, :]).then_inc(staged, 1)
                    eng.wait_ge(turned_s, j + 1)
                    mark(eng, placed)
                    eng.tensor_copy(lt[:, bass.ds(j * UNIT, UNIT)].rearrange("p (q k) -> p k q", k=K4), turned[:, :, :]).then_inc(placed, 1)

            @block.tensor
            def _(eng):
                for j in turns(eng, CU):
                    eng.wait_ge(placed, j * 2)
                    eng.wait_ge(staged, j * 5 + 5)
                    for k in range(K4):
                        mm = eng.transpose(turned[:, k, :], stage[:, k, :], net.ident[:, :])
                    mm.then_inc(turned_s, 1)

        with nc.Block() as block:
            @block.vector
            def _(eng):
                steps = Steps(eng, dve)
                d = best
                steps.done(eng.tensor_tensor(pen[:, 1:CE], d[:, 1:CE], d[:, 0:CE - 1], ALU.not_equal))
                steps.done(eng.tensor_tensor(pen[:, 0:1], d[:, 0:1], edge_dst[:, 0:1], ALU.not_equal))
                steps.done(eng.tensor_tensor(pen[:, CE:CE + 1], d[:, last:CE], edge_dst[:, 1:2], ALU.not_equal))
                steps.done(eng.tensor_tensor(start[:, :], d[:, 0:1], d[:, last:CE], ALU.not_equal))
                steps.settle()
                steps.done(eng.tensor_scalar(pen[:, :], pen[:, :], -BIG, None, ALU.mult))
                steps.done(eng.tensor_scalar(start[:, :], start[:, :], -BIG, None, ALU.mult))
                steps.settle()
                steps.done(eng.tensor_tensor_scan(run[:, :], pen[:, 0:CE], lt[:, :], -BIG, ALU.add, ALU.max))
                steps.done(eng.tensor_tensor(pair[:, 0:1], start[:, :], pen[:, 0:1], ALU.add))
                steps.settle()
                steps.done(eng.tensor_copy(pair[:, 1:2], run[:, last:CE]))

        def carry_over(name, at, backward):
            wrote, scanned = n.sem(name + "wrote"), n.sem(name + "scanned")
            with nc.Block() as block:
                @block.sync
                def _(eng):
                    eng.dma_start(cells[at], pair[:, :]).then_inc(wrote, 16)
                    eng.wait_ge(wrote, 16)
                    for w in range(2):
                        eng.dma_start(carry[:, w, :], cells[at, :, w:w + 1].rearrange("(c h) o -> h (c o)", h=H), allow_slow_non_contiguous=True).then_inc(wrote, 16)
                    eng.wait_ge(scanned, 2)
                    eng.dma_start(carried[at].rearrange("c h -> h c"), carry[:, 2, :], allow_slow_non_contiguous=True).then_inc(wrote, 16)
                    eng.wait_ge(wrote, 64)
                    lo, hi = (0, P - H) if backward else (H, P)
                    rows = carried[at].rearrange("c h -> (c h)").rearrange("(p o) -> p o", o=1)
                    eng.dma_start(start[lo:hi, :], rows[H:P, :] if backward else rows[0:P - H, :]).then_inc(wrote, 16)
                    eng.wait_ge(wrote, 80)

                @block.vector
                def _(eng):
                    eng.memset(start[:, :], -BIG).then_inc(scanned, 1)
                    eng.wait_ge(wrote, 48)
                    s = slice(None, None, -1) if backward else slice(None)
                    eng.tensor_tensor_scan(carry[:, 2, s], carry[:, 0, s], carry[:, 1, s], -BIG, ALU.add, ALU.max).then_inc(scanned, 1)

        carry_over("f_", 0, False)
        dve2 = n.sem("dve2")
        with nc.Block() as block:
            @block.vector
            def _(eng):
                steps = Steps(eng, dve2)
                steps.done(eng.tensor_tensor_scan(run[:, :], pen[:, 0:CE], lt[:, :], start[:, 0:1], ALU.add, ALU.max))
                steps.settle()
                steps.done(eng.tensor_tensor_scan(best[:, ::-1], pen[:, 1:CE + 1][:, ::-1], run[:, ::-1], -BIG, ALU.add, ALU.max))
                steps.done(eng.tensor_tensor(pair[:, 0:1], pair[:, 0:1], pen[:, 0:1], ALU.subtract))
                steps.settle()
                steps.done(eng.tensor_tensor(pair[:, 0:1], pair[:, 0:1], pen[:, CE:CE + 1], ALU.add))
                steps.done(eng.tensor_copy(pair[:, 1:2], best[:, 0:1]))
        carry_over("b_", 1, True)
        dve3, act = n.sem("dve3"), n.sem("act")
        with nc.Block() as block:
            @block.vector
            def _(eng):
                steps = Steps(eng, dve3)
                steps.done(eng.tensor_tensor_scan(best[:, ::-1], pen[:, 1:CE + 1][:, ::-1], run[:, ::-1], start[:, 0:1], ALU.add, ALU.max))
                steps.settle()
                steps.done(eng.tensor_tensor(lt[:, :], lt[:, :], best[:, :], ALU.subtract))

            @block.scalar
            def _(eng):
                eng.wait_ge(dve3, 2)
                eng.activation(lt[:, :], lt[:, :], ACT.Exp).then_inc(act, 1)

        staged, turned_s, placed = n.sem("staged2"), n.sem("turned2"), n.sem("placed2")
        with nc.Block() as block:
            @block.vector
            def _(eng):
                for j in turns(eng, CU):
                    eng.wait_ge(turned_s, j)
                    mark(eng, staged)
                    eng.tensor_copy(stage[:, :, :], lt[:, bass.ds(j * UNIT, UNIT)].rearrange("p (q k) -> p k q", k=K4)).then_inc(staged, 1)
                    eng.wait_ge(turned_s, j + 1)
                    mark(eng, placed)
                    for k in range(K4):
                        eng.tensor_copy(view[:, :, bass.ds(j, 1), k, :],
                                        turned[:, k, :].rearrange("p (c a h) -> p c a h", a=1, h=H)).then_inc(placed, 1)

            @block.tensor
            def _(eng):
                for j in turns(eng, CU):
                    eng.wait_ge(placed, j * 5)
                    eng.wait_ge(staged, j * 2 + 2)
                    for k in range(K4):
                        mm = eng.transpose(turned[:, k, :], stage[:, k, :], net.ident[:, :])
                    mm.then_inc(turned_s, 1)


def edges_weighted(net, ex, v_rows, acc, acc_z):
    nc, dram = net.nc, net.dram
    n = net.scope("l4_")
    with n:
        v = n.sb("v", [P, R, K4, D])
        hot = n.sb("hot", [P, R, K4, P])
        e = n.sb("e", [P, R, K4, H])
        sums = [n.ps(f"sums{b}", [P, P]) for b in range(R)]
        zs = [n.ps(f"zs{b}", [H, P]) for b in range(R)]
        v_in, hot_in, ready, summed, sums_free = (n.sems(x, R) for x in ("v_in", "hot_in", "ready", "summed", "sums_free"))
        marks = n.sem("marks")
        with nc.Block() as block:
            @block.sync
            def _(eng):
                for i in turns(eng, NI):
                    for b in range(R):
                        eng.wait_ge(summed[b], i)
                        mark(eng, marks)
                        eng.dma_start(v[:, b], v_rows[bass.ds((i * R + b) * UNIT, UNIT), :].rearrange(
                            "(p k) d -> p k d", k=K4)).then_inc(v_in[b], 16)

            @block.vector
            def _(eng):
                for i in turns(eng, NI):
                    for b in range(R):
                        u = i * R + b
                        eng.wait_ge(summed[b], i)
                        build_hot(net, eng, hot, i, b).then_inc(hot_in[b], 1)
                        eng.tensor_copy(e[:, b], ex[:, bass.ds(u * K4, K4), :]).then_inc(hot_in[b], 1)
                        eng.wait_ge(v_in[b], i * 16 + 16)
                        eng.tensor_tensor(v[:, b].rearrange("p k (h c) -> p k h c", h=H),
                                          v[:, b].rearrange("p k (h c) -> p k h c", h=H),
                                          bc(ex[:, bass.ds(u * K4, K4), :].unsqueeze(3), [P, K4, H, DH]), ALU.mult).then_inc(ready[b], 1)
                    for b in range(R):
                        eng.wait_ge(summed[b], i + 1)
                        add_window(net, eng, i, b, [(acc, sums[b][:, :]), (acc_z, zs[b][:, :])], sums_free)

            @block.tensor
            def _(eng):
                for i in turns(eng, NI):
                    for b in range(R):
                        eng.wait_ge(hot_in[b], i * 2 + 2)
                        eng.wait_ge(sums_free[b], i * 2)
                        mark(eng, marks)
                        for k in range(K4):
                            eng.matmul(zs[b][:, :], e[:, b, k, :], hot[:, b, k, :], start=(k == 0), stop=(k == K4 - 1))
                        eng.wait_ge(ready[b], i + 1)
                        for k in range(K4):
                            mm = eng.matmul(sums[b][:, :], v[:, b, k, :], hot[:, b, k, :], start=(k == 0), stop=(k == K4 - 1))
                        mm.then_inc(summed[b], 1)


def nodes_relational(net, acc, acc_z, x_row, out):
    nc, dram = net.nc, net.dram
    n = net.scope("n3_")
    A = 3 + 2 + LN_STEPS + 2
    B = 1 + 2 + LN_STEPS + 2 + 1
    PER = A + B + LN_STEPS
    with n:
        wo, wf1, wf2 = n.sb("wo", [D, D]), n.sb("wf1", [D, 4, P]), n.sb("wf2", [P, 4, D])
        rows = n.sb("rows", [P, 6, D])
        bf1 = n.sb("bf1", [P, 4])
        z = n.sb("z", [H, GC])
        agg, x4t, h = n.sb("agg", [P, GC]), n.sb("x4t", [P, GC]), n.sb("h", [P, 4, GC])
        y, x4 = n.sb("y", [P, 4, D]), n.sb("x4", [P, 4, D])
        stats, moments, std = n.sb("stats", [P, 4, 6]), n.sb("moments", [P, 4, 2]), n.sb("std", [P, 4])
        pz, po, pt = n.ps("pz", [P, GC]), n.ps("po", [P, 4, D]), n.ps("pt", [P, GC])
        pf = [n.ps(f"pf{f}", [P, GC]) for f in range(4)]
        loaded, dve, spread, made, turned, hid, gelu, fed, rooted, marks, stored = (n.sem(s) for s in (
            "loaded", "dve", "spread", "made", "turned", "hid", "gelu", "fed", "rooted", "marks", "stored"))
        NL = 6 + 3 + 4
        row = lambda c: bc(rows[:, c, :].unsqueeze(1), [P, 4, D])
        with nc.Block() as block:
            @block.sync
            def _(eng):
                eng.dma_start(wo[:, :], dram["L3_gnn_Wo"]).then_inc(loaded, 16)
                eng.dma_start(wf1[:, :, :], dram["L3_gnn_Wf1"].rearrange("d (f o) -> d f o", f=4)).then_inc(loaded, 16)
                eng.dma_start(wf2[:, :, :], dram["L3_gnn_Wf2"].rearrange("(f o) d -> o f d", f=4)).then_inc(loaded, 16)
                for f in range(4):
                    eng.dma_start(bf1[:, f:f + 1], cols(dram["L3_gnn_bf1"][f * P:(f + 1) * P])).then_inc(loaded, 16)
                for c, name in enumerate(("bo", "g1", "be1", "g2", "be2", "bf2")):
                    eng.dma_start(rows[:, c, :], everywhere(dram["L3_gnn_" + name], D)).then_inc(loaded, 16)
                eng.wait_ge(dve, NG * PER)
                full = N // P
                eng.dma_start(out[0:full * P, :].rearrange("(t p) d -> p t d", p=P), x_row[:, 0:full, :]).then_inc(stored, 16)
                eng.dma_start(out[full * P:N, :], x_row[0:N - full * P, full, :]).then_inc(stored, 16)
                eng.wait_ge(stored, 32)

            @block.vector
            def _(eng):
                eng.wait_ge(loaded, 16 * NL)
                for g in turns(eng, NG):
                    steps = Steps(eng, dve, g, PER)
                    mine = x_row[:, bass.ds(g * 4, 4), :]
                    steps.done(eng.tensor_scalar(z[:, :], acc_z[:, bass.ds(g * GC, GC)], 1e-30, None, ALU.max))
                    steps.settle()
                    steps.done(eng.reciprocal(z[:, :], z[:, :]))
                    eng.wait_ge(spread, g + 1)
                    steps.done(eng.tensor_tensor(agg[:, :], acc[:, bass.ds(g * GC, GC)], pz[:, :], ALU.mult))
                    eng.wait_ge(made, g + 1)
                    steps.done(eng.tensor_tensor(y[:, :, :], po[:, :, :], row(0), ALU.add))
                    steps.settle()
                    steps.done(eng.tensor_tensor(y[:, :, :], y[:, :, :], mine, ALU.add))
                    steps.settle()
                    layer_norm(eng, steps, y, stats, moments, std, x4, marks, rooted, g * 3 + 1, 1e-5)
                    steps.done(eng.tensor_tensor(x4[:, :, :], x4[:, :, :], row(1), ALU.mult))
                    steps.settle()
                    steps.done(eng.tensor_tensor(x4[:, :, :], x4[:, :, :], row(2), ALU.add))
                    steps.settle()
                    eng.wait_ge(turned, g + 1)
                    steps.done(eng.tensor_copy(x4t[:, :], pt[:, :]))
                    eng.wait_ge(fed, g + 1)
                    steps.done(eng.tensor_tensor(y[:, :, :], po[:, :, :], row(5), ALU.add))
                    steps.settle()
                    steps.done(eng.tensor_tensor(y[:, :, :], y[:, :, :], x4[:, :, :], ALU.add))
                    steps.settle()
                    layer_norm(eng, steps, y, stats, moments, std, x4, marks, rooted, g * 3 + 2, 1e-5)
                    steps.done(eng.tensor_tensor(x4[:, :, :], x4[:, :, :], row(3), ALU.mult))
                    steps.settle()
                    steps.done(eng.tensor_tensor(x4[:, :, :], x4[:, :, :], row(4), ALU.add))
                    steps.settle()
                    steps.done(eng.tensor_tensor(y[:, :, :], x4[:, :, :], mine, ALU.add))
                    steps.settle()
                    layer_norm(eng, steps, y, stats, moments, std, mine, marks, rooted, g * 3 + 3, 1e-5)
                    steps.end()

            @block.scalar
            def _(eng):
                for g in turns(eng, NG):
                    eng.wait_ge(dve, g * PER + 5 + 9)
                    eng.activation(std[:, :], std[:, :], ACT.Sqrt).then_inc(rooted, 1)
                    for f in range(4):
                        eng.wait_ge(hid, g * 4 + f + 1)
                        eng.activation(h[:, f, :], pf[f][:, :], ACT.Gelu, bias=bf1[:, f:f + 1]).then_inc(gelu, 1)
                    eng.wait_ge(dve, g * PER + A + 3 + 9)
                    eng.activation(std[:, :], std[:, :], ACT.Sqrt).then_inc(rooted, 1)
                    eng.wait_ge(dve, g * PER + A + B + 9)
                    eng.activation(std[:, :], std[:, :], ACT.Sqrt).then_inc(rooted, 1)

            @block.tensor
            def _(eng):
                eng.wait_ge(loaded, 16 * NL)
                for g in turns(eng, NG):
                    eng.wait_ge(dve, g * PER + 2)
                    eng.matmul(pz[:, :], net.expand[:, :], z[:, :], start=True, stop=True).then_inc(spread, 1)
                    eng.wait_ge(dve, g * PER + 3)
                    for j in range(4):
                        mm = eng.matmul(po[:, j, :], agg[:, j * P:(j + 1) * P], wo[:, :], start=True, stop=True)
                    mm.then_inc(made, 1)
                    eng.wait_ge(dve, g * PER + A)
                    for j in range(4):
                        mm = eng.transpose(pt[:, j * P:(j + 1) * P], x4[:, j, :], net.ident[:, :])
                    mm.then_inc(turned, 1)
                    eng.wait_ge(dve, g * PER + A + 1)
                    for f in range(4):
                        eng.matmul(pf[f][:, :], wf1[:, f, :], x4t[:, :], start=True, stop=True).then_inc(hid, 1)
                    eng.wait_ge(gelu, g * 4 + 4)
                    for j in range(4):
                        for f in range(4):
                            mm = eng.matmul(po[:, j, :], h[:, f, j * P:(j + 1) * P], wf2[:, f, :], start=(f == 0), stop=(f == 3))
                    mm.then_inc(fed, 1)


def load_rows(net, x_row):
    n = net.scope("ld_")
    with n:
        loaded = n.sem("loaded")
        with net.nc.Block() as block:
            @block.sync
            def _(eng):
                eng.dma_start(x_row[:, :, :], net.dram["x"].rearrange("(t p) d -> p t d", p=P)).then_inc(loaded, 16)
                eng.wait_ge(loaded, 16)


def graph_network(nc, dram, out):
    net = Net(nc, ExitStack(), dram)
    with net:
        setup(net)
        x_row = net.sb("x_row", [P, NT, D])
        load_rows(net, x_row)
        hs, x1 = net.table("hs", (NP, D)), net.table("x1", (NP, D))
        tabs = [net.table(f"tab{k}", (TR, D)) for k in range(K4)]
        kv, q = net.table("kv", (NP, 2 * D)), net.table("q", (NP, D))
        kvm, qm = net.table("kvm", (NP, 3 * D)), net.table("qm", (NP, 2 * D))
        v_rows = net.table("v_rows", (EP, D))
        clear_tables(net, tabs)

        layer = net.scope("a_")
        with layer:
            acc, hs_row = layer.sb("acc", [P, NP]), layer.sb("hs_row", [P, NT, D])
            clear(net, "c0_", [acc])
            project(net, "p0_", ["L0_gnn_W"], [(hs, 0, D, 0)], x_row, scale=net.dinv, keep=hs_row)
            edges_gcn(net, hs, acc)
            nodes_gcn(net, acc, hs_row, x_row, x1)

        layer = net.scope("b_")
        with layer:
            acc = layer.sb("acc", [P, NP])
            clear(net, "c1_", [acc])
            edges_gated(net, x1, acc, tabs)
            nodes_gated(net, acc, tabs, x_row)

        layer = net.scope("c_")
        with layer:
            acc, acc_z, x_T = layer.sb("acc", [P, NP]), layer.sb("acc_z", [H, NP]), layer.sb("x_T", [P, NP])
            clear(net, "c2_", [acc, acc_z])
            project(net, "p2_", ["L2_gnn_Wk", "L2_gnn_Wv", "L2_gnn_Wq"], [(kv, 0, 2 * D, 0), (q, 2 * D, D, 0)], x_row, x_T=x_T)
            edges_attention(net, kv, q, acc, acc_z)
            nodes_attention(net, acc, acc_z, x_row, x_T)

        project(net, "p3_", ["L3_gnn_Wk", "L3_gnn_Wv", "L3_gnn_Wq"], [(kvm, 0, 2 * D, 0), (qm, 2 * D, D, 0)], x_row)
        hyperbolic(net, x_row, kvm, qm)
        layer = net.scope("d_")
        with layer:
            dot, dist2 = layer.sb("dot", [P, NU * K4, H]), layer.sb("dist2", [P, NU * K4])
            first = net.scope("e_")
            with first:
                dec = first.sb("dec", [P, NU * K4, H])
                edges_relational(net, kvm, qm, dot, dec, dist2, v_rows)
                logits(net, dot, dec, dist2)
            segment_softmax(net, dot)
            acc, acc_z = layer.sb("acc", [P, NP]), layer.sb("acc_z", [H, NP])
            clear(net, "c3_", [acc, acc_z])
            edges_weighted(net, dot, v_rows, acc, acc_z)
            nodes_relational(net, acc, acc_z, x_row, out)


def kernel(**inputs):
    import concourse.bacc as bacc
    from concourse.bass_utils import run_bass_kernel_spmd

    a = {k: np.asarray(v) for k, v in inputs.items()}
    tail = EP - E
    tiled = lambda v: np.ascontiguousarray(v.reshape(NU, P, K4).transpose(1, 0, 2).reshape(P, NU * K4))
    by_tile = lambda v: np.ascontiguousarray(v.reshape(NU, P, K4, -1).transpose(3, 0, 2, 1).reshape(-1, EP))
    src = np.pad(a["src"], (0, tail), constant_values=N)
    dst = np.pad(a["dst"], (0, tail), constant_values=N)
    pair = np.stack([src.reshape(NU, P, K4), dst.reshape(NU, P, K4)], axis=2)
    te = by_tile(np.pad(a["edge_attr_32"], ((0, tail), (0, 0))))
    weight = by_tile(np.pad(a["edge_weight"], (0, tail)))
    arrays = {
        "x": np.pad(a["x"], ((0, NP - N), (0, 0))),
        "src_row": src, "dst_row": dst, "src_tiles": tiled(src), "dst_tiles": tiled(dst),
        "idx": np.ascontiguousarray(pair.transpose(1, 0, 2, 3).reshape(P, NU * 8)),
        "type_row": by_tile(np.pad(a["edge_type_2"], (0, tail)))[0],
        "ea": np.pad(a["edge_attr_128"], ((0, tail), (0, 0))),
        "te": np.concatenate([te, weight, np.ones((1, EP), np.float32)]),
        "one": np.ones((1,), np.float32),
    }
    for name, shape in WEIGHTS.items():
        arrays[name] = a[name].reshape(shape)
    nc = bacc.Bacc("TRN2", target_bir_lowering=False, num_devices=1)
    dram = {k: nc.dram_tensor(f"in_{k}", v.shape, mybir.dt.from_np(v.dtype), kind="ExternalInput").ap() for k, v in arrays.items()}
    out = nc.dram_tensor("out", (N, D), F32, kind="ExternalOutput").ap()
    graph_network(nc, dram, out)
    r = run_bass_kernel_spmd(nc, [{f"in_{k}": v for k, v in arrays.items()}], core_ids=[0])
    return r.results[0]["out"]
```

```python
from contextlib import ExitStack

import numpy as np
import concourse.bass as bass
from concourse import mybir

P = 128
D = 128
N = 6250
E = 106250
H = 8
DH = D // H
K4 = 4
UNIT = P * K4
NU = 208
EP = NU * UNIT
NT = 52
NG = NT // 4
GC = 512
NP = NT * P
TR = NP + P
R = 4
VMAX = (NU * ((N + P - 1) // P) // P + 1) * P
LASTN = N - (NG - 1) * GC
CH = 16
CU = NU // CH
CE = CU * UNIT
TE = 35
TB = 15
HID = 64
BIG = 1e30

ALU = mybir.AluOpType
ACT = mybir.ActivationFunctionType
AX = mybir.AxisListType.X
F32 = mybir.dt.float32
BF16 = mybir.dt.bfloat16
I32 = mybir.dt.int32

WEIGHTS = {
    "L0_gnn_W": (D, D), "L0_gnn_b": (D,),
    "L2_gnn_Wq": (D, D), "L2_gnn_Wk": (D, D), "L2_gnn_Wv": (D, D), "L2_gnn_Wo": (D, D), "L2_gnn_bo": (D,),
    "L2_gnn_W1": (D, 256), "L2_gnn_b1": (256,), "L2_gnn_W2": (256, D), "L2_gnn_b2": (D,),
    "L2_gnn_bn1_g": (D,), "L2_gnn_bn1_b": (D,), "L2_gnn_bn2_g": (D,), "L2_gnn_bn2_b": (D,),
    "L3_gnn_Wq": (D, D), "L3_gnn_Wk": (D, D), "L3_gnn_Wv": (D, D),
    "L3_gnn_rel_q": (2, D), "L3_gnn_rel_k": (2, D), "L3_gnn_rel_v": (2, D),
    "L3_gnn_Wt": (32, D), "L3_gnn_bt": (D,), "L3_gnn_Wd1": (2, HID), "L3_gnn_bd1": (HID,),
    "L3_gnn_Wd2": (HID, H), "L3_gnn_bd2": (H,), "L3_gnn_decay_scale": (H,), "L3_gnn_c_mag": (1,),
    "L3_gnn_hyp_beta": (H,), "L3_gnn_logit_alpha": (H,), "L3_gnn_Wo": (D, D), "L3_gnn_bo": (D,),
    "L3_gnn_g1": (D,), "L3_gnn_be1": (D,), "L3_gnn_g2": (D,), "L3_gnn_be2": (D,),
    "L3_gnn_Wf1": (D, 512), "L3_gnn_bf1": (512,), "L3_gnn_Wf2": (512, D), "L3_gnn_bf2": (D,),
}


class Steps:

    def __init__(self, eng, sem, turn=0, per=0):
        self.eng, self.sem, self.start, self.n, self.per = eng, sem, turn * per, 0, per

    def done(self, ins):
        ins.then_inc(self.sem, 1)
        self.n += 1

    def settle(self):
        self.eng.wait_ge(self.sem, self.start + self.n)

    def end(self):
        assert not self.per or self.n == self.per, (self.n, self.per)


def turns(eng, n):
    yield 0
    with eng.Fori(1, n) as i:
        yield i


def rolling(eng, last):
    yield 0, False
    with eng.Fori(1, last) as i:
        yield i, False
    yield last, True


def later(i, b, k, final):
    return [] if final and b + k >= R else [(i + (b + k) // R, (b + k) % R)]


def bc(ap, shape):
    return ap.broadcast_to(shape)


def cols(vec):
    return vec.rearrange("(p o) -> p o", o=1)


def everywhere(vec, n):
    return bc(vec.rearrange("(o n) -> o n", o=1), [P, n])


class Net:
    def __init__(self, nc, stack, dram):
        self.nc, self.stack, self.dram = nc, stack, dram
        self.phase = ""
        self.lasting = stack
        self.semaphores = []
        self.registers = {}

    def scope(self, name):
        scope = Net(self.nc, ExitStack(), self.dram)
        scope.lasting = self.lasting
        scope.phase = name
        scope.semaphores = []
        return scope

    def sb(self, name, shape, dt=F32):
        return self.stack.enter_context(self.nc.sbuf_tensor(f"{self.phase}{name}", shape, dt))

    def ps(self, name, shape, dt=F32):
        return self.stack.enter_context(self.nc.psum_tensor(f"{self.phase}{name}", shape, dt))

    def sem(self, name):
        self.semaphores.append(self.stack.enter_context(self.nc.semaphore(f"{self.phase}{name}")))
        return self.semaphores[-1]

    def __enter__(self):
        return self

    def __exit__(self, *error):
        if error[0] is None and self.semaphores:
            with self.nc.Block() as block:
                @block.gpsimd
                def _(eng):
                    for s in self.semaphores:
                        eng.sem_clear(s)
        self.stack.close()

    def gather_sems(self, name, n):
        return [self.lasting.enter_context(self.nc.semaphore(f"{self.phase}{name}{i}")) for i in range(n)]

    def sems(self, name, n):
        return [self.sem(f"{name}{i}") for i in range(n)]

    def table(self, name, shape, dt=F32):
        return self.nc.dram_tensor(name, shape, dt, kind="Internal").ap()


def layer_norm(eng, steps, y, stats, moments, std, out, sqrt_in, sqrt_done, sqrt_count, eps):
    for j in range(4):
        steps.done(eng.bn_stats(stats[:, j, :], y[:, j, :]))
    steps.settle()
    mark(eng, sqrt_in)
    for j in range(4):
        steps.done(eng.bn_aggr(moments[:, j, :], stats[:, j, :]))
    steps.settle()
    steps.done(eng.tensor_scalar(std[:, :], moments[:, :, 1], eps, None, ALU.add))
    steps.settle()
    mark(eng, sqrt_in)
    eng.wait_ge(sqrt_done, sqrt_count)
    mark(eng, sqrt_in)
    steps.done(eng.reciprocal(std[:, :], std[:, :]))
    steps.settle()
    for j in range(4):
        steps.done(eng.tensor_scalar(out[:, j, :], y[:, j, :], moments[:, j, 0:1], std[:, j:j + 1],
                                     ALU.subtract, ALU.mult))
    steps.settle()


def split(eng, steps, x, hi, mid, lo):
    steps.done(eng.tensor_copy(hi, x))
    steps.settle()
    steps.done(eng.tensor_tensor(x, x, hi, ALU.subtract))
    steps.settle()
    steps.done(eng.tensor_copy(mid, x))
    steps.settle()
    steps.done(eng.tensor_tensor(x, x, mid, ALU.subtract))
    steps.settle()
    steps.done(eng.tensor_copy(lo, x))


SPLIT_STEPS = 5
LN_STEPS = 4 + 4 + 1 + 1 + 4


def mark(eng, sem):
    eng.sem_inc(sem, 1)


def setup(net):
    nc, dram = net.nc, net.dram
    net.ident = net.sb("ident", [P, P])
    net.ident_b = net.sb("ident_b", [P, P], BF16)
    net.iota = net.sb("iota", [P, P])
    net.lower = net.sb("lower", [P, P])
    net.spare = net.sb("spare", [P, 1])
    net.ones = net.sb("ones", [P, P])
    net.expand = net.sb("expand", [2 * H, P])
    net.dst_f = net.sb("dst_f", [P, NU * K4])
    net.src_f = net.sb("src_f", [P, NU * K4])
    net.type_f = net.sb("type_f", [P, NU * K4])
    net.last_i = net.sb("last_i", [1, 1], I32)
    net.type_scale = net.sb("type_scale", [P, 1])
    net.dinv = net.sb("dinv", [P, NT])
    net.dst_rows = net.table("dst_rows", (EP,))
    net.type_rows = net.table("type_rows", (2, EP))
    net.parts = net.table("parts", (TB, EP), BF16)
    net.visits = net.table("visits", (VMAX * 2,), I32)
    net.visit_base = net.table("visit_base", (VMAX,))
    net.dst_cols = net.table("dst_cols", (P, NU * K4))
    ends = net.table("ends", (2, NU))
    HU = NU // 2

    n = net.scope("s0_")
    with n:
        src_i = n.sb("src_i", [P, NU * K4], I32)
        dst_i = n.sb("dst_i", [P, NU * K4], I32)
        type_i = n.sb("type_i", [P, NU * K4], I32)
        rows_i = n.sb("rows_i", [HU, 2, UNIT], I32)
        rows_f = n.sb("rows_f", [HU, 2, UNIT])
        types_i = n.sb("types_i", [HU, 2, UNIT], I32)
        types_f = n.sb("types_f", [HU, 2, 2, UNIT])
        types_b = n.sb("types_b", [HU, 3, 2, UNIT], BF16)
        weight = n.sb("weight", [HU, 2, UNIT])
        weight_b = n.sb("weight_b", [HU, 3, 2, UNIT], BF16)
        least, most = n.sb("least", [HU, 2]), n.sb("most", [HU, 2])
        top = n.sb("top", [HU, 1])
        row = n.sb("row", [1, 8])
        sel = n.sb("sel", [1, 2, P])
        pm = n.ps("pm", [P, P])
        loaded, pool_built, written = n.sem("loaded"), n.sem("pool_built"), n.sem("written")
        dve, top_turned, scale_spread = n.sem("dve"), n.sem("top_turned"), n.sem("scale_spread")
        with nc.Block() as block:
            @block.sync
            def _(eng):
                eng.dma_start(src_i[:, :], dram["src_tiles"]).then_inc(loaded, 16)
                eng.dma_start(dst_i[:, :], dram["dst_tiles"]).then_inc(loaded, 16)
                eng.dma_start(type_i[:, :], dram["type_tiles"]).then_inc(loaded, 16)
                for to, of in ((rows_i, "dst_row"), (types_i, "type_row"), (weight, "weight_row")):
                    eng.dma_start(to[:, :, :], dram[of].rearrange("(p a e) -> p a e", a=2, e=UNIT)).then_inc(loaded, 16)
                eng.wait_ge(dve, 17)
                for c, ap in enumerate((least, most)):
                    eng.dma_start(ends[c].rearrange("(p a) -> p a", a=2), ap[:, :]).then_inc(written, 16)
                eng.dma_start(net.dst_rows.rearrange("(p a e) -> p a e", a=2, e=UNIT), rows_f[:, :, :]).then_inc(written, 16)
                for c in range(2):
                    eng.dma_start(net.type_rows[c].rearrange("(p a e) -> p a e", a=2, e=UNIT), types_f[:, c, :, :]).then_inc(written, 16)
                rows = [weight_b[:, c, :, :] for c in (0, 0, 0, 1, 1, 2)]
                rows += [types_b[:, c, :, :] for c in (2, 2, 2, 0, 0, 0, 1, 1, 1)]
                for c, ap in enumerate(rows):
                    eng.dma_start(net.parts[c].rearrange("(p a e) -> p a e", a=2, e=UNIT), ap).then_inc(written, 16)
                eng.dma_start(net.dst_cols, net.dst_f[:, :]).then_inc(written, 16)
                eng.wait_ge(written, 16 * (6 + TB))

            @block.gpsimd
            def _(eng):
                eng.memset(net.ident[:, :], 0.0).then_inc(pool_built, 1)
                eng.memset(net.lower[:, :], 1.0).then_inc(pool_built, 1)
                eng.memset(net.expand[:, :], 1.0).then_inc(pool_built, 1)
                eng.memset(net.ones[:, :], 1.0).then_inc(pool_built, 1)
                eng.memset(sel[:, 0, :], 0.0).then_inc(pool_built, 1)
                eng.memset(sel[:, 1, :], 1.0).then_inc(pool_built, 1)
                eng.iota(net.iota[:, :], pattern=[[1, P]], base=0, channel_multiplier=0,
                         allow_small_or_imprecise_dtypes=True).then_inc(pool_built, 1)
                eng.iota(net.spare[:, :], pattern=[[1, 1]], base=NP, channel_multiplier=1,
                         allow_small_or_imprecise_dtypes=True).then_inc(pool_built, 1)
                eng.wait_ge(pool_built, 8)
                eng.affine_select(out=net.ident[:, :], in_=net.ident[:, :], compare_op=ALU.not_equal, fill=1.0,
                                  base=0, pattern=[[-1, P]], channel_multiplier=1).then_inc(pool_built, 1)
                eng.affine_select(out=net.lower[:, :], in_=net.lower[:, :], compare_op=ALU.is_gt, fill=0.0,
                                  base=0, pattern=[[-1, P]], channel_multiplier=1).then_inc(pool_built, 1)
                eng.affine_select(out=net.expand[:, :], in_=net.expand[:, :], compare_op=ALU.is_ge, fill=0.0,
                                  base=0, pattern=[[1, P]], channel_multiplier=-DH).then_inc(pool_built, 1)
                eng.wait_ge(pool_built, 11)
                eng.affine_select(out=net.expand[:, :], in_=net.expand[:, :], compare_op=ALU.is_ge, fill=0.0,
                                  base=DH - 1, pattern=[[-1, P]], channel_multiplier=DH).then_inc(pool_built, 1)
                eng.memset(sel[:, 0, 2:3], 1.0).then_inc(pool_built, 1)
                eng.memset(sel[:, 1, 2:3], 0.0).then_inc(pool_built, 1)

            @block.vector
            def _(eng):
                eng.wait_ge(loaded, 96)
                steps = Steps(eng, dve)
                steps.done(eng.tensor_copy(net.src_f[:, :], src_i[:, :]))
                steps.done(eng.tensor_copy(net.dst_f[:, :], dst_i[:, :]))
                steps.done(eng.tensor_copy(net.type_f[:, :], type_i[:, :]))
                steps.done(eng.tensor_copy(rows_f[:, :, :], rows_i[:, :, :]))
                steps.done(eng.tensor_copy(types_f[:, 0, :, :], types_i[:, :, :]))
                steps.done(eng.memset(types_b[:, 2, :, :], 1.0))
                steps.settle()
                steps.done(eng.tensor_reduce(top[:, :], types_f[:, 0, :, :].rearrange("p a e -> p (a e)"), AX, ALU.max))
                steps.done(eng.tensor_scalar(types_f[:, 1, :, :], types_f[:, 0, :, :], -1.0, 1.0, ALU.mult, ALU.add))
                steps.done(eng.tensor_reduce(least[:, :], rows_f[:, :, :], AX, ALU.min))
                steps.done(eng.tensor_reduce(most[:, :], rows_f[:, :, :], AX, ALU.max))
                steps.settle()
                steps.done(eng.tensor_copy(types_b[:, 0:2, :, :], types_f[:, :, :, :]))
                split(eng, steps, weight[:, :, :], weight_b[:, 0], weight_b[:, 1], weight_b[:, 2])
                steps.done(eng.memset(row[:, 3:4], 0.0))
                steps.settle()
                assert steps.n == 17, steps.n
                eng.wait_ge(top_turned, 1)
                steps.done(eng.tensor_reduce(row[:, 0:1], pm[0:1, 0:HU], AX, ALU.max))
                steps.settle()
                steps.done(eng.tensor_scalar(row[:, 1:2], row[:, 0:1], 1.0, 1.0, ALU.add, ALU.max))
                steps.settle()
                steps.done(eng.reciprocal(row[:, 2:3], row[:, 1:2]))
                eng.wait_ge(scale_spread, 1)
                steps.done(eng.tensor_copy(net.type_scale[:, :], pm[:, 0:1]))
                eng.wait_ge(pool_built, 14)
                steps.done(eng.tensor_copy(net.ident_b[:, :], net.ident[:, :]))

            @block.tensor
            def _(eng):
                eng.wait_ge(pool_built, 14)
                eng.wait_ge(dve, 7)
                eng.transpose(pm[0:1, 0:HU], top[:, :], net.ident[0:HU, 0:HU]).then_inc(top_turned, 1)
                eng.wait_ge(dve, 20)
                eng.matmul(pm[:, 0:1], sel[:, 0, :], row[:, 2:3], start=True, stop=False)
                eng.matmul(pm[:, 0:1], sel[:, 1, :], net.ones[0:1, 0:1], start=False, stop=True).then_inc(scale_spread, 1)

    n = net.scope("s2_")
    with n:
        rows3 = n.sb("rows3", [1, 3, NU])
        end_f, end_i = n.sb("end_f", [1, 2, NU]), n.sb("end_i", [1, NU], I32)
        all3 = n.sb("all3", [P, 3, NU])
        v, ge, got, unit = n.sb("v", [P, 1]), n.sb("ge", [P, NU]), n.sb("got", [P, NU]), n.sb("unit", [P, 1])
        first, base, base0 = n.sb("first", [P, 1]), n.sb("base", [P, 1]), n.sb("base0", [P, 1])
        pair = n.sb("pair", [P, 2], I32)
        count = n.sb("count", [1, 2], I32)
        pb = n.ps("pb", [P, 3, GC])
        loaded, dve, spread, chunk, chunk_ready, written, marks = (n.sem(s) for s in (
            "loaded", "dve", "spread", "chunk", "chunk_ready", "written", "marks"))
        PER = 12
        with nc.Block() as block:
            @block.sync
            def _(eng):
                eng.dma_start(end_f[:, :, :], ends.rearrange("(o c) n -> o c n", o=1)).then_inc(loaded, 16)
                eng.dma_start(base0[:, :], everywhere(ends[0, 0:1], 1)).then_inc(loaded, 16)
                eng.dma_start(net.expand[H:2 * H, :], net.expand[0:H, :]).then_inc(loaded, 16)
                eng.wait_ge(loaded, 48)

            @block.vector
            def _(eng):
                eng.wait_ge(loaded, 48)
                steps = Steps(eng, dve)
                steps.done(eng.tensor_tensor(end_i[:, :], end_f[:, 1, :], end_f[:, 0, :], ALU.subtract))
                steps.settle()
                steps.done(eng.tensor_scalar(end_i[:, :], end_i[:, :], 7, None, ALU.logical_shift_right))
                steps.settle()
                steps.done(eng.tensor_scalar(rows3[:, 0, :], end_i[:, :], 1, None, ALU.add))
                steps.done(eng.memset(rows3[:, 2, :], 4.0 * NP))
                steps.settle()
                steps.done(eng.tensor_tensor(rows3[:, 2, 0:NU - 1], end_f[:, 0, 1:NU], end_f[:, 0, 0:NU - 1], ALU.subtract))
                steps.done(eng.tensor_tensor_scan(rows3[:, 1, :], rows3[:, 0, :], rows3[:, 0, :], 0.0, ALU.add, ALU.max))
                steps.settle()
                steps.done(eng.tensor_scalar(count[:, 0:1], rows3[:, 1, NU - 1:NU], -1.0, None, ALU.add))
                steps.done(eng.tensor_scalar(count[:, 1:2], rows3[:, 1, NU - 1:NU], float(P - 1 + R), None, ALU.add))
                steps.settle()
                steps.done(eng.tensor_scalar(net.last_i[:, :], count[:, 0:1], 2, None, ALU.logical_shift_right))
                steps.done(eng.tensor_scalar(count[:, 1:2], count[:, 1:2], 7, None, ALU.logical_shift_right))
                eng.wait_ge(spread, 1)
                steps.done(eng.tensor_copy(all3[:, :, :], pb[:, :, 0:NU]))
                steps.done(eng.tensor_scalar(v[:, :], net.spare[:, :], float(-NP), None, ALU.add))
                steps.settle()

            @block.tensor
            def _(eng):
                eng.wait_ge(dve, 8)
                for c in range(3):
                    mm = eng.matmul(pb[:, c, 0:NU], net.ones[0:1, :], rows3[:, c, :], start=True, stop=True)
                mm.then_inc(spread, 1)

        with nc.Block() as block:
            @block.sync
            def _(eng):
                rounds = eng.value_load(count[0:1, 1:2], min_val=2, max_val=VMAX // P)
                for c in turns(eng, rounds):
                    eng.wait_ge(chunk_ready, c + 1)
                    mark(eng, marks)
                    eng.dma_start(net.visits[bass.ds(c * (2 * P), 2 * P)].rearrange("(p a) -> p a", a=2), pair[:, :]).then_inc(written, 16)
                    eng.dma_start(net.visit_base[bass.ds(c * P, P)].rearrange("(p a) -> p a", a=1), base[:, :]).then_inc(written, 16)
                eng.wait_ge(written, rounds * 32)
                mark(eng, marks)

            @block.vector
            def _(eng):
                rounds = eng.value_load(count[0:1, 1:2], min_val=2, max_val=VMAX // P)
                for c in turns(eng, rounds):
                    steps = Steps(eng, chunk, c, PER)
                    steps.done(eng.tensor_scalar(ge[:, :], all3[:, 1, :], v[:, 0:1], None, ALU.is_le))
                    steps.settle()
                    steps.done(eng.tensor_reduce(unit[:, :], ge[:, :], AX, ALU.add))
                    steps.done(eng.tensor_tensor(got[:, :], ge[:, :], all3[:, 0, :], ALU.mult))
                    steps.settle()
                    steps.done(eng.tensor_reduce(first[:, :], got[:, :], AX, ALU.add))
                    steps.settle()
                    steps.done(eng.tensor_tensor(got[:, :], ge[:, :], all3[:, 2, :], ALU.mult))
                    steps.done(eng.tensor_tensor(first[:, :], v[:, :], first[:, :], ALU.subtract))
                    steps.settle()
                    eng.wait_ge(written, c * 32)
                    mark(eng, marks)
                    steps.done(eng.tensor_reduce(base[:, :], got[:, :], AX, ALU.add))
                    steps.settle()
                    steps.done(eng.tensor_tensor(base[:, :], base[:, :], base0[:, :], ALU.add))
                    steps.settle()
                    steps.done(eng.scalar_tensor_tensor(out=base[:, :], in0=first[:, :], scalar=float(P), in1=base[:, :],
                                                        op0=ALU.mult, op1=ALU.add))
                    steps.settle()
                    steps.done(eng.tensor_scalar(base[:, :], base[:, :], float(NP - P), None, ALU.min))
                    steps.done(eng.tensor_scalar(pair[:, 0:1], unit[:, :], float(NU - 1), None, ALU.min))
                    steps.settle()
                    eng.tensor_copy(pair[:, 1:2], base[:, :]).then_inc(chunk_ready, 1)
                    steps.done(eng.tensor_scalar(v[:, :], v[:, :], float(P), None, ALU.add))
                    steps.settle()
                    mark(eng, marks)
                    steps.end()

    n = net.scope("s1_")
    with n:
        dst_i = n.sb("dst_i", [P, NU * K4], I32)
        hi_i = n.sb("hi_i", [P, NU * K4], I32)
        lo_i = n.sb("lo_i", [P, NU * K4], I32)
        hi = n.sb("hi", [P, NU * K4])
        lo = n.sb("lo", [P, NU * K4])
        hot_lo = n.sb("hot_lo", [P, R, K4, P], BF16)
        hot_hi = n.sb("hot_hi", [P, R, K4, NT], BF16)
        deg = n.sb("deg", [P, NT])
        counts = n.ps("counts", [P, NT])
        loaded, dve = n.sem("loaded"), n.sem("dve")
        hot, used = n.sems("hot", R), n.sems("used", R)
        counted, rooted, zeroed = n.sem("counted"), n.sem("rooted"), n.sem("zeroed")
        zero = n.sb("zero", [P, P], BF16)
        with nc.Block() as block:
            @block.sync
            def _(eng):
                eng.dma_start(dst_i[:, :], dram["dst_tiles"]).then_inc(loaded, 16)

            @block.gpsimd
            def _(eng):
                eng.memset(zero[:, :], 0.0).then_inc(zeroed, 1)

            @block.vector
            def _(eng):
                eng.wait_ge(loaded, 16)
                steps = Steps(eng, dve)
                steps.done(eng.tensor_scalar(hi_i[:, :], dst_i[:, :], 7, None, ALU.logical_shift_right))
                steps.done(eng.tensor_scalar(lo_i[:, :], dst_i[:, :], P - 1, None, ALU.bitwise_and))
                steps.settle()
                steps.done(eng.tensor_copy(hi[:, :], hi_i[:, :]))
                steps.done(eng.tensor_copy(lo[:, :], lo_i[:, :]))
                steps.settle()
                for i in turns(eng, NU // R):
                    for b in range(R):
                        u = i * R + b
                        eng.wait_ge(used[b], i)
                        eng.tensor_tensor(hot_lo[:, b], bc(net.iota[:, :].unsqueeze(1), [P, K4, P]),
                                          bc(lo[:, bass.ds(u * K4, K4)].unsqueeze(2), [P, K4, P]), ALU.is_equal).then_inc(hot[b], 1)
                        eng.tensor_tensor(hot_hi[:, b], bc(net.iota[:, 0:NT].unsqueeze(1), [P, K4, NT]),
                                          bc(hi[:, bass.ds(u * K4, K4)].unsqueeze(2), [P, K4, NT]), ALU.is_equal).then_inc(hot[b], 1)
                eng.wait_ge(counted, 1)
                steps.done(eng.tensor_scalar(deg[:, :], counts[:, :], 1.0, None, ALU.add))
                eng.wait_ge(rooted, 1)
                steps.done(eng.reciprocal(net.dinv[:, :], deg[:, :]))

            @block.scalar
            def _(eng):
                eng.wait_ge(dve, 5)
                eng.activation(deg[:, :], deg[:, :], ACT.Sqrt).then_inc(rooted, 1)

            @block.tensor
            def _(eng):
                eng.wait_ge(zeroed, 1)
                eng.matmul(counts[:, :], zero[:, :], zero[:, 0:NT], start=True, stop=False, skip_group_check=True)
                for i in turns(eng, NU // R):
                    for b in range(R):
                        eng.wait_ge(hot[b], i * 2 + 2)
                        for k in range(K4):
                            mm = eng.matmul(counts[:, :], hot_lo[:, b, k, :], hot_hi[:, b, k, :], start=False,
                                            stop=False, skip_group_check=True)
                        mm.then_inc(used[b], 1)
                eng.matmul(counts[:, :], zero[:, :], zero[:, 0:NT], start=False, stop=True, skip_group_check=True).then_inc(counted, 1)


def rows_of(table, lo, n=GC):
    return table[bass.ds(lo, n), :].rearrange("(t p) d -> p t d", p=P)


def part_rows(table, g, width):
    return table[bass.ds(g * GC, GC), :].rearrange("(t p) (c d) -> p t c d", p=P, d=width)


def project(net, name, weights, outs, x_row, x_T=None, scale=None, keep=None, parts=None):
    nc, dram = net.nc, net.dram
    n = net.scope(name)
    with n:
        F = D * len(weights)
        w = n.sb("w", [D, len(weights), D])
        xt = n.sb("xt", [P, GC])
        prod = n.sb("prod", [P, 4, F])
        three = n.sb("three", [P, 4, 3, D], BF16)
        NS = len(outs) + (3 if parts is not None else 0)
        splits = n.sem("splits")
        turned = n.ps("turned", [P, GC])
        pp = [n.ps(f"pp{j}", [P, F]) for j in range(4)]
        loaded, turned_s, copied, made, kept, stored = (n.sem(s) for s in (
            "loaded", "turned_s", "copied", "made", "kept", "stored"))
        moved = n.sem("moved")
        with nc.Block() as block:
            @block.sync
            def _(eng):
                for c, name_ in enumerate(weights):
                    eng.dma_start(w[:, c, :], dram[name_]).then_inc(loaded, 16)
                for g in turns(eng, NG):
                    eng.wait_ge(kept, g + 1)
                    mark(eng, moved)
                    for table, at, width, to in outs:
                        eng.dma_start(rows_of(table, g * GC)[:, :, to:to + width],
                                      prod[:, :, at:at + width]).then_inc(stored, 16)
                    if parts is not None:
                        eng.wait_ge(splits, g * SPLIT_STEPS + SPLIT_STEPS)
                        mark(eng, moved)
                        for c in range(3):
                            eng.dma_start(part_rows(parts, g, parts.shape[1] // 3)[:, :, c, 0:D], three[:, :, c, :]).then_inc(stored, 16)
                eng.wait_ge(stored, 16 * NS * NG)

            @block.tensor
            def _(eng):
                eng.wait_ge(loaded, 16 * len(weights))
                for g in turns(eng, NG):
                    eng.wait_ge(copied, g * 2 + 1)
                    for j in range(4):
                        mm = eng.transpose(turned[:, j * P:(j + 1) * P], prod[:, j, 0:D], net.ident[:, :])
                    mm.then_inc(turned_s, 1)
                    eng.wait_ge(copied, g * 2 + 2)
                    for j in range(4):
                        mm = eng.matmul(pp[j][:, :], xt[:, j * P:(j + 1) * P], w[:, :, :].rearrange("p c d -> p (c d)"),
                                        start=True, stop=True)
                    mm.then_inc(made, 1)

            @block.vector
            def _(eng):
                for g in turns(eng, NG):
                    eng.wait_ge(stored, g * (16 * NS))
                    mark(eng, moved)
                    eng.tensor_copy(prod[:, :, 0:D], x_row[:, bass.ds(g * 4, 4), :]).then_inc(copied, 1)
                    eng.wait_ge(turned_s, g + 1)
                    eng.tensor_copy(xt[:, :], turned[:, :]).then_inc(copied, 1)
                    if x_T is not None:
                        eng.tensor_copy(x_T[:, bass.ds(g * GC, GC)], turned[:, :])
                    eng.wait_ge(made, g + 1)
                    mark(eng, moved)
                    for j in range(4):
                        if scale is None:
                            cp = eng.tensor_copy(prod[:, j, :], pp[j][:, :])
                        else:
                            cp = eng.tensor_scalar(prod[:, j, :], pp[j][:, :], scale[:, bass.ds(g * 4 + j, 1)], None, ALU.mult)
                            cp = eng.tensor_scalar(keep[:, bass.ds(g * 4 + j, 1), :].rearrange("p a d -> p (a d)"),
                                                   pp[j][:, :], scale[:, bass.ds(g * 4 + j, 1)], None, ALU.mult)
                    cp.then_inc(kept, 1)
                    if parts is not None:
                        eng.wait_ge(kept, g + 1)
                        steps = Steps(eng, splits, g, SPLIT_STEPS)
                        split(eng, steps, prod[:, :, F - D:F], *(three[:, :, c, :] for c in range(3)))


def gather(eng, out, table, idx):
    return eng.indirect_dma_start(out=out, out_offset=None, in_=table,
                                  in_offset=bass.IndirectOffsetOnAxis(ap=idx, axis=0))


def visit_registers(net, eng):
    if eng.engine not in net.registers:
        net.registers[eng.engine] = [eng.alloc_register(f"visit{k}") for k in range(2 * R)]
    return net.registers[eng.engine]


def look_up(net, eng, regs, i):
    eng.load(regs, net.visits[bass.ds(i * (2 * R), 2 * R)].rearrange("(o a) -> o a", o=1))
    return [(eng.snap(regs[2 * b], min_val=0, max_val=NU - 1), eng.snap(regs[2 * b + 1], min_val=0, max_val=NP - P))
            for b in range(R)]


def last_turn(net, eng):
    return eng.value_load(net.last_i[0:1, 0:1], min_val=NU // R - 1, max_val=VMAX // R - 1)


def turn_count(net, eng):
    return last_turn(net, eng) + 1


def small_loads(net, eng, i, b, unit, idx, idx_in, got, base, base_in, base_used):
    eng.wait_ge(got[b], i * 64)
    eng.dma_start(idx[:, b, :], net.dram["src_tiles"][:, bass.ds(unit * K4, K4)]).then_inc(idx_in[b], 16)
    eng.wait_ge(base_used[b], i)
    mark(eng, net.marks)
    eng.dma_start(base[:, b:b + 1], bc(net.visit_base[bass.ds(i * R + b, 1)].rearrange("(o a) -> o a", o=1), [P, 1])).then_inc(base_in[b], 16)


def visit_loads(net, eng, i, b, unit, dst, base, base_in, base_used):
    eng.wait_ge(base_used[b], i)
    mark(eng, net.marks)
    eng.dma_start(dst[:, b, :], net.dst_cols[:, bass.ds(unit * K4, K4)]).then_inc(base_in[b], 16)
    eng.dma_start(base[:, b:b + 1], bc(net.visit_base[bass.ds(i * R + b, 1)].rearrange("(o a) -> o a", o=1), [P, 1])).then_inc(base_in[b], 16)


def source_loads(net, eng, i, b, unit, idx, idx_in, got):
    eng.wait_ge(got[b], i * 64)
    eng.dma_start(idx[:, b, :], net.dram["src_tiles"][:, bass.ds(unit * K4, K4)]).then_inc(idx_in[b], 16)


def hot_here(net, eng, hot, dst, base, b):
    return eng.scalar_tensor_tensor(out=hot[:, b], in0=bc(net.iota[:, :].unsqueeze(1), [P, K4, P]), scalar=base[:, b:b + 1],
                                    in1=bc(dst[:, b, :].unsqueeze(2), [P, K4, P]), op0=ALU.add, op1=ALU.is_equal)


def gather_unit(eng, marks, i, b, rows, table, idx, idx_in, got):
    eng.wait_ge(idx_in[b], i * 16 + 16)
    mark(eng, marks)
    for k in range(K4):
        gather(eng, rows[:, b, k, :], table, idx[:, b, k:k + 1]).then_inc(got[b], 16)


def build_hot(net, eng, hot, base, b, unit):
    return eng.scalar_tensor_tensor(out=hot[:, b], in0=bc(net.iota[:, :].unsqueeze(1), [P, K4, P]), scalar=base[:, b:b + 1],
                                    in1=bc(net.dst_f[:, bass.ds(unit * K4, K4)].unsqueeze(2), [P, K4, P]),
                                    op0=ALU.add, op1=ALU.is_equal)


def turn_hot(eng, i, b, hot, hot_in, ident, turned, turned_in, pt_in):
    eng.wait_ge(hot_in[b], i + 1)
    if b >= len(turned):
        eng.wait_ge(pt_in[b - len(turned)], i + 1)
    else:
        eng.wait_ge(pt_in[b + R - len(turned)], i)
    h = b % len(turned)
    for k in range(K4):
        mm = eng.transpose(turned[h][:, k, :], hot[:, b, k, :], ident)
    mm.then_inc(turned_in[b], 1)


def copy_turned(eng, marks, i, b, turned, turned_in, pt, pt_in, q_in):
    eng.wait_ge(q_in[b], i)
    eng.wait_ge(turned_in[b], i + 1)
    mark(eng, marks)
    eng.activation(pt[:, b], turned[b % len(turned)][:, :, :], ACT.Copy).then_inc(pt_in[b], 1)


def add_window(net, eng, i, b, base, adds, sums_free):
    if b:
        eng.wait_ge(sums_free[b - 1], i * len(adds) + len(adds))
    else:
        eng.wait_ge(sums_free[R - 1], i * len(adds))
    mark(eng, net.marks)
    for acc, sums in adds:
        at = acc[:, bass.ds(base, P)]
        eng.tensor_tensor(at, at, sums, ALU.add).then_inc(sums_free[b], 1)


def clear(net, name, acc):
    n = net.scope(name)
    with n, net.nc.Block() as block:
        @block.gpsimd
        def _(eng):
            for a in acc:
                eng.memset(a[:, :], 0.0)


def edges_gcn(net, hs, acc):
    nc = net.nc
    n = net.scope("l0_")
    with n:
        idx = n.sb("idx", [P, R, K4], I32)
        base = n.sb("base", [P, R])
        msg = n.sb("msg", [P, R, K4, D])
        hot = n.sb("hot", [P, R, K4, P])
        sums = [n.ps(f"sums{b}", [P, P]) for b in range(R)]
        idx_in, base_in, hot_in, summed, sums_free = (n.sems(s, R) for s in ("idx_in", "base_in", "hot_in", "summed", "sums_free"))
        got = n.gather_sems("got", R)
        with nc.Block() as block:
            @block.sync
            def _(eng):
                regs = visit_registers(net, eng)
                for i in turns(eng, turn_count(net, eng)):
                    visit = look_up(net, eng, regs, i)
                    for b in range(R):
                        small_loads(net, eng, i, b, visit[b][0], idx, idx_in, got, base, base_in, hot_in)

            @block.gpsimd
            def _(eng):
                for i in turns(eng, turn_count(net, eng)):
                    for b in range(R):
                        eng.wait_ge(summed[b], i)
                        gather_unit(eng, net.marks, i, b, msg, hs, idx, idx_in, got)

            @block.vector
            def _(eng):
                regs = visit_registers(net, eng)
                for i in turns(eng, turn_count(net, eng)):
                    visit = look_up(net, eng, regs, i)
                    for b in range(R):
                        eng.wait_ge(base_in[b], i * 16 + 16)
                        eng.wait_ge(summed[b], i)
                        build_hot(net, eng, hot, base, b, visit[b][0]).then_inc(hot_in[b], 1)
                    for b in range(R):
                        eng.wait_ge(summed[b], i + 1)
                        add_window(net, eng, i, b, visit[b][1], [(acc, sums[b][:, :])], sums_free)

            @block.tensor
            def _(eng):
                for i in turns(eng, turn_count(net, eng)):
                    for b in range(R):
                        eng.wait_ge(hot_in[b], i + 1)
                        eng.wait_ge(sums_free[b], i)
                        eng.wait_ge(got[b], i * 64 + 64)
                        for k in range(K4):
                            mm = eng.matmul(sums[b][:, :], msg[:, b, k, :], hot[:, b, k, :], start=(k == 0), stop=(k == K4 - 1))
                        mm.then_inc(summed[b], 1)


def nodes_gcn(net, acc, hs_row, x_row, table, parts):
    nc, dram = net.nc, net.dram
    n = net.scope("n0_")
    PER = 1 + 1 + 4 + 1 + 1 + LN_STEPS + 1 + SPLIT_STEPS
    with n:
        bias = n.sb("bias", [P, D])
        st = n.sb("st", [P, GC])
        y = n.sb("y", [P, 4, D])
        z = n.sb("z", [P, 4, D])
        three = n.sb("three", [P, 4, 3, D], BF16)
        stats, moments, std = n.sb("stats", [P, 4, 6]), n.sb("moments", [P, 4, 2]), n.sb("std", [P, 4])
        turned = n.ps("turned", [P, GC])
        loaded, dve, turned_s, rooted, stored, marks = (n.sem(s) for s in ("loaded", "dve", "turned_s", "rooted", "stored", "marks"))
        with nc.Block() as block:
            @block.sync
            def _(eng):
                eng.dma_start(bias[:, :], everywhere(dram["L0_gnn_b"], D)).then_inc(loaded, 16)
                for g in turns(eng, NG):
                    eng.wait_ge(dve, g * PER + PER)
                    mark(eng, marks)
                    eng.dma_start(rows_of(table, g * GC), x_row[:, bass.ds(g * 4, 4), :]).then_inc(stored, 16)
                    eng.dma_start(part_rows(parts, g, D), three[:, :, :, :]).then_inc(stored, 16)
                eng.wait_ge(stored, 32 * NG)

            @block.tensor
            def _(eng):
                for g in turns(eng, NG):
                    eng.wait_ge(dve, g * PER + 1)
                    for j in range(4):
                        mm = eng.transpose(turned[:, j * P:(j + 1) * P], st[:, j * P:(j + 1) * P], net.ident[:, :])
                    mm.then_inc(turned_s, 1)

            @block.scalar
            def _(eng):
                for g in turns(eng, NG):
                    eng.wait_ge(dve, g * PER + 8 + 9)
                    eng.activation(std[:, :], std[:, :], ACT.Sqrt).then_inc(rooted, 1)

            @block.vector
            def _(eng):
                eng.wait_ge(loaded, 16)
                for g in turns(eng, NG):
                    steps = Steps(eng, dve, g, PER)
                    steps.done(eng.tensor_copy(st[:, :], acc[:, bass.ds(g * GC, GC)]))
                    eng.wait_ge(turned_s, g + 1)
                    steps.done(eng.tensor_tensor(y[:, :, :], turned[:, :].rearrange("p (t d) -> p t d", d=D),
                                                 hs_row[:, bass.ds(g * 4, 4), :], ALU.add))
                    steps.settle()
                    for j in range(4):
                        steps.done(eng.scalar_tensor_tensor(out=z[:, j, :], in0=y[:, j, :], scalar=net.dinv[:, bass.ds(g * 4 + j, 1)],
                                                            in1=bias[:, :], op0=ALU.mult, op1=ALU.add))
                    steps.settle()
                    steps.done(eng.tensor_scalar(y[:, :, :], z[:, :, :], 0.0, None, ALU.max))
                    steps.settle()
                    steps.done(eng.tensor_tensor(z[:, :, :], y[:, :, :], x_row[:, bass.ds(g * 4, 4), :], ALU.add))
                    steps.settle()
                    layer_norm(eng, steps, z, stats, moments, std, x_row[:, bass.ds(g * 4, 4), :], marks, rooted, g + 1, 1e-5)
                    mark(eng, marks)
                    steps.done(eng.tensor_copy(y[:, :, :], x_row[:, bass.ds(g * 4, 4), :]))
                    eng.wait_ge(stored, g * 32)
                    steps.settle()
                    mark(eng, marks)
                    split(eng, steps, y[:, :, :], *(three[:, :, c, :] for c in range(3)))
                    steps.end()


def edges_gated(net, x1, x1_parts, acc, tabs):
    nc, dram = net.nc, net.dram
    n = net.scope("l1_")
    IDX = 6
    with n:
        idx = n.sb("idx", [P, R, K4], I32)
        base = n.sb("base", [P, R])
        src_all = n.sb("src_all", [P, R, UNIT], I32)
        xs, xd, ea = (n.sb(s, [P, R, K4, D]) for s in ("xs", "xd", "ea"))
        hot = n.sb("hot", [P, R, K4, P])
        pt = n.sb("pt", [P, R, K4, P], BF16)
        slab = n.sb("slab", [P, R, 3, D], BF16)
        same = n.sb("same", [P, R, K4, P])
        before = n.sb("before", [P, K4, P])
        again = n.sb("again", [P, K4])
        off = n.sb("off", [P, K4])
        to_i = n.sb("to_i", [P, R, K4], I32)
        total = n.sb("total", [P, R, K4, D])
        turned = [n.ps(f"turned{b}", [P, K4, P]) for b in range(2)]
        q = [n.ps(f"q{b}", [P, K4, D]) for b in range(2)]
        pres = [n.ps(f"pres{b}", [P, K4, D]) for b in range(2)]
        sums = [n.ps(f"sums{b}", [P, P]) for b in range(2)]
        got = n.gather_sems("got", R)
        idx_in, base_in, ea_in, hot_in, slab_in, turned_in, pt_in, q_in, gated, summed, sums_free, total_in, to_in = (
            n.sems(s, R) for s in ("idx_in", "base_in", "ea_in", "hot_in", "slab_in", "turned_in", "pt_in", "q_in", "gated",
                                   "summed", "sums_free", "total_in", "to_in"))
        pre_in = n.sems("pre_in", 2)
        tab_added = n.gather_sems("tab_added", K4)
        marks, dve = net.marks, n.sem("dve")
        with nc.Block() as block:
            @block.sync
            def _(eng):
                regs = visit_registers(net, eng)
                for i in turns(eng, turn_count(net, eng)):
                    visit = look_up(net, eng, regs, i)
                    for b in range(R):
                        unit, at = visit[b]
                        small_loads(net, eng, i, b, unit, idx, idx_in, got, base, base_in, hot_in)
                        eng.wait_ge(q_in[b], i)
                        mark(eng, marks)
                        eng.dma_start(slab[:, b, :, :], x1_parts[bass.ds(at, P), :].rearrange("p (c d) -> p c d", d=D)).then_inc(slab_in[b], 16)
                        eng.wait_ge(summed[b], i)
                        mark(eng, marks)
                        eng.dma_start(ea[:, b], dram["ea"][bass.ds(unit * UNIT, UNIT), :].rearrange(
                            "(p k) d -> p k d", k=K4)).then_inc(ea_in[b], 16)
                        eng.dma_start(src_all[:, b, :], bc(dram["src_row"][bass.ds(unit * UNIT, UNIT)].rearrange(
                            "(o e) -> o e", o=1), [P, UNIT])).then_inc(ea_in[b], 16)

            @block.gpsimd
            def _(eng):
                n_turns = turn_count(net, eng)
                for i in turns(eng, n_turns):
                    for b in range(R):
                        eng.wait_ge(summed[b], i)
                        gather_unit(eng, marks, i, b, xs, x1, idx, idx_in, got)
                    for b in range(R):
                        eng.wait_ge(total_in[b], i + 1)
                        eng.wait_ge(to_in[b], i + 1)
                        for k in range(K4):
                            eng.wait_ge(tab_added[k], (i * R + b) * 16)
                            mark(eng, marks)
                            eng.indirect_dma_start(out=tabs[k], out_offset=bass.IndirectOffsetOnAxis(ap=to_i[:, b, k:k + 1], axis=0),
                                                   in_=total[:, b, k, :], in_offset=None, compute_op=ALU.add).then_inc(tab_added[k], 16)
                for k in range(K4):
                    eng.wait_ge(tab_added[k], n_turns * (R * 16))
                mark(eng, marks)

            @block.vector
            def _(eng):
                def add(i, b):
                    eng.wait_ge(summed[b], i + 1)
                    add_window(net, eng, i, b, visit[b][1], [(acc, sums[b % 2][:, :])], sums_free)

                regs = visit_registers(net, eng)
                for i in turns(eng, turn_count(net, eng)):
                    visit = look_up(net, eng, regs, i)
                    for b in range(R):
                        eng.wait_ge(base_in[b], i * 16 + 16)
                        eng.wait_ge(summed[b], i)
                        build_hot(net, eng, hot, base, b, visit[b][0]).then_inc(hot_in[b], 1)
                    for b in range(R):
                        unit = visit[b][0]
                        src = net.src_f[:, bass.ds(unit * K4, K4)]
                        steps = Steps(eng, dve, i * R + b, IDX)
                        eng.wait_ge(ea_in[b], i * 32 + 32)
                        mark(eng, marks)
                        steps.done(eng.tensor_tensor(same[:, b], src_all[:, b, :].rearrange("p (q k) -> p k q", k=K4),
                                                     bc(src.unsqueeze(2), [P, K4, P]), ALU.is_equal))
                        steps.settle()
                        steps.done(eng.tensor_tensor(before[:, :, :], same[:, b], bc(net.lower[:, :].unsqueeze(1), [P, K4, P]), ALU.mult))
                        steps.done(eng.tensor_scalar(off[:, :], src, -1.0, net.spare[:, 0:1], ALU.mult, ALU.add))
                        steps.settle()
                        steps.done(eng.tensor_reduce(again[:, :], before[:, :, :], AX, ALU.max))
                        steps.settle()
                        steps.done(eng.tensor_tensor(off[:, :], off[:, :], again[:, :], ALU.mult))
                        for k in range(K4):
                            eng.wait_ge(tab_added[k], i * (16 * R))
                        steps.settle()
                        mark(eng, marks)
                        steps.done(eng.tensor_tensor(off[:, :], off[:, :], src, ALU.add))
                        steps.settle()
                        mark(eng, marks)
                        eng.tensor_copy(to_i[:, b, :], off[:, :]).then_inc(to_in[b], 1)
                        eng.wait_ge(q_in[b], i + 1)
                        eng.tensor_tensor(xd[:, b], q[b % 2][:, :, :], ea[:, b], ALU.mult).then_inc(gated[b], 1)
                        eng.wait_ge(got[b], i * 64 + 64)
                        eng.tensor_tensor(xs[:, b], xs[:, b], ea[:, b], ALU.mult).then_inc(gated[b], 1)
                        steps.end()
                        if b:
                            add(i, b - 1)
                    add(i, R - 1)

            @block.scalar
            def _(eng):
                for i in turns(eng, turn_count(net, eng)):
                    for b in range(R):
                        copy_turned(eng, marks, i, b, turned, turned_in, pt, pt_in, q_in)
                    for b in range(R):
                        h = b % 2
                        eng.wait_ge(pre_in[h], i * (R // 2) + b // 2 + 1)
                        for k in range(K4):
                            eng.wait_ge(tab_added[k], i * (16 * R))
                        mark(eng, marks)
                        eng.activation(total[:, b], pres[h][:, :, :], ACT.Copy).then_inc(total_in[b], 1)

            @block.tensor
            def _(eng):
                def hand_out(i, b):
                    eng.wait_ge(pt_in[b], i + 1)
                    eng.wait_ge(slab_in[b], i * 16 + 16)
                    eng.wait_ge(gated[(b + 2) % R], i * 2 + (2 if b >= 2 else 0))
                    for k in range(K4):
                        for c in range(3):
                            mm = eng.matmul(q[b % 2][:, k, :], pt[:, b, k, :], slab[:, b, c, :], start=(c == 0), stop=(c == 2))
                    mm.then_inc(q_in[b], 1)

                def sum_up(i, b):
                    h = b % 2
                    eng.wait_ge(gated[b], i * 2 + 2)
                    eng.wait_ge(sums_free[(b + 2) % R], i + (1 if b >= 2 else 0))
                    eng.wait_ge(total_in[(b + 2) % R], i + (1 if b >= 2 else 0))
                    for k in range(K4):
                        mm = eng.matmul(pres[h][:, k, :], same[:, b, k, :], xd[:, b, k, :], start=True, stop=True)
                    mm.then_inc(pre_in[h], 1)
                    for k in range(K4):
                        mm = eng.matmul(sums[h][:, :], xs[:, b, k, :], hot[:, b, k, :], start=(k == 0), stop=(k == K4 - 1))
                    mm.then_inc(summed[b], 1)

                for i in turns(eng, turn_count(net, eng)):
                    for b in range(R):
                        turn_hot(eng, i, b, hot, hot_in, net.ident[:, :], turned, turned_in, pt_in)
                    hand_out(i, 0)
                    for b in range(R):
                        if b + 1 < R:
                            hand_out(i, b + 1)
                        sum_up(i, b)


def clear_tables(net, tabs):
    nc = net.nc
    n = net.scope("ct_")
    with n:
        zeros = n.sb("zeros", [P, NT, D])
        zeroed, written = n.sem("zeroed"), n.sem("written")
        with nc.Block() as block:
            @block.gpsimd
            def _(eng):
                eng.memset(zeros[:, :, :], 0.0).then_inc(zeroed, 1)

            @block.sync
            def _(eng):
                eng.wait_ge(zeroed, 1)
                for t in tabs:
                    eng.dma_start(t[0:NP, :].rearrange("(p t) d -> p t d", p=P), zeros[:, :, :]).then_inc(written, 16)
                    eng.dma_start(t[NP:TR, :], zeros[:, 0, :]).then_inc(written, 16)
                eng.wait_ge(written, 32 * len(tabs))


def nodes_gated(net, acc, tabs, x_row):
    nc, dram = net.nc, net.dram
    n = net.scope("n1_")
    PER = 1 + 3 + 2 + LN_STEPS
    with n:
        st = n.sb("st", [P, GC])
        parts = n.sb("parts", [P, K4, 4, D])
        z = n.sb("z", [P, 4, D])
        stats, moments, std = n.sb("stats", [P, 4, 6]), n.sb("moments", [P, 4, 2]), n.sb("std", [P, 4])
        turned = n.ps("turned", [P, GC])
        loaded, dve, turned_s, rooted, marks = (n.sem(s) for s in ("loaded", "dve", "turned_s", "rooted", "marks"))
        with nc.Block() as block:
            @block.sync
            def _(eng):
                for g in turns(eng, NG):
                    eng.wait_ge(dve, g * PER)
                    mark(eng, marks)
                    for k in range(K4):
                        eng.dma_start(parts[:, k], rows_of(tabs[k], g * GC)).then_inc(loaded, 16)

            @block.tensor
            def _(eng):
                for g in turns(eng, NG):
                    eng.wait_ge(dve, g * PER + 1)
                    for j in range(4):
                        mm = eng.transpose(turned[:, j * P:(j + 1) * P], st[:, j * P:(j + 1) * P], net.ident[:, :])
                    mm.then_inc(turned_s, 1)

            @block.scalar
            def _(eng):
                for g in turns(eng, NG):
                    eng.wait_ge(dve, g * PER + 6 + 9)
                    eng.activation(std[:, :], std[:, :], ACT.Sqrt).then_inc(rooted, 1)

            @block.vector
            def _(eng):
                for g in turns(eng, NG):
                    steps = Steps(eng, dve, g, PER)
                    steps.done(eng.tensor_copy(st[:, :], acc[:, bass.ds(g * GC, GC)]))
                    eng.wait_ge(loaded, g * (16 * K4) + 16 * K4)
                    steps.done(eng.tensor_tensor(parts[:, 0], parts[:, 0], parts[:, 1], ALU.add))
                    steps.done(eng.tensor_tensor(parts[:, 2], parts[:, 2], parts[:, 3], ALU.add))
                    steps.settle()
                    steps.done(eng.tensor_tensor(z[:, :, :], parts[:, 0], parts[:, 2], ALU.add))
                    steps.settle()
                    eng.wait_ge(turned_s, g + 1)
                    steps.done(eng.tensor_tensor(z[:, :, :], turned[:, :].rearrange("p (t d) -> p t d", d=D), z[:, :, :], ALU.add))
                    steps.settle()
                    steps.done(eng.tensor_tensor(z[:, :, :], z[:, :, :], x_row[:, bass.ds(g * 4, 4), :], ALU.add))
                    steps.settle()
                    layer_norm(eng, steps, z, stats, moments, std, x_row[:, bass.ds(g * 4, 4), :], marks, rooted, g + 1, 1e-5)
                    steps.end()


def edges_attention(net, kv, q_parts, acc, acc_z):
    nc = net.nc
    n = net.scope("l2_")
    PER = 3
    with n:
        idx = n.sb("idx", [P, R, K4], I32)
        base, dst = n.sb("base", [P, R]), n.sb("dst", [P, R, K4])
        kvs = n.sb("kvs", [P, R, K4, 2 * D])
        qk = n.sb("qk", [P, K4, D])
        hot = n.sb("hot", [P, R, K4, P])
        pt = n.sb("pt", [P, R, K4, P], BF16)
        slab = n.sb("slab", [P, R, 3, D], BF16)
        s = n.sb("s", [P, R, K4, H])
        msg = n.sb("msg", [P, R, K4, D])
        turned = [n.ps(f"turned{b}", [P, K4, P]) for b in range(2)]
        q = [n.ps(f"q{b}", [P, K4, D]) for b in range(2)]
        both = [n.ps(f"both{b}", [P, 2, P]) for b in range(R)]
        sums, zs = [t[:, 0, :] for t in both], [t[0:H, 1, :] for t in both]
        got = n.gather_sems("got", R)
        idx_in, base_in, hot_in, slab_in, turned_in, pt_in, q_in, scored, weighed, ready, summed, sums_free = (n.sems(x, R) for x in (
            "idx_in", "base_in", "hot_in", "slab_in", "turned_in", "pt_in", "q_in", "scored", "weighed", "ready", "summed", "sums_free"))
        marks, dve = net.marks, n.sem("dve")
        with nc.Block() as block:
            @block.sync
            def _(eng):
                regs = visit_registers(net, eng)
                for i in turns(eng, turn_count(net, eng)):
                    visit = look_up(net, eng, regs, i)
                    for b in range(R):
                        unit, at = visit[b]
                        source_loads(net, eng, i, b, unit, idx, idx_in, got)
                        visit_loads(net, eng, i, b, unit, dst, base, base_in, hot_in)
                        eng.wait_ge(q_in[b], i)
                        mark(eng, marks)
                        eng.dma_start(slab[:, b, :, :], q_parts[bass.ds(at, P), :].rearrange("p (c d) -> p c d", d=D)).then_inc(slab_in[b], 16)

            @block.gpsimd
            def _(eng):
                for i in turns(eng, turn_count(net, eng)):
                    for b in range(R):
                        eng.wait_ge(ready[b], i)
                        gather_unit(eng, marks, i, b, kvs, kv, idx, idx_in, got)

            @block.vector
            def _(eng):
                def score(i, b):
                    steps = Steps(eng, dve, i * R + b, PER)
                    eng.wait_ge(q_in[b], i + 1)
                    eng.wait_ge(got[b], i * 64 + 64)
                    steps.done(eng.tensor_tensor(qk[:, :, :], q[b % 2][:, :, :], kvs[:, b, :, 0:D], ALU.mult))
                    steps.settle()
                    steps.done(eng.tensor_reduce(s[:, b], qk[:, :, :].rearrange("p k (h c) -> p k h c", h=H), AX, ALU.add))
                    steps.settle()
                    steps.done(eng.tensor_scalar(s[:, b], s[:, b], 1.0 / DH ** 0.5, 5.0, ALU.mult, ALU.min))
                    steps.settle()
                    eng.tensor_scalar(s[:, b], s[:, b], -5.0, None, ALU.max).then_inc(scored[b], 1)
                    steps.end()

                def weigh(i, b):
                    eng.wait_ge(weighed[b], i + 1)
                    eng.tensor_tensor(msg[:, b].rearrange("p k (h c) -> p k h c", h=H),
                                      kvs[:, b, :, D:2 * D].rearrange("p k (h c) -> p k h c", h=H),
                                      bc(s[:, b].unsqueeze(3), [P, K4, H, DH]), ALU.mult).then_inc(ready[b], 1)

                def add(i, b):
                    eng.wait_ge(summed[b], i + 1)
                    add_window(net, eng, i, b, visit[b][1], [(acc, sums[b]), (acc_z, zs[b])], sums_free)

                def build(i, b):
                    eng.wait_ge(base_in[b], i * 32 + 32)
                    eng.wait_ge(summed[b], i)
                    hot_here(net, eng, hot, dst, base, b).then_inc(hot_in[b], 1)

                regs = visit_registers(net, eng)
                for b in range(R):
                    build(0, b)
                for i, final in rolling(eng, last_turn(net, eng)):
                    visit = look_up(net, eng, regs, i)
                    for b in range(R + 2):
                        if b < R:
                            score(i, b)
                        if 1 <= b <= R:
                            weigh(i, b - 1)
                        if b >= 2:
                            add(i, b - 2)
                            for visit_later in later(i, b - 2, R, final):
                                build(*visit_later)
                    mark(eng, marks)

            @block.scalar
            def _(eng):
                for b in range(3):
                    copy_turned(eng, marks, 0, b, turned, turned_in, pt, pt_in, q_in)
                for i, final in rolling(eng, last_turn(net, eng)):
                    for b in range(R):
                        eng.wait_ge(scored[b], i + 1)
                        eng.activation(s[:, b], s[:, b], ACT.Exp).then_inc(weighed[b], 1)
                        for visit in later(i, b, 3, final):
                            copy_turned(eng, marks, *visit, turned, turned_in, pt, pt_in, q_in)

            @block.tensor
            def _(eng):
                def hand_out(i, b):
                    eng.wait_ge(pt_in[b], i + 1)
                    eng.wait_ge(slab_in[b], i * 16 + 16)
                    eng.wait_ge(scored[(b + 2) % R], i + (1 if b >= 2 else 0))
                    for k in range(K4):
                        for c in range(3):
                            mm = eng.matmul(q[b % 2][:, k, :], pt[:, b, k, :], slab[:, b, c, :], start=(c == 0), stop=(c == 2))
                    mm.then_inc(q_in[b], 1)

                def sum_up(i, b):
                    eng.wait_ge(sums_free[b], i * 2)
                    eng.wait_ge(weighed[b], i + 1)
                    for k in range(K4):
                        eng.matmul(zs[b], s[:, b, k, :], hot[:, b, k, :], start=(k == 0), stop=(k == K4 - 1))
                    eng.wait_ge(ready[b], i + 1)
                    for k in range(K4):
                        mm = eng.matmul(sums[b], msg[:, b, k, :], hot[:, b, k, :], start=(k == 0), stop=(k == K4 - 1))
                    mm.then_inc(summed[b], 1)

                for b in range(3):
                    turn_hot(eng, 0, b, hot, hot_in, net.ident[:, :], turned, turned_in, pt_in)
                for b in range(2):
                    hand_out(0, b)
                for i, final in rolling(eng, last_turn(net, eng)):
                    for b in range(R):
                        for visit in later(i, b, 2, final):
                            hand_out(*visit)
                        for visit in later(i, b, 3, final):
                            turn_hot(eng, *visit, hot, hot_in, net.ident[:, :], turned, turned_in, pt_in)
                        sum_up(i, b)


def nodes_attention(net, acc, acc_z, x_row, x_T):
    nc, dram = net.nc, net.dram
    n = net.scope("n2_")
    with n:
        hx = n.sb("hx", [P, NP])
        wo, w1, w2 = n.sb("wo", [D, D]), n.sb("w1", [D, 2, P]), n.sb("w2", [P, 2, D])
        bo, b1, b2 = n.sb("bo", [P, 1]), n.sb("b1", [P, 2]), n.sb("b2", [P, 1])
        bn = n.sb("bn", [P, 4])
        z = n.sb("z", [H, GC])
        h, h1 = n.sb("h", [P, GC]), n.sb("h1", [P, 2, GC])
        stats, mv, coef, std = n.sb("stats", [P, NG, 6]), n.sb("mv", [P, 2]), n.sb("coef", [P, 2]), n.sb("std", [P, 1])
        pz, po = n.ps("pz", [P, GC]), n.ps("po", [P, GC])
        p1 = [n.ps(f"p1{f}", [P, GC]) for f in range(2)]
        marks = n.sem("marks")

        def batch_coefficients(name, gain, bias):
            dve, rooted = n.sem(name + "dve"), n.sem(name + "rooted")
            with nc.Block() as block:
                @block.scalar
                def _(eng):
                    eng.wait_ge(dve, 2)
                    eng.activation(std[:, :], std[:, :], ACT.Sqrt).then_inc(rooted, 1)

                @block.vector
                def _(eng):
                    steps = Steps(eng, dve)
                    steps.done(eng.bn_aggr(mv[:, :], stats[:, :, :]))
                    steps.settle()
                    steps.done(eng.tensor_scalar(std[:, :], mv[:, 1:2], 1e-5, None, ALU.add))
                    eng.wait_ge(rooted, 1)
                    steps.done(eng.reciprocal(std[:, :], std[:, :]))
                    steps.settle()
                    steps.done(eng.tensor_tensor(coef[:, 0:1], std[:, :], gain, ALU.mult))
                    steps.settle()
                    steps.done(eng.tensor_tensor(std[:, :], mv[:, 0:1], coef[:, 0:1], ALU.mult))
                    steps.settle()
                    steps.done(eng.tensor_tensor(coef[:, 1:2], bias, std[:, :], ALU.subtract))

        loaded, dve, spread, made = n.sem("loaded"), n.sem("dve"), n.sem("spread"), n.sem("made")
        with nc.Block() as block:
            @block.sync
            def _(eng):
                eng.dma_start(wo[:, :], dram["L2_gnn_Wo"]).then_inc(loaded, 16)
                eng.dma_start(w1[:, :, :], dram["L2_gnn_W1"].rearrange("d (f o) -> d f o", f=2)).then_inc(loaded, 16)
                eng.dma_start(w2[:, :, :], dram["L2_gnn_W2"].rearrange("(f o) d -> o f d", f=2)).then_inc(loaded, 16)
                eng.dma_start(bo[:, :], cols(dram["L2_gnn_bo"])).then_inc(loaded, 16)
                for f in range(2):
                    eng.dma_start(b1[:, f:f + 1], cols(dram["L2_gnn_b1"][f * P:(f + 1) * P])).then_inc(loaded, 16)
                eng.dma_start(b2[:, :], cols(dram["L2_gnn_b2"])).then_inc(loaded, 16)
                for c, name in enumerate(("bn1_g", "bn1_b", "bn2_g", "bn2_b")):
                    eng.dma_start(bn[:, c:c + 1], cols(dram["L2_gnn_" + name])).then_inc(loaded, 16)
                eng.wait_ge(loaded, 16 * 11)

            @block.vector
            def _(eng):
                eng.wait_ge(loaded, 16 * 11)

                def group(g, width):
                    steps = Steps(eng, dve, g, 5)
                    steps.done(eng.tensor_scalar(z[:, :], acc_z[:, bass.ds(g * GC, GC)], 1e-6, None, ALU.add))
                    steps.settle()
                    steps.done(eng.reciprocal(z[:, :], z[:, :]))
                    eng.wait_ge(spread, g + 1)
                    steps.done(eng.tensor_tensor(h[:, :], acc[:, bass.ds(g * GC, GC)], pz[:, :], ALU.mult))
                    eng.wait_ge(made, g + 1)
                    steps.done(eng.scalar_tensor_tensor(out=hx[:, bass.ds(g * GC, GC)], in0=po[:, :], scalar=bo[:, 0:1],
                                                        in1=x_T[:, bass.ds(g * GC, GC)], op0=ALU.add, op1=ALU.add))
                    steps.settle()
                    mark(eng, marks)
                    steps.done(eng.bn_stats(stats[:, bass.ds(g, 1), :].rearrange("p a s -> p (a s)"), hx[:, bass.ds(g * GC, width)]))
                    steps.end()

                for g in turns(eng, NG - 1):
                    group(g, GC)
                group(NG - 1, LASTN)

            @block.tensor
            def _(eng):
                for g in turns(eng, NG):
                    eng.wait_ge(dve, g * 5 + 2)
                    eng.matmul(pz[:, :], net.expand[0:H, :], z[:, :], start=True, stop=True).then_inc(spread, 1)
                    eng.wait_ge(dve, g * 5 + 3)
                    eng.matmul(po[:, :], wo[:, :], h[:, :], start=True, stop=True).then_inc(made, 1)
        batch_coefficients("a_", bn[:, 0:1], bn[:, 1:2])

        dve, hid, relu, made2 = n.sem("dve2"), n.sem("hid"), n.sem("relu"), n.sem("made2")
        with nc.Block() as block:
            @block.vector
            def _(eng):
                def group(g, width):
                    steps = Steps(eng, dve, g, 3)
                    steps.done(eng.tensor_scalar(h[:, :], hx[:, bass.ds(g * GC, GC)], coef[:, 0:1], coef[:, 1:2], ALU.mult, ALU.add))
                    steps.settle()
                    eng.wait_ge(made2, g + 1)
                    steps.done(eng.scalar_tensor_tensor(out=hx[:, bass.ds(g * GC, GC)], in0=po[:, :], scalar=b2[:, 0:1],
                                                        in1=h[:, :], op0=ALU.add, op1=ALU.add))
                    steps.settle()
                    mark(eng, marks)
                    steps.done(eng.bn_stats(stats[:, bass.ds(g, 1), :].rearrange("p a s -> p (a s)"), hx[:, bass.ds(g * GC, width)]))
                    steps.end()

                for g in turns(eng, NG - 1):
                    group(g, GC)
                group(NG - 1, LASTN)

            @block.scalar
            def _(eng):
                for g in turns(eng, NG):
                    for f in range(2):
                        eng.wait_ge(hid, g * 2 + f + 1)
                        eng.activation(h1[:, f, :], p1[f][:, :], ACT.Relu, bias=b1[:, f:f + 1]).then_inc(relu, 1)

            @block.tensor
            def _(eng):
                for g in turns(eng, NG):
                    eng.wait_ge(dve, g * 3 + 1)
                    for f in range(2):
                        eng.matmul(p1[f][:, :], w1[:, f, :], h[:, :], start=True, stop=True).then_inc(hid, 1)
                    for f in range(2):
                        eng.wait_ge(relu, g * 2 + f + 1)
                        mm = eng.matmul(po[:, :], w2[:, f, :], h1[:, f, :], start=(f == 0), stop=(f == 1))
                    mm.then_inc(made2, 1)
        batch_coefficients("b_", bn[:, 2:3], bn[:, 3:4])

        PER = 2 + LN_STEPS
        y = h1[:, 0, :].rearrange("p (t d) -> p t d", d=D)
        rs, rm, rstd = n.sb("rs", [P, 4, 6]), n.sb("rm", [P, 4, 2]), n.sb("rstd", [P, 4])
        dve, turned, rooted = n.sem("dve3"), n.sem("turned"), n.sem("rooted")
        with nc.Block() as block:
            @block.vector
            def _(eng):
                for g in turns(eng, NG):
                    steps = Steps(eng, dve, g, PER)
                    steps.done(eng.tensor_scalar(h[:, :], hx[:, bass.ds(g * GC, GC)], coef[:, 0:1], coef[:, 1:2], ALU.mult, ALU.add))
                    eng.wait_ge(turned, g + 1)
                    steps.done(eng.tensor_tensor(y, po[:, :].rearrange("p (t d) -> p t d", d=D), x_row[:, bass.ds(g * 4, 4), :], ALU.add))
                    steps.settle()
                    layer_norm(eng, steps, y, rs, rm, rstd, x_row[:, bass.ds(g * 4, 4), :], marks, rooted, g + 1, 1e-5)
                    steps.end()

            @block.scalar
            def _(eng):
                for g in turns(eng, NG):
                    eng.wait_ge(dve, g * PER + 2 + 9)
                    eng.activation(rstd[:, :], rstd[:, :], ACT.Sqrt).then_inc(rooted, 1)

            @block.tensor
            def _(eng):
                for g in turns(eng, NG):
                    eng.wait_ge(dve, g * PER + 1)
                    for j in range(4):
                        mm = eng.transpose(po[:, j * P:(j + 1) * P], h[:, j * P:(j + 1) * P], net.ident[:, :])
                    mm.then_inc(turned, 1)


def hyperbolic(net, x_row, kvm, qm_parts):
    nc, dram = net.nc, net.dram
    n = net.scope("hy_")
    with n:
        xx = n.sb("xx", [P, 4, D])
        m = n.sb("m", [P, 2, 4, D])
        three = n.sb("three", [P, 4, 3, D], BF16)
        splits = n.sem("splits")
        norm, y, th, f = (n.sb(s, [P, NT]) for s in ("norm", "y", "th", "f"))
        c, most = n.sb("c", [P, 2]), n.sb("most", [P, 1])
        loaded, squared, dve, act, made, stored, marks = (n.sem(s) for s in ("loaded", "squared", "dve", "act", "made", "stored", "marks"))
        with nc.Block() as block:
            @block.sync
            def _(eng):
                eng.dma_start(c[:, 0:1], everywhere(dram["L3_gnn_c_mag"], 1)).then_inc(loaded, 16)
                for g in turns(eng, NG):
                    eng.wait_ge(made, g * 4 + 4)
                    mark(eng, marks)
                    eng.dma_start(rows_of(kvm, g * GC)[:, :, 2 * D:3 * D], m[:, 0]).then_inc(stored, 16)
                    eng.wait_ge(splits, g * (1 + SPLIT_STEPS) + 1 + SPLIT_STEPS)
                    mark(eng, marks)
                    for part in range(3):
                        eng.dma_start(part_rows(qm_parts, g, 2 * D)[:, :, part, D:2 * D], three[:, :, part, :]).then_inc(stored, 16)
                eng.wait_ge(stored, 64 * NG)

            @block.scalar
            def _(eng):
                eng.wait_ge(dve, 4)
                eng.activation(norm[:, :], norm[:, :], ACT.Sqrt).then_inc(act, 1)
                eng.activation(c[:, 1:2], c[:, 0:1], ACT.Sqrt).then_inc(act, 1)
                eng.wait_ge(dve, 5)
                eng.activation(th[:, :], y[:, :], ACT.Tanh).then_inc(act, 1)

            @block.vector
            def _(eng):
                for g in turns(eng, NG):
                    eng.wait_ge(squared, g * 2)
                    mark(eng, marks)
                    eng.tensor_tensor(xx[:, :, :], x_row[:, bass.ds(g * 4, 4), :], x_row[:, bass.ds(g * 4, 4), :], ALU.mult).then_inc(squared, 1)
                    eng.wait_ge(squared, g * 2 + 1)
                    mark(eng, marks)
                    eng.tensor_reduce(norm[:, bass.ds(g * 4, 4)], xx[:, :, :], AX, ALU.add).then_inc(squared, 1)
                eng.wait_ge(squared, 2 * NG)
                eng.wait_ge(loaded, 16)
                steps = Steps(eng, dve)
                steps.done(eng.tensor_scalar(norm[:, :], norm[:, :], 1e-30, None, ALU.max))
                steps.done(eng.tensor_scalar(c[:, 1:2], c[:, 0:1], -1.0, None, ALU.mult))
                steps.settle()
                steps.done(eng.tensor_tensor(c[:, 0:1], c[:, 0:1], c[:, 1:2], ALU.max))
                steps.settle()
                steps.done(eng.tensor_scalar(c[:, 0:1], c[:, 0:1], 1e-15, None, ALU.max))
                eng.wait_ge(act, 2)
                steps.done(eng.tensor_scalar(y[:, :], norm[:, :], c[:, 1:2], None, ALU.mult))
                steps.settle()
                eng.wait_ge(act, 3)
                steps.done(eng.reciprocal(f[:, :], y[:, :]))
                steps.done(eng.reciprocal(most[:, :], c[:, 1:2]))
                steps.settle()
                steps.done(eng.tensor_tensor(f[:, :], f[:, :], th[:, :], ALU.mult))
                steps.done(eng.tensor_scalar(most[:, :], most[:, :], 1.0 - 1e-5, None, ALU.mult))
                steps.settle()
                steps.done(eng.tensor_tensor(norm[:, :], norm[:, :], f[:, :], ALU.mult))
                steps.settle()
                steps.done(eng.reciprocal(norm[:, :], norm[:, :]))
                steps.settle()
                steps.done(eng.tensor_scalar(norm[:, :], norm[:, :], most[:, 0:1], 1.0, ALU.mult, ALU.min))
                steps.settle()
                steps.done(eng.tensor_tensor(f[:, :], f[:, :], norm[:, :], ALU.mult))
                steps.settle()
                for g in turns(eng, NG):
                    eng.wait_ge(stored, g * 64)
                    mark(eng, marks)
                    for j in range(4):
                        eng.tensor_scalar(m[:, 0, j, :], x_row[:, bass.ds(g * 4 + j, 1), :].rearrange("p a d -> p (a d)"),
                                          f[:, bass.ds(g * 4 + j, 1)], None, ALU.mult).then_inc(made, 1)
                    steps = Steps(eng, splits, g, 1 + SPLIT_STEPS)
                    eng.wait_ge(made, g * 4 + 4)
                    steps.done(eng.tensor_scalar(m[:, 1], m[:, 0], -1.0, None, ALU.mult))
                    steps.settle()
                    split(eng, steps, m[:, 1], *(three[:, :, c, :] for c in range(3)))
                    steps.settle()
                    mark(eng, marks)


def edges_relational(net, kvm, qm_parts, dot, dec, dist2, v_rows):
    nc, dram = net.nc, net.dram
    n = net.scope("l3_")
    PARTS3 = 3 * 5
    with n:
        idx = n.sb("idx", [P, R, K4], I32)
        base, dst = n.sb("base", [P, R]), n.sb("dst", [P, R, K4])
        ks = n.sb("ks", [P, R, K4, 3 * D])
        qk = n.sb("qk", [P, K4, D])
        hot = n.sb("hot", [P, R, K4, P], BF16)
        pt = n.sb("pt", [P, R, K4, P], BF16)
        slab = n.sb("slab", [P, R, 3, 2 * D], BF16)
        te = n.sb("te", [TE, R, UNIT])
        tb = n.sb("tb", [TB, R, UNIT], BF16)
        wk = n.sb("wk", [TE, D])
        w3 = n.sb("w3", [3, P])
        rel = n.sb("rel", [2, D])
        cut3, cut2 = n.sb("cut3", [3, 3, P], BF16), n.sb("cut2", [2, 3, D], BF16)
        wd1 = n.sb("wd1", [TB, P], BF16)
        wq = n.sb("wq", [TB, D], BF16)
        wd2 = n.sb("wd2", [P, H])
        hid = n.sb("hid", [P, UNIT])
        inside, shifted = n.sb("inside", [P, K4]), n.sb("shifted", [P, R, K4])
        new_dot, new_dist = n.sb("new_dot", [P, K4, H]), n.sb("new_dist", [P, K4])
        turned = [n.ps("turned", [P, K4, P], BF16)]
        q = [n.ps(f"q{b}", [P, K4, 2 * D]) for b in range(2)]
        kadd, ph, pd = n.ps("kadd", [P, K4, D]), n.ps("ph", [P, UNIT]), n.ps("pd", [P, K4, H])
        got = n.gather_sems("got", R)
        idx_in, base_in, hot_in, slab_in, turned_in, pt_in, q_in, te_in, v_out, used, squared, shift_in = (n.sems(x, R) for x in (
            "idx_in", "base_in", "hot_in", "slab_in", "turned_in", "pt_in", "q_in", "te_in", "v_out", "used", "squared", "shift_in"))
        zeroed, loaded, cut, placed, dve, hid_in, relu, k_in, pd_in, dec_in = (n.sem(x) for x in (
            "zeroed", "loaded", "cut", "placed", "dve", "hid_in", "relu", "k_in", "pd_in", "dec_in"))
        marks = net.marks
        PER = 10
        with nc.Block() as block:
            @block.gpsimd
            def _(eng):
                for w in (wk, w3, wd2, wd1, wq, dist2):
                    eng.memset(w[:, :], 0.0).then_inc(zeroed, 1)
                eng.memset(dot[:, :, :], 0.0).then_inc(zeroed, 1)

            @block.sync
            def _(eng):
                eng.wait_ge(zeroed, 7)
                eng.dma_start(wk[0:32, :], dram["L3_gnn_Wt"]).then_inc(loaded, 16)
                eng.dma_start(wk[32:33, :], dram["L3_gnn_bt"].rearrange("(o d) -> o d", o=1)).then_inc(loaded, 16)
                for t in range(2):
                    eng.dma_start(wk[34 - t:35 - t, :], dram["L3_gnn_rel_k"][t:t + 1, :]).then_inc(loaded, 16)
                eng.dma_start(rel[:, :], dram["L3_gnn_rel_q"]).then_inc(loaded, 16)
                eng.dma_start(w3[0:1, 0:HID], dram["L3_gnn_Wd1"][0:1, :]).then_inc(loaded, 16)
                eng.dma_start(w3[2:3, 0:HID], dram["L3_gnn_Wd1"][1:2, :]).then_inc(loaded, 16)
                eng.dma_start(w3[1:2, 0:HID], dram["L3_gnn_bd1"].rearrange("(o d) -> o d", o=1)).then_inc(loaded, 16)
                eng.dma_start(w3[1:2, HID:HID + 1], dram["one"].rearrange("(o d) -> o d", o=1)).then_inc(loaded, 16)
                eng.dma_start(wd2[0:HID, :], dram["L3_gnn_Wd2"]).then_inc(loaded, 16)
                eng.dma_start(wd2[HID:HID + 1, :], dram["L3_gnn_bd2"].rearrange("(o d) -> o d", o=1)).then_inc(loaded, 16)
                eng.wait_ge(cut, 1 + 2 * SPLIT_STEPS)
                rows = [(0, 0, 0), (1, 0, 1), (2, 0, 2), (3, 0, 0), (4, 0, 1), (5, 0, 0)]
                rows += [(6 + c, 1, c) for c in range(3)] + [(9 + c, 2, c) for c in range(3)]
                for to, of, c in rows:
                    eng.dma_start(wd1[to:to + 1, :], cut3[of:of + 1, c, :]).then_inc(placed, 16)
                for c in range(3):
                    eng.dma_start(wq[9 + c:10 + c, :], cut2[1:2, c, :]).then_inc(placed, 16)
                    eng.dma_start(wq[12 + c:13 + c, :], cut2[0:1, c, :]).then_inc(placed, 16)
                eng.wait_ge(placed, 16 * 18)

            @block.vector
            def _(eng):
                eng.wait_ge(loaded, 16 * 11)
                steps = Steps(eng, cut)
                steps.done(eng.tensor_scalar(w3[:, :], w3[:, :], net.type_scale[0:3, 0:1], None, ALU.mult))
                steps.settle()
                split(eng, steps, w3[:, :], cut3[:, 0, :], cut3[:, 1, :], cut3[:, 2, :])
                split(eng, steps, rel[:, :], cut2[:, 0, :], cut2[:, 1, :], cut2[:, 2, :])

        with nc.Block() as block:
            @block.sync
            def _(eng):
                regs = visit_registers(net, eng)
                for i in turns(eng, turn_count(net, eng)):
                    visit = look_up(net, eng, regs, i)
                    for b in range(R):
                        unit, at = visit[b]
                        source_loads(net, eng, i, b, unit, idx, idx_in, got)
                        visit_loads(net, eng, i, b, unit, dst, base, base_in, shift_in)
                        eng.wait_ge(used[b], i)
                        mark(eng, marks)
                        eng.dma_start(slab[:, b, :, :], qm_parts[bass.ds(at, P), :].rearrange("p (c d) -> p c d", d=2 * D)).then_inc(slab_in[b], 16)
                        eng.dma_start(te[0:33, b, :], dram["te"][:, bass.ds(unit * UNIT, UNIT)]).then_inc(te_in[b], 16)
                        eng.dma_start(te[33:35, b, :], net.type_rows[:, bass.ds(unit * UNIT, UNIT)]).then_inc(te_in[b], 16)
                        eng.dma_start(tb[:, b, :], net.parts[:, bass.ds(unit * UNIT, UNIT)]).then_inc(te_in[b], 16)

            @block.gpsimd
            def _(eng):
                for i in turns(eng, turn_count(net, eng)):
                    for b in range(R):
                        eng.wait_ge(used[b], i)
                        eng.wait_ge(v_out[b], i * 16)
                        gather_unit(eng, marks, i, b, ks, kvm, idx, idx_in, got)

            @block.vector
            def _(eng):
                def build(i, b):
                    eng.wait_ge(base_in[b], i * 32 + 32)
                    eng.tensor_scalar(shifted[:, b, :], dst[:, b, :], base[:, b:b + 1], None, ALU.subtract).then_inc(shift_in[b], 1)
                    eng.wait_ge(pt_in[b], i)
                    eng.wait_ge(shift_in[b], i + 1)
                    eng.tensor_tensor(hot[:, b], bc(net.iota[:, :].unsqueeze(1), [P, K4, P]),
                                      bc(shifted[:, b, :].unsqueeze(2), [P, K4, P]), ALU.is_equal).then_inc(hot_in[b], 1)

                def meet(i, b, unit):
                    u4 = bass.ds(unit * K4, K4)
                    steps = Steps(eng, dve, i * R + b, PER)
                    mk = ks[:, b, :, 2 * D:3 * D]
                    steps.done(eng.tensor_scalar(inside[:, :], shifted[:, b, :], 0.0, None, ALU.is_ge))
                    eng.wait_ge(q_in[b], i + 1)
                    eng.wait_ge(got[b], i * 64 + 64)
                    eng.tensor_tensor(mk, mk, q[b % 2][:, :, D:2 * D], ALU.add).then_inc(squared[b], 1)
                    eng.wait_ge(k_in, i * R + b + 1)
                    steps.settle()
                    mark(eng, marks)
                    steps.done(eng.tensor_tensor(ks[:, b, :, 0:D], ks[:, b, :, 0:D], kadd[:, :, :], ALU.add))
                    steps.settle()
                    steps.done(eng.tensor_tensor(qk[:, :, :], q[b % 2][:, :, 0:D], ks[:, b, :, 0:D], ALU.mult))
                    steps.done(eng.scalar_tensor_tensor(out=inside[:, :], in0=shifted[:, b, :], scalar=float(P), in1=inside[:, :],
                                                        op0=ALU.is_lt, op1=ALU.mult))
                    steps.settle()
                    steps.done(eng.tensor_reduce(new_dot[:, :, :], qk[:, :, :].rearrange("p k (h c) -> p k h c", h=H), AX, ALU.add))
                    steps.settle()
                    steps.done(eng.tensor_tensor(new_dot[:, :, :], new_dot[:, :, :], bc(inside[:, :].unsqueeze(2), [P, K4, H]), ALU.mult))
                    steps.settle()
                    mark(eng, marks)
                    steps.done(eng.tensor_tensor(dot[:, u4, :], dot[:, u4, :], new_dot[:, :, :], ALU.add))
                    eng.wait_ge(squared[b], i * 2 + 2)
                    steps.done(eng.tensor_reduce(new_dist[:, :], mk, AX, ALU.add))
                    steps.settle()
                    steps.done(eng.tensor_tensor(new_dist[:, :], new_dist[:, :], inside[:, :], ALU.mult))
                    steps.settle()
                    mark(eng, marks)
                    steps.done(eng.tensor_tensor(dist2[:, u4], dist2[:, u4], new_dist[:, :], ALU.add))
                    steps.settle()
                    mark(eng, used[b])
                    steps.end()

                regs = visit_registers(net, eng)
                for b in range(3):
                    build(0, b)
                for i, final in rolling(eng, last_turn(net, eng)):
                    visit = look_up(net, eng, regs, i)
                    for b in range(R):
                        meet(i, b, visit[b][0])
                        for visit_later in later(i, b, 3, final):
                            build(*visit_later)

            @block.scalar
            def _(eng):
                def open_hidden(u):
                    eng.wait_ge(hid_in, u + 1)
                    if not isinstance(u, int) or u:
                        eng.wait_ge(pd_in, u)
                    mark(eng, marks)
                    eng.activation(hid[:, :], ph[:, :], ACT.Relu).then_inc(relu, 1)

                regs = visit_registers(net, eng)
                last = last_turn(net, eng)
                for b in range(2):
                    copy_turned(eng, marks, 0, b, turned, turned_in, pt, pt_in, q_in)
                open_hidden(0)
                for i, final in rolling(eng, last):
                    visit = look_up(net, eng, regs, i)
                    for b in range(R):
                        u, unit = i * R + b, visit[b][0]
                        for visit_later in later(i, b, 2, final):
                            copy_turned(eng, marks, *visit_later, turned, turned_in, pt, pt_in, q_in)
                        for _ in later(i, b, 1, final):
                            open_hidden(u + 1)
                        eng.wait_ge(pd_in, u + 1)
                        eng.wait_ge(dec_in, u)
                        mark(eng, marks)
                        eng.activation(dec[:, bass.ds(unit * K4, K4), :], pd[:, :, :], ACT.Copy).then_inc(dec_in, 1)
                        mk = ks[:, b, :, 2 * D:3 * D]
                        eng.wait_ge(squared[b], i * 2 + 1)
                        eng.activation(mk, mk, ACT.Square).then_inc(squared[b], 1)
                        eng.dma_start(v_rows[bass.ds(unit * UNIT, UNIT), :].rearrange("(p k) d -> p k d", k=K4),
                                      ks[:, b, :, D:2 * D]).then_inc(v_out[b], 16)
                for b in range(R):
                    eng.wait_ge(v_out[b], (last + 1) * 16)
                mark(eng, marks)

            @block.tensor
            def _(eng):
                def hidden_sums(i, b):
                    eng.wait_ge(te_in[b], i * 48 + 48)
                    eng.wait_ge(relu, i * R + b)
                    eng.matmul(ph[:, :], wd1[:, :], tb[:, b, :], start=True, stop=True).then_inc(hid_in, 1)

                def hand_out(i, b):
                    eng.wait_ge(pt_in[b], i + 1)
                    eng.wait_ge(slab_in[b], i * 16 + 16)
                    eng.wait_ge(used[(b + 2) % R], i + (1 if b >= 2 else 0))
                    for k in range(K4):
                        for c in range(3):
                            eng.matmul(q[b % 2][:, k, :], pt[:, b, k, :], slab[:, b, c, :], start=(c == 0), stop=False, skip_group_check=True)
                        mm = eng.matmul(q[b % 2][:, k, 0:D], tb[:, b, k * P:(k + 1) * P], wq[:, :], start=False, stop=True, skip_group_check=True)
                    mm.then_inc(q_in[b], 1)

                def key_sums(i, b):
                    u = i * R + b
                    if not isinstance(u, int) or u:
                        eng.wait_ge(dve, (u - 1) * PER + 2)
                    for k in range(K4):
                        mm = eng.matmul(kadd[:, k, :], te[:, b, k * P:(k + 1) * P], wk[:, :], start=True, stop=True)
                    mm.then_inc(k_in, 1)

                def decay_sums(u):
                    eng.wait_ge(relu, u + 1)
                    eng.wait_ge(dec_in, u)
                    for k in range(K4):
                        mm = eng.matmul(pd[:, k, :], hid[:, k * P:(k + 1) * P], wd2[:, :], start=True, stop=True)
                    mm.then_inc(pd_in, 1)

                for b in range(2):
                    turn_hot(eng, 0, b, hot, hot_in, net.ident_b[:, :], turned, turned_in, pt_in)
                hidden_sums(0, 0)
                hand_out(0, 0)
                key_sums(0, 0)
                for i, final in rolling(eng, last_turn(net, eng)):
                    for b in range(R):
                        for visit in later(i, b, 2, final):
                            turn_hot(eng, *visit, hot, hot_in, net.ident_b[:, :], turned, turned_in, pt_in)
                        decay_sums(i * R + b)
                        for visit in later(i, b, 1, final):
                            hidden_sums(*visit)
                            hand_out(*visit)
                            key_sums(*visit)


def logits(net, dot, dec, dist2):
    nc, dram = net.nc, net.dram
    n = net.scope("lg_")
    with n:
        small = n.sb("small", [P, 6, H])
        far = n.sb("far", [P, NU * K4, H])
        loaded, dve, act = n.sem("loaded"), n.sem("dve"), n.sem("act")
        every = [P, NU * K4, H]
        with nc.Block() as block:
            @block.sync
            def _(eng):
                for c, name in enumerate(("decay_scale", "logit_alpha", "hyp_beta")):
                    eng.dma_start(small[:, c, :], everywhere(dram["L3_gnn_" + name], H)).then_inc(loaded, 16)
                eng.wait_ge(loaded, 48)

            @block.scalar
            def _(eng):
                eng.activation(dec[:, :, :], dec[:, :, :], ACT.Tanh).then_inc(act, 1)
                eng.wait_ge(loaded, 48)
                eng.activation(small[:, 3, :], small[:, 1, :], ACT.Exp, scale=-1.0).then_inc(act, 1)
                eng.wait_ge(dve, 1)
                eng.activation(dec[:, :, :], dec[:, :, :], ACT.Exp).then_inc(act, 1)
                eng.activation(dist2[:, :], dist2[:, :], ACT.Sqrt).then_inc(act, 1)

            @block.vector
            def _(eng):
                steps = Steps(eng, dve)
                eng.wait_ge(loaded, 48)
                eng.wait_ge(act, 2)
                steps.done(eng.tensor_tensor(dec[:, :, :], dec[:, :, :], bc(small[:, 0, :].unsqueeze(1), every), ALU.mult))
                steps.done(eng.tensor_scalar(small[:, 3, :], small[:, 3, :], 1.0, None, ALU.add))
                steps.settle()
                steps.done(eng.reciprocal(small[:, 4, :], small[:, 3, :]))
                steps.settle()
                steps.done(eng.tensor_scalar(small[:, 5, :], small[:, 4, :], -1.0, 1.0, ALU.mult, ALU.add))
                steps.done(eng.tensor_scalar(small[:, 3, :], small[:, 4, :], 1.0 / DH ** 0.5, None, ALU.mult))
                steps.settle()
                steps.done(eng.tensor_tensor(small[:, 5, :], small[:, 5, :], small[:, 2, :], ALU.mult))
                steps.done(eng.tensor_tensor(dot[:, :, :], dot[:, :, :], bc(small[:, 3, :].unsqueeze(1), every), ALU.mult))
                steps.settle()
                eng.wait_ge(act, 4)
                steps.done(eng.tensor_tensor(far[:, :, :], bc(dist2[:, :].unsqueeze(2), every), bc(small[:, 5, :].unsqueeze(1), every), ALU.mult))
                steps.settle()
                steps.done(eng.tensor_tensor(dot[:, :, :], dot[:, :, :], far[:, :, :], ALU.subtract))
                steps.settle()
                steps.done(eng.tensor_tensor(dot[:, :, :], dot[:, :, :], dec[:, :, :], ALU.mult))


def segment_softmax(net, dot):
    nc, dram = net.nc, net.dram
    n = net.scope("sm_")
    last = CE - 1
    with n:
        lt = n.sb("lt", [P, CE])
        pen = n.sb("pen", [P, CE + 1])
        run = n.sb("run", [P, CE])
        best = n.sb("best", [P, CE])
        stage = n.sb("stage", [P, K4, P])
        edge_dst = n.sb("edge_dst", [P, 2])
        pair = n.sb("pair", [P, 2])
        carry = n.sb("carry", [H, 3, CH])
        start = n.sb("start", [P, 1])
        turned = n.ps("turned", [P, K4, P])
        loaded, staged, turned_s, placed, marks, dve = (n.sem(s) for s in ("loaded", "staged", "turned_s", "placed", "marks", "dve"))
        cells = net.table("cells", (2, P, 2))
        carried = net.table("carried", (2, CH, H))
        chunks = net.dst_rows.rearrange("(c e) -> c e", c=CH)
        view = dot[:, :, :].rearrange("p (c j k) h -> p c j k h", c=CH, k=K4)
        with nc.Block() as block:
            @block.gpsimd
            def _(eng):
                eng.memset(edge_dst[:, :], -1.0).then_inc(marks, 1)

            @block.sync
            def _(eng):
                for c in range(CH):
                    eng.dma_start(best[c * H:(c + 1) * H, :], bc(chunks[c:c + 1, :], [H, CE])).then_inc(loaded, 16)
                eng.wait_ge(marks, 1)
                for c in range(1, CH):
                    eng.dma_start(edge_dst[c * H:(c + 1) * H, 0:1], bc(chunks[c - 1:c, last:CE], [H, 1])).then_inc(loaded, 16)
                for c in range(CH - 1):
                    eng.dma_start(edge_dst[c * H:(c + 1) * H, 1:2], bc(chunks[c + 1:c + 2, 0:1], [H, 1])).then_inc(loaded, 16)
                eng.wait_ge(loaded, 16 * (3 * CH - 2))

            @block.vector
            def _(eng):
                for j in turns(eng, CU):
                    eng.wait_ge(turned_s, j)
                    mark(eng, staged)
                    for k in range(K4):
                        eng.tensor_copy(stage[:, k, :].rearrange("p (c a h) -> p c a h", a=1, h=H),
                                        view[:, :, bass.ds(j, 1), k, :]).then_inc(staged, 1)
                    eng.wait_ge(turned_s, j + 1)
                    mark(eng, placed)
                    eng.tensor_copy(lt[:, bass.ds(j * UNIT, UNIT)].rearrange("p (q k) -> p k q", k=K4), turned[:, :, :]).then_inc(placed, 1)

            @block.tensor
            def _(eng):
                for j in turns(eng, CU):
                    eng.wait_ge(placed, j * 2)
                    eng.wait_ge(staged, j * 5 + 5)
                    for k in range(K4):
                        mm = eng.transpose(turned[:, k, :], stage[:, k, :], net.ident[:, :])
                    mm.then_inc(turned_s, 1)

        with nc.Block() as block:
            @block.vector
            def _(eng):
                steps = Steps(eng, dve)
                d = best
                steps.done(eng.tensor_tensor(pen[:, 1:CE], d[:, 1:CE], d[:, 0:CE - 1], ALU.not_equal))
                steps.done(eng.tensor_tensor(pen[:, 0:1], d[:, 0:1], edge_dst[:, 0:1], ALU.not_equal))
                steps.done(eng.tensor_tensor(pen[:, CE:CE + 1], d[:, last:CE], edge_dst[:, 1:2], ALU.not_equal))
                steps.done(eng.tensor_tensor(start[:, :], d[:, 0:1], d[:, last:CE], ALU.not_equal))
                steps.settle()
                steps.done(eng.tensor_scalar(pen[:, :], pen[:, :], -BIG, None, ALU.mult))
                steps.done(eng.tensor_scalar(start[:, :], start[:, :], -BIG, None, ALU.mult))
                steps.settle()
                steps.done(eng.tensor_tensor_scan(run[:, :], pen[:, 0:CE], lt[:, :], -BIG, ALU.add, ALU.max))
                steps.done(eng.tensor_tensor(pair[:, 0:1], start[:, :], pen[:, 0:1], ALU.add))
                steps.settle()
                steps.done(eng.tensor_copy(pair[:, 1:2], run[:, last:CE]))

        def carry_over(name, at, backward):
            wrote, scanned = n.sem(name + "wrote"), n.sem(name + "scanned")
            with nc.Block() as block:
                @block.sync
                def _(eng):
                    eng.dma_start(cells[at], pair[:, :]).then_inc(wrote, 16)
                    eng.wait_ge(wrote, 16)
                    for w in range(2):
                        eng.dma_start(carry[:, w, :], cells[at, :, w:w + 1].rearrange("(c h) o -> h (c o)", h=H), allow_slow_non_contiguous=True).then_inc(wrote, 16)
                    eng.wait_ge(scanned, 2)
                    eng.dma_start(carried[at].rearrange("c h -> h c"), carry[:, 2, :], allow_slow_non_contiguous=True).then_inc(wrote, 16)
                    eng.wait_ge(wrote, 64)
                    lo, hi = (0, P - H) if backward else (H, P)
                    rows = carried[at].rearrange("c h -> (c h)").rearrange("(p o) -> p o", o=1)
                    eng.dma_start(start[lo:hi, :], rows[H:P, :] if backward else rows[0:P - H, :]).then_inc(wrote, 16)
                    eng.wait_ge(wrote, 80)

                @block.vector
                def _(eng):
                    eng.memset(start[:, :], -BIG).then_inc(scanned, 1)
                    eng.wait_ge(wrote, 48)
                    s = slice(None, None, -1) if backward else slice(None)
                    eng.tensor_tensor_scan(carry[:, 2, s], carry[:, 0, s], carry[:, 1, s], -BIG, ALU.add, ALU.max).then_inc(scanned, 1)

        carry_over("f_", 0, False)
        dve2 = n.sem("dve2")
        with nc.Block() as block:
            @block.vector
            def _(eng):
                steps = Steps(eng, dve2)
                steps.done(eng.tensor_tensor_scan(run[:, :], pen[:, 0:CE], lt[:, :], start[:, 0:1], ALU.add, ALU.max))
                steps.settle()
                steps.done(eng.tensor_tensor_scan(best[:, ::-1], pen[:, 1:CE + 1][:, ::-1], run[:, ::-1], -BIG, ALU.add, ALU.max))
                steps.done(eng.tensor_tensor(pair[:, 0:1], pair[:, 0:1], pen[:, 0:1], ALU.subtract))
                steps.settle()
                steps.done(eng.tensor_tensor(pair[:, 0:1], pair[:, 0:1], pen[:, CE:CE + 1], ALU.add))
                steps.done(eng.tensor_copy(pair[:, 1:2], best[:, 0:1]))
        carry_over("b_", 1, True)
        dve3, act = n.sem("dve3"), n.sem("act")
        with nc.Block() as block:
            @block.vector
            def _(eng):
                steps = Steps(eng, dve3)
                steps.done(eng.tensor_tensor_scan(best[:, ::-1], pen[:, 1:CE + 1][:, ::-1], run[:, ::-1], start[:, 0:1], ALU.add, ALU.max))
                steps.settle()
                steps.done(eng.tensor_tensor(lt[:, :], lt[:, :], best[:, :], ALU.subtract))

            @block.scalar
            def _(eng):
                eng.wait_ge(dve3, 2)
                eng.activation(lt[:, :], lt[:, :], ACT.Exp).then_inc(act, 1)

        staged, turned_s, placed = n.sem("staged2"), n.sem("turned2"), n.sem("placed2")
        with nc.Block() as block:
            @block.vector
            def _(eng):
                for j in turns(eng, CU):
                    eng.wait_ge(turned_s, j)
                    mark(eng, staged)
                    eng.tensor_copy(stage[:, :, :], lt[:, bass.ds(j * UNIT, UNIT)].rearrange("p (q k) -> p k q", k=K4)).then_inc(staged, 1)
                    eng.wait_ge(turned_s, j + 1)
                    mark(eng, placed)
                    for k in range(K4):
                        eng.tensor_copy(view[:, :, bass.ds(j, 1), k, :],
                                        turned[:, k, :].rearrange("p (c a h) -> p c a h", a=1, h=H)).then_inc(placed, 1)

            @block.tensor
            def _(eng):
                for j in turns(eng, CU):
                    eng.wait_ge(placed, j * 5)
                    eng.wait_ge(staged, j * 2 + 2)
                    for k in range(K4):
                        mm = eng.transpose(turned[:, k, :], stage[:, k, :], net.ident[:, :])
                    mm.then_inc(turned_s, 1)


def edges_weighted(net, ex, v_rows, acc, acc_z):
    nc = net.nc
    n = net.scope("l4_")
    with n:
        base, dst = n.sb("base", [P, R]), n.sb("dst", [P, R, K4])
        v = n.sb("v", [P, R, K4, D])
        hot = n.sb("hot", [P, R, K4, P])
        e = n.sb("e", [P, R, K4, 2, H])
        sums = [n.ps(f"sums{b}", [P, P]) for b in range(R)]
        zs = [n.ps(f"zs{b}", [2 * H, P]) for b in range(R)]
        out, out_z = n.sb("out", [P, R, P]), n.sb("out_z", [2 * H, R, P])
        base_in, v_in, hot_in, e_in, ready, summed, sums_out, added = (n.sems(x, R) for x in (
            "base_in", "v_in", "hot_in", "e_in", "ready", "summed", "sums_out", "added"))
        marks = net.marks
        with nc.Block() as block:
            @block.sync
            def _(eng):
                regs = visit_registers(net, eng)
                for i in turns(eng, turn_count(net, eng)):
                    visit = look_up(net, eng, regs, i)
                    for b in range(R):
                        visit_loads(net, eng, i, b, visit[b][0], dst, base, base_in, hot_in)
                        eng.wait_ge(summed[b], i)
                        mark(eng, marks)
                        eng.dma_start(v[:, b], v_rows[bass.ds(visit[b][0] * UNIT, UNIT), :].rearrange(
                            "(p k) d -> p k d", k=K4)).then_inc(v_in[b], 16)

            @block.vector
            def _(eng):
                def build(i, b):
                    eng.wait_ge(base_in[b], i * 32 + 32)
                    eng.wait_ge(summed[b], i)
                    hot_here(net, eng, hot, dst, base, b).then_inc(hot_in[b], 1)

                def weigh(i, b, unit):
                    u4 = bass.ds(unit * K4, K4)
                    eng.wait_ge(summed[b], i)
                    mark(eng, marks)
                    eng.tensor_tensor(e[:, b, :, 1, :], ex[:, u4, :], bc(net.type_f[:, u4].unsqueeze(2), [P, K4, H]), ALU.mult).then_inc(e_in[b], 1)
                    eng.wait_ge(v_in[b], i * 16 + 16)
                    eng.tensor_tensor(v[:, b].rearrange("p k (h c) -> p k h c", h=H),
                                      v[:, b].rearrange("p k (h c) -> p k h c", h=H),
                                      bc(ex[:, u4, :].unsqueeze(3), [P, K4, H, DH]), ALU.mult).then_inc(ready[b], 1)
                    eng.wait_ge(e_in[b], i * 2 + 1)
                    eng.tensor_tensor(e[:, b, :, 0, :], ex[:, u4, :], e[:, b, :, 1, :], ALU.subtract).then_inc(e_in[b], 1)

                regs = visit_registers(net, eng)
                for b in range(3):
                    build(0, b)
                for i, final in rolling(eng, last_turn(net, eng)):
                    visit = look_up(net, eng, regs, i)
                    for b in range(R):
                        weigh(i, b, visit[b][0])
                        for visit_later in later(i, b, 3, final):
                            build(*visit_later)
                    mark(eng, marks)

            @block.gpsimd
            def _(eng):
                regs = visit_registers(net, eng)
                for i in turns(eng, turn_count(net, eng)):
                    visit = look_up(net, eng, regs, i)
                    for b in range(R):
                        eng.wait_ge(sums_out[b], i * 2 + 2)
                        add_window(net, eng, i, b, visit[b][1], [(acc, out[:, b, :]), (acc_z, out_z[:, b, :])], added)

            @block.scalar
            def _(eng):
                for i in turns(eng, turn_count(net, eng)):
                    for b in range(R):
                        eng.wait_ge(summed[b], i + 1)
                        eng.wait_ge(added[b], i * 2)
                        eng.activation(out[:, b, :], sums[b][:, :], ACT.Copy).then_inc(sums_out[b], 1)
                        eng.activation(out_z[:, b, :], zs[b][:, :], ACT.Copy).then_inc(sums_out[b], 1)

            @block.tensor
            def _(eng):
                for i in turns(eng, turn_count(net, eng)):
                    for b in range(R):
                        eng.wait_ge(hot_in[b], i + 1)
                        eng.wait_ge(sums_out[b], i * 2)
                        eng.wait_ge(ready[b], i + 1)
                        mark(eng, marks)
                        for k in range(K4):
                            mm = eng.matmul(sums[b][:, :], v[:, b, k, :], hot[:, b, k, :], start=(k == 0), stop=(k == K4 - 1))
                        eng.wait_ge(e_in[b], i * 2 + 2)
                        mark(eng, marks)
                        for k in range(K4):
                            mm = eng.matmul(zs[b][:, :], e[:, b, k, :, :].rearrange("p t h -> p (t h)"), hot[:, b, k, :], start=(k == 0), stop=(k == K4 - 1))
                        mm.then_inc(summed[b], 1)


def nodes_relational(net, acc, acc_z, x_row, out):
    nc, dram = net.nc, net.dram
    n = net.scope("n3_")
    A = 6 + 2 + LN_STEPS + 2
    B = 1 + 2 + LN_STEPS + 2 + 1
    PER = A + B + LN_STEPS
    with n:
        wo, wf1, wf2 = n.sb("wo", [D, D]), n.sb("wf1", [D, 4, P]), n.sb("wf2", [P, 4, D])
        rows = n.sb("rows", [P, 6, D])
        bf1 = n.sb("bf1", [P, 4])
        z = n.sb("z", [2 * H, GC])
        rel_v = n.sb("rel_v", [2 * H, D])
        recip = n.sb("recip", [P, GC])
        agg, x4t, h = n.sb("agg", [P, GC]), n.sb("x4t", [P, GC]), n.sb("h", [P, 4, GC])
        y, x4 = n.sb("y", [P, 4, D]), n.sb("x4", [P, 4, D])
        stats, moments, std = n.sb("stats", [P, 4, 6]), n.sb("moments", [P, 4, 2]), n.sb("std", [P, 4])
        pz, pr, po, pt = n.ps("pz", [P, GC]), n.ps("pr", [P, GC]), n.ps("po", [P, 4, D]), n.ps("pt", [P, GC])
        pf = [n.ps(f"pf{f}", [P, GC]) for f in range(4)]
        masked = n.sem("masked")
        loaded, dve, spread, made, turned, hid, gelu, fed, rooted, marks, stored = (n.sem(s) for s in (
            "loaded", "dve", "spread", "made", "turned", "hid", "gelu", "fed", "rooted", "marks", "stored"))
        NL = 6 + 3 + 4 + 2
        row = lambda c: bc(rows[:, c, :].unsqueeze(1), [P, 4, D])
        with nc.Block() as block:
            @block.sync
            def _(eng):
                eng.dma_start(wo[:, :], dram["L3_gnn_Wo"]).then_inc(loaded, 16)
                eng.dma_start(wf1[:, :, :], dram["L3_gnn_Wf1"].rearrange("d (f o) -> d f o", f=4)).then_inc(loaded, 16)
                eng.dma_start(wf2[:, :, :], dram["L3_gnn_Wf2"].rearrange("(f o) d -> o f d", f=4)).then_inc(loaded, 16)
                for f in range(4):
                    eng.dma_start(bf1[:, f:f + 1], cols(dram["L3_gnn_bf1"][f * P:(f + 1) * P])).then_inc(loaded, 16)
                for c, name in enumerate(("bo", "g1", "be1", "g2", "be2", "bf2")):
                    eng.dma_start(rows[:, c, :], everywhere(dram["L3_gnn_" + name], D)).then_inc(loaded, 16)
                for t in range(2):
                    eng.dma_start(rel_v[t * H:(t + 1) * H, :], bc(dram["L3_gnn_rel_v"][t:t + 1, :], [H, D])).then_inc(loaded, 16)
                eng.wait_ge(dve, NG * PER)
                full = N // P
                eng.dma_start(out[0:full * P, :].rearrange("(t p) d -> p t d", p=P), x_row[:, 0:full, :]).then_inc(stored, 16)
                eng.dma_start(out[full * P:N, :], x_row[0:N - full * P, full, :]).then_inc(stored, 16)
                eng.wait_ge(stored, 32)

            @block.vector
            def _(eng):
                eng.wait_ge(loaded, 16 * NL)
                eng.tensor_tensor(rel_v[:, :], rel_v[:, :], net.expand[:, :], ALU.mult).then_inc(masked, 1)
                for g in turns(eng, NG):
                    steps = Steps(eng, dve, g, PER)
                    mine = x_row[:, bass.ds(g * 4, 4), :]
                    steps.done(eng.tensor_copy(z[:, :], acc_z[:, bass.ds(g * GC, GC)]))
                    eng.wait_ge(spread, g + 1)
                    steps.done(eng.tensor_scalar(recip[:, :], pz[:, :], 1e-30, None, ALU.max))
                    steps.settle()
                    steps.done(eng.reciprocal(recip[:, :], recip[:, :]))
                    steps.done(eng.tensor_copy(agg[:, :], acc[:, bass.ds(g * GC, GC)]))
                    steps.settle()
                    steps.done(eng.tensor_tensor(agg[:, :], agg[:, :], pr[:, :], ALU.add))
                    steps.settle()
                    steps.done(eng.tensor_tensor(agg[:, :], agg[:, :], recip[:, :], ALU.mult))
                    eng.wait_ge(made, g + 1)
                    steps.done(eng.tensor_tensor(y[:, :, :], po[:, :, :], row(0), ALU.add))
                    steps.settle()
                    steps.done(eng.tensor_tensor(y[:, :, :], y[:, :, :], mine, ALU.add))
                    steps.settle()
                    layer_norm(eng, steps, y, stats, moments, std, x4, marks, rooted, g * 3 + 1, 1e-5)
                    steps.done(eng.tensor_tensor(x4[:, :, :], x4[:, :, :], row(1), ALU.mult))
                    steps.settle()
                    steps.done(eng.tensor_tensor(x4[:, :, :], x4[:, :, :], row(2), ALU.add))
                    steps.settle()
                    eng.wait_ge(turned, g + 1)
                    steps.done(eng.tensor_copy(x4t[:, :], pt[:, :]))
                    eng.wait_ge(fed, g + 1)
                    steps.done(eng.tensor_tensor(y[:, :, :], po[:, :, :], row(5), ALU.add))
                    steps.settle()
                    steps.done(eng.tensor_tensor(y[:, :, :], y[:, :, :], x4[:, :, :], ALU.add))
                    steps.settle()
                    layer_norm(eng, steps, y, stats, moments, std, x4, marks, rooted, g * 3 + 2, 1e-5)
                    steps.done(eng.tensor_tensor(x4[:, :, :], x4[:, :, :], row(3), ALU.mult))
                    steps.settle()
                    steps.done(eng.tensor_tensor(x4[:, :, :], x4[:, :, :], row(4), ALU.add))
                    steps.settle()
                    steps.done(eng.tensor_tensor(y[:, :, :], x4[:, :, :], mine, ALU.add))
                    steps.settle()
                    layer_norm(eng, steps, y, stats, moments, std, mine, marks, rooted, g * 3 + 3, 1e-5)
                    steps.end()

            @block.scalar
            def _(eng):
                for g in turns(eng, NG):
                    eng.wait_ge(dve, g * PER + 8 + 9)
                    eng.activation(std[:, :], std[:, :], ACT.Sqrt).then_inc(rooted, 1)
                    for f in range(4):
                        eng.wait_ge(hid, g * 4 + f + 1)
                        eng.activation(h[:, f, :], pf[f][:, :], ACT.Gelu, bias=bf1[:, f:f + 1]).then_inc(gelu, 1)
                    eng.wait_ge(dve, g * PER + A + 3 + 9)
                    eng.activation(std[:, :], std[:, :], ACT.Sqrt).then_inc(rooted, 1)
                    eng.wait_ge(dve, g * PER + A + B + 9)
                    eng.activation(std[:, :], std[:, :], ACT.Sqrt).then_inc(rooted, 1)

            @block.tensor
            def _(eng):
                eng.wait_ge(masked, 1)
                for g in turns(eng, NG):
                    eng.wait_ge(dve, g * PER + 1)
                    eng.matmul(pz[:, :], net.expand[:, :], z[:, :], start=True, stop=True)
                    eng.matmul(pr[:, :], rel_v[:, :], z[:, :], start=True, stop=True).then_inc(spread, 1)
                    eng.wait_ge(dve, g * PER + 6)
                    for j in range(4):
                        mm = eng.matmul(po[:, j, :], agg[:, j * P:(j + 1) * P], wo[:, :], start=True, stop=True)
                    mm.then_inc(made, 1)
                    eng.wait_ge(dve, g * PER + A)
                    for j in range(4):
                        mm = eng.transpose(pt[:, j * P:(j + 1) * P], x4[:, j, :], net.ident[:, :])
                    mm.then_inc(turned, 1)
                    eng.wait_ge(dve, g * PER + A + 1)
                    for f in range(4):
                        eng.matmul(pf[f][:, :], wf1[:, f, :], x4t[:, :], start=True, stop=True).then_inc(hid, 1)
                    eng.wait_ge(gelu, g * 4 + 4)
                    for j in range(4):
                        for f in range(4):
                            mm = eng.matmul(po[:, j, :], h[:, f, j * P:(j + 1) * P], wf2[:, f, :], start=(f == 0), stop=(f == 3))
                    mm.then_inc(fed, 1)


def load_rows(net, x_row):
    n = net.scope("ld_")
    with n:
        loaded = n.sem("loaded")
        with net.nc.Block() as block:
            @block.sync
            def _(eng):
                eng.dma_start(x_row[:, :, :], net.dram["x"].rearrange("(t p) d -> p t d", p=P)).then_inc(loaded, 16)
                eng.wait_ge(loaded, 16)


def graph_network(nc, dram, out):
    net = Net(nc, ExitStack(), dram)
    with net:
        net.marks = net.lasting.enter_context(nc.semaphore("marks"))
        setup(net)
        x_row = net.sb("x_row", [P, NT, D])
        load_rows(net, x_row)
        hs, x1 = net.table("hs", (NP, D)), net.table("x1", (NP, D))
        x1_parts, q_parts = net.table("x1_parts", (NP, 3 * D), BF16), net.table("q_parts", (NP, 3 * D), BF16)
        tabs = [net.table(f"tab{k}", (TR, D)) for k in range(K4)]
        kv, kvm = net.table("kv", (NP, 2 * D)), net.table("kvm", (NP, 3 * D))
        qm_parts = net.table("qm_parts", (NP, 3 * 2 * D), BF16)
        v_rows = net.table("v_rows", (EP, D))
        clear_tables(net, tabs)

        layer = net.scope("a_")
        with layer:
            acc, hs_row = layer.sb("acc", [P, NP]), layer.sb("hs_row", [P, NT, D])
            clear(net, "c0_", [acc])
            project(net, "p0_", ["L0_gnn_W"], [(hs, 0, D, 0)], x_row, scale=net.dinv, keep=hs_row)
            edges_gcn(net, hs, acc)
            nodes_gcn(net, acc, hs_row, x_row, x1, x1_parts)

        layer = net.scope("b_")
        with layer:
            acc = layer.sb("acc", [P, NP])
            clear(net, "c1_", [acc])
            edges_gated(net, x1, x1_parts, acc, tabs)
            nodes_gated(net, acc, tabs, x_row)

        layer = net.scope("c_")
        with layer:
            acc, acc_z, x_T = layer.sb("acc", [P, NP]), layer.sb("acc_z", [H, NP]), layer.sb("x_T", [P, NP])
            clear(net, "c2_", [acc, acc_z])
            project(net, "p2_", ["L2_gnn_Wk", "L2_gnn_Wv", "L2_gnn_Wq"], [(kv, 0, 2 * D, 0)], x_row, x_T=x_T, parts=q_parts)
            edges_attention(net, kv, q_parts, acc, acc_z)
            nodes_attention(net, acc, acc_z, x_row, x_T)

        project(net, "p3_", ["L3_gnn_Wk", "L3_gnn_Wv", "L3_gnn_Wq"], [(kvm, 0, 2 * D, 0)], x_row, parts=qm_parts)
        hyperbolic(net, x_row, kvm, qm_parts)
        layer = net.scope("d_")
        with layer:
            dot, dist2 = layer.sb("dot", [P, NU * K4, H]), layer.sb("dist2", [P, NU * K4])
            first = net.scope("e_")
            with first:
                dec = first.sb("dec", [P, NU * K4, H])
                edges_relational(net, kvm, qm_parts, dot, dec, dist2, v_rows)
                logits(net, dot, dec, dist2)
            segment_softmax(net, dot)
            acc, acc_z = layer.sb("acc", [P, NP]), layer.sb("acc_z", [2 * H, NP])
            clear(net, "c3_", [acc, acc_z])
            edges_weighted(net, dot, v_rows, acc, acc_z)
            nodes_relational(net, acc, acc_z, x_row, out)


def kernel(**inputs):
    import concourse.bacc as bacc
    from concourse.bass_utils import run_bass_kernel_spmd

    a = {k: np.asarray(v) for k, v in inputs.items()}
    tail = EP - E
    tiled = lambda v: np.ascontiguousarray(v.reshape(NU, P, K4).transpose(1, 0, 2).reshape(P, NU * K4))
    by_tile = lambda v: np.ascontiguousarray(v.reshape(NU, P, K4, -1).transpose(3, 0, 2, 1).reshape(-1, EP))
    src = np.pad(a["src"], (0, tail), constant_values=N)
    dst = np.pad(a["dst"], (0, tail), constant_values=N)
    te = by_tile(np.pad(a["edge_attr_32"], ((0, tail), (0, 0))))
    types = np.pad(a["edge_type_2"], (0, tail))
    arrays = {
        "x": np.pad(a["x"], ((0, NP - N), (0, 0))),
        "src_row": src, "dst_row": dst, "src_tiles": tiled(src), "dst_tiles": tiled(dst),
        "type_tiles": tiled(types), "type_row": by_tile(types)[0], "weight_row": by_tile(np.pad(a["edge_weight"], (0, tail)))[0],
        "ea": np.pad(a["edge_attr_128"], ((0, tail), (0, 0))),
        "te": np.concatenate([te, np.ones((1, EP), np.float32)]),
        "one": np.ones((1,), np.float32),
    }
    for name, shape in WEIGHTS.items():
        arrays[name] = a[name].reshape(shape)
    nc = bacc.Bacc("TRN2", target_bir_lowering=False, num_devices=1)
    dram = {k: nc.dram_tensor(f"in_{k}", v.shape, mybir.dt.from_np(v.dtype), kind="ExternalInput").ap() for k, v in arrays.items()}
    out = nc.dram_tensor("out", (N, D), F32, kind="ExternalOutput").ap()
    graph_network(nc, dram, out)
    r = run_bass_kernel_spmd(nc, [{f"in_{k}": v for k, v in arrays.items()}], core_ids=[0])
    return r.results[0]["out"]
```

```python
from contextlib import ExitStack

import numpy as np
import concourse.bass as bass
from concourse import mybir

P = 128
D = 128
N = 6250
E = 106250
H = 8
DH = D // H
K4 = 4
UNIT = P * K4
NU = 208
EP = NU * UNIT
NT = 52
NG = NT // 4
GC = 512
NP = NT * P
TR = NP + P
R = 4
VMAX = (NU * ((N + P - 1) // P) // P + 1) * P
LASTN = N - (NG - 1) * GC
CH = 16
CU = NU // CH
CE = CU * UNIT
TE = 35
TB = 15
WB = 12
HID = 64
BIG = 1e30

ALU = mybir.AluOpType
ACT = mybir.ActivationFunctionType
AX = mybir.AxisListType.X
F32 = mybir.dt.float32
BF16 = mybir.dt.bfloat16
I32 = mybir.dt.int32

WEIGHTS = {
    "L0_gnn_W": (D, D), "L0_gnn_b": (D,),
    "L2_gnn_Wq": (D, D), "L2_gnn_Wk": (D, D), "L2_gnn_Wv": (D, D), "L2_gnn_Wo": (D, D), "L2_gnn_bo": (D,),
    "L2_gnn_W1": (D, 256), "L2_gnn_b1": (256,), "L2_gnn_W2": (256, D), "L2_gnn_b2": (D,),
    "L2_gnn_bn1_g": (D,), "L2_gnn_bn1_b": (D,), "L2_gnn_bn2_g": (D,), "L2_gnn_bn2_b": (D,),
    "L3_gnn_Wq": (D, D), "L3_gnn_Wk": (D, D), "L3_gnn_Wv": (D, D),
    "L3_gnn_rel_q": (2, D), "L3_gnn_rel_k": (2, D), "L3_gnn_rel_v": (2, D),
    "L3_gnn_Wt": (32, D), "L3_gnn_bt": (D,), "L3_gnn_Wd1": (2, HID), "L3_gnn_bd1": (HID,),
    "L3_gnn_Wd2": (HID, H), "L3_gnn_bd2": (H,), "L3_gnn_decay_scale": (H,), "L3_gnn_c_mag": (1,),
    "L3_gnn_hyp_beta": (H,), "L3_gnn_logit_alpha": (H,), "L3_gnn_Wo": (D, D), "L3_gnn_bo": (D,),
    "L3_gnn_g1": (D,), "L3_gnn_be1": (D,), "L3_gnn_g2": (D,), "L3_gnn_be2": (D,),
    "L3_gnn_Wf1": (D, 512), "L3_gnn_bf1": (512,), "L3_gnn_Wf2": (512, D), "L3_gnn_bf2": (D,),
}


class Steps:

    def __init__(self, eng, sem, turn=0, per=0):
        self.eng, self.sem, self.start, self.n, self.per = eng, sem, turn * per, 0, per

    def done(self, ins):
        ins.then_inc(self.sem, 1)
        self.n += 1

    def settle(self):
        self.eng.wait_ge(self.sem, self.start + self.n)

    def end(self):
        assert not self.per or self.n == self.per, (self.n, self.per)


def turns(eng, n):
    yield 0
    with eng.Fori(1, n) as i:
        yield i


def rolling(eng, last):
    yield 0, False
    with eng.Fori(1, last) as i:
        yield i, False
    yield last, True


def groups(eng):
    for i in turns(eng, NG // 2):
        yield i, 0, i * 2
        yield i, 1, i * 2 + 1
    yield NG // 2, 0, NG - 1


def groups_ahead(eng):
    for i in turns(eng, NG // 2):
        yield i, 0, i * 2, [(i, 1, i * 2 + 1)]
        yield i, 1, i * 2 + 1, [(i + 1, 0, i * 2 + 2)]
    yield NG // 2, 0, NG - 1, []


def later(i, b, k, final):
    return [] if final and b + k >= R else [(i + (b + k) // R, (b + k) % R)]


def bc(ap, shape):
    return ap.broadcast_to(shape)


def cols(vec):
    return vec.rearrange("(p o) -> p o", o=1)


def everywhere(vec, n):
    return bc(vec.rearrange("(o n) -> o n", o=1), [P, n])


class Net:
    def __init__(self, nc, stack, dram):
        self.nc, self.stack, self.dram = nc, stack, dram
        self.phase = ""
        self.lasting = stack
        self.semaphores = []
        self.registers = {}

    def scope(self, name):
        scope = Net(self.nc, ExitStack(), self.dram)
        scope.lasting = self.lasting
        scope.phase = name
        scope.semaphores = []
        return scope

    def sb(self, name, shape, dt=F32):
        return self.stack.enter_context(self.nc.sbuf_tensor(f"{self.phase}{name}", shape, dt))

    def ps(self, name, shape, dt=F32):
        return self.stack.enter_context(self.nc.psum_tensor(f"{self.phase}{name}", shape, dt))

    def sem(self, name):
        self.semaphores.append(self.stack.enter_context(self.nc.semaphore(f"{self.phase}{name}")))
        return self.semaphores[-1]

    def __enter__(self):
        return self

    def __exit__(self, *error):
        if error[0] is None and self.semaphores:
            with self.nc.Block() as block:
                @block.gpsimd
                def _(eng):
                    for s in self.semaphores:
                        eng.sem_clear(s)
        self.stack.close()

    def gather_sems(self, name, n):
        return [self.lasting.enter_context(self.nc.semaphore(f"{self.phase}{name}{i}")) for i in range(n)]

    def sems(self, name, n):
        return [self.sem(f"{name}{i}") for i in range(n)]

    def table(self, name, shape, dt=F32):
        return self.nc.dram_tensor(name, shape, dt, kind="Internal").ap()


def layer_norm(eng, steps, y, stats, moments, std, out, sqrt_in, sqrt_done, sqrt_count, eps):
    for j in range(4):
        steps.done(eng.bn_stats(stats[:, j, :], y[:, j, :]))
    steps.settle()
    mark(eng, sqrt_in)
    for j in range(4):
        steps.done(eng.bn_aggr(moments[:, j, :], stats[:, j, :]))
    steps.settle()
    steps.done(eng.tensor_scalar(std[:, :], moments[:, :, 1], eps, None, ALU.add))
    steps.settle()
    mark(eng, sqrt_in)
    eng.wait_ge(sqrt_done, sqrt_count)
    mark(eng, sqrt_in)
    steps.done(eng.reciprocal(std[:, :], std[:, :]))
    steps.settle()
    for j in range(4):
        steps.done(eng.tensor_scalar(out[:, j, :], y[:, j, :], moments[:, j, 0:1], std[:, j:j + 1],
                                     ALU.subtract, ALU.mult))
    steps.settle()


def split(eng, steps, x, hi, mid, lo):
    steps.done(eng.tensor_copy(hi, x))
    steps.settle()
    steps.done(eng.tensor_tensor(x, x, hi, ALU.subtract))
    steps.settle()
    steps.done(eng.tensor_copy(mid, x))
    steps.settle()
    steps.done(eng.tensor_tensor(x, x, mid, ALU.subtract))
    steps.settle()
    steps.done(eng.tensor_copy(lo, x))


def split_of(eng, steps, x, rest, hi, mid, lo, marks):
    steps.done(eng.tensor_copy(hi, x))
    steps.settle()
    mark(eng, marks)
    steps.done(eng.tensor_tensor(rest, x, hi, ALU.subtract))
    steps.settle()
    mark(eng, marks)
    steps.done(eng.tensor_copy(mid, rest))
    steps.settle()
    steps.done(eng.tensor_tensor(rest, rest, mid, ALU.subtract))
    steps.settle()
    mark(eng, marks)
    steps.done(eng.tensor_copy(lo, rest))


SPLIT_STEPS = 5
LN_STEPS = 4 + 4 + 1 + 1 + 4


def mark(eng, sem):
    eng.sem_inc(sem, 1)


def setup(net, x_row, tabs):
    nc, dram = net.nc, net.dram
    net.ident = net.sb("ident", [P, P])
    net.ident_b = net.sb("ident_b", [P, P], BF16)
    net.iota = net.sb("iota", [P, P])
    net.lower = net.sb("lower", [P, P])
    net.spare = net.sb("spare", [P, 1])
    net.ones = net.sb("ones", [P, P])
    net.expand = net.sb("expand", [2 * H, P])
    net.dst_f = net.sb("dst_f", [P, NU * K4])
    net.src_f = net.sb("src_f", [P, NU * K4])
    net.type_f = net.sb("type_f", [P, NU * K4])
    net.last_i = net.sb("last_i", [1, 1], I32)
    net.type_scale = net.sb("type_scale", [P, 1])
    net.dinv = net.sb("dinv", [P, NT])
    net.dst_rows = net.table("dst_rows", (EP,))
    net.type_rows = net.table("type_rows", (2, EP))
    net.parts = net.table("parts", (TB, EP), BF16)
    net.visits = net.table("visits", (VMAX * 2,), I32)
    net.visit_base = net.table("visit_base", (VMAX,))
    net.dst_cols = net.table("dst_cols", (P, NU * K4))
    ends = net.table("ends", (2, NU))
    HU = NU // 2

    n = net.scope("s0_")
    with n:
        src_i = n.sb("src_i", [P, NU * K4], I32)
        dst_i = n.sb("dst_i", [P, NU * K4], I32)
        type_i = n.sb("type_i", [P, NU * K4], I32)
        rows_i = n.sb("rows_i", [HU, 2, UNIT], I32)
        rows_f = n.sb("rows_f", [HU, 2, UNIT])
        types_i = n.sb("types_i", [HU, 2, UNIT], I32)
        types_f = n.sb("types_f", [HU, 2, 2, UNIT])
        types_b = n.sb("types_b", [HU, 3, 2, UNIT], BF16)
        weight = n.sb("weight", [HU, 2, UNIT])
        weight_b = n.sb("weight_b", [HU, 3, 2, UNIT], BF16)
        least, most = n.sb("least", [HU, 2]), n.sb("most", [HU, 2])
        top = n.sb("top", [HU, 1])
        row = n.sb("row", [1, 8])
        sel = n.sb("sel", [1, 2, P])
        pm = n.ps("pm", [P, P])
        loaded, pool_built, written = n.sem("loaded"), n.sem("pool_built"), n.sem("written")
        dve, top_turned, scale_spread = n.sem("dve"), n.sem("top_turned"), n.sem("scale_spread")
        with nc.Block() as block:
            @block.sync
            def _(eng):
                eng.dma_start(src_i[:, :], dram["src_tiles"]).then_inc(loaded, 16)
                eng.dma_start(dst_i[:, :], dram["dst_tiles"]).then_inc(loaded, 16)
                eng.dma_start(type_i[:, :], dram["type_tiles"]).then_inc(loaded, 16)
                for to, of in ((rows_i, "dst_row"), (types_i, "type_row"), (weight, "weight_row")):
                    eng.dma_start(to[:, :, :], dram[of].rearrange("(p a e) -> p a e", a=2, e=UNIT)).then_inc(loaded, 16)
                eng.wait_ge(dve, 17)
                for c, ap in enumerate((least, most)):
                    eng.dma_start(ends[c].rearrange("(p a) -> p a", a=2), ap[:, :]).then_inc(written, 16)
                eng.dma_start(net.dst_rows.rearrange("(p a e) -> p a e", a=2, e=UNIT), rows_f[:, :, :]).then_inc(written, 16)
                for c in range(2):
                    eng.dma_start(net.type_rows[c].rearrange("(p a e) -> p a e", a=2, e=UNIT), types_f[:, c, :, :]).then_inc(written, 16)
                rows = [weight_b[:, c, :, :] for c in (0, 0, 0, 1, 1, 2)]
                rows += [types_b[:, c, :, :] for c in (2, 2, 2, 0, 0, 0, 1, 1, 1)]
                for c, ap in enumerate(rows):
                    eng.dma_start(net.parts[c].rearrange("(p a e) -> p a e", a=2, e=UNIT), ap).then_inc(written, 16)
                eng.dma_start(net.dst_cols, net.dst_f[:, :]).then_inc(written, 16)
                eng.wait_ge(written, 16 * (6 + TB))

            @block.gpsimd
            def _(eng):
                eng.memset(net.ident[:, :], 0.0).then_inc(pool_built, 1)
                eng.memset(net.lower[:, :], 1.0).then_inc(pool_built, 1)
                eng.memset(net.expand[:, :], 1.0).then_inc(pool_built, 1)
                eng.memset(net.ones[:, :], 1.0).then_inc(pool_built, 1)
                eng.memset(sel[:, 0, :], 0.0).then_inc(pool_built, 1)
                eng.memset(sel[:, 1, :], 1.0).then_inc(pool_built, 1)
                eng.iota(net.iota[:, :], pattern=[[1, P]], base=0, channel_multiplier=0,
                         allow_small_or_imprecise_dtypes=True).then_inc(pool_built, 1)
                eng.iota(net.spare[:, :], pattern=[[1, 1]], base=NP, channel_multiplier=1,
                         allow_small_or_imprecise_dtypes=True).then_inc(pool_built, 1)
                eng.wait_ge(pool_built, 8)
                eng.affine_select(out=net.ident[:, :], in_=net.ident[:, :], compare_op=ALU.not_equal, fill=1.0,
                                  base=0, pattern=[[-1, P]], channel_multiplier=1).then_inc(pool_built, 1)
                eng.affine_select(out=net.lower[:, :], in_=net.lower[:, :], compare_op=ALU.is_gt, fill=0.0,
                                  base=0, pattern=[[-1, P]], channel_multiplier=1).then_inc(pool_built, 1)
                eng.affine_select(out=net.expand[:, :], in_=net.expand[:, :], compare_op=ALU.is_ge, fill=0.0,
                                  base=0, pattern=[[1, P]], channel_multiplier=-DH).then_inc(pool_built, 1)
                eng.wait_ge(pool_built, 11)
                eng.affine_select(out=net.expand[:, :], in_=net.expand[:, :], compare_op=ALU.is_ge, fill=0.0,
                                  base=DH - 1, pattern=[[-1, P]], channel_multiplier=DH).then_inc(pool_built, 1)
                eng.memset(sel[:, 0, 2:3], 1.0).then_inc(pool_built, 1)
                eng.memset(sel[:, 1, 2:3], 0.0).then_inc(pool_built, 1)

            @block.vector
            def _(eng):
                eng.wait_ge(loaded, 96)
                steps = Steps(eng, dve)
                steps.done(eng.tensor_copy(net.src_f[:, :], src_i[:, :]))
                steps.done(eng.tensor_copy(net.dst_f[:, :], dst_i[:, :]))
                steps.done(eng.tensor_copy(net.type_f[:, :], type_i[:, :]))
                steps.done(eng.tensor_copy(rows_f[:, :, :], rows_i[:, :, :]))
                steps.done(eng.tensor_copy(types_f[:, 0, :, :], types_i[:, :, :]))
                steps.done(eng.memset(types_b[:, 2, :, :], 1.0))
                steps.settle()
                steps.done(eng.tensor_reduce(top[:, :], types_f[:, 0, :, :].rearrange("p a e -> p (a e)"), AX, ALU.max))
                steps.done(eng.tensor_scalar(types_f[:, 1, :, :], types_f[:, 0, :, :], -1.0, 1.0, ALU.mult, ALU.add))
                steps.done(eng.tensor_reduce(least[:, :], rows_f[:, :, :], AX, ALU.min))
                steps.done(eng.tensor_reduce(most[:, :], rows_f[:, :, :], AX, ALU.max))
                steps.settle()
                steps.done(eng.tensor_copy(types_b[:, 0:2, :, :], types_f[:, :, :, :]))
                split(eng, steps, weight[:, :, :], weight_b[:, 0], weight_b[:, 1], weight_b[:, 2])
                steps.done(eng.memset(row[:, 3:4], 0.0))
                steps.settle()
                assert steps.n == 17, steps.n
                eng.wait_ge(top_turned, 1)
                steps.done(eng.tensor_reduce(row[:, 0:1], pm[0:1, 0:HU], AX, ALU.max))
                steps.settle()
                steps.done(eng.tensor_scalar(row[:, 1:2], row[:, 0:1], 1.0, 1.0, ALU.add, ALU.max))
                steps.settle()
                steps.done(eng.reciprocal(row[:, 2:3], row[:, 1:2]))
                eng.wait_ge(scale_spread, 1)
                steps.done(eng.tensor_copy(net.type_scale[:, :], pm[:, 0:1]))
                eng.wait_ge(pool_built, 14)
                steps.done(eng.tensor_copy(net.ident_b[:, :], net.ident[:, :]))

            @block.tensor
            def _(eng):
                eng.wait_ge(pool_built, 14)
                eng.wait_ge(dve, 7)
                eng.transpose(pm[0:1, 0:HU], top[:, :], net.ident[0:HU, 0:HU]).then_inc(top_turned, 1)
                eng.wait_ge(dve, 20)
                eng.matmul(pm[:, 0:1], sel[:, 0, :], row[:, 2:3], start=True, stop=False)
                eng.matmul(pm[:, 0:1], sel[:, 1, :], net.ones[0:1, 0:1], start=False, stop=True).then_inc(scale_spread, 1)

    n = net.scope("s2_")
    with n:
        rows3 = n.sb("rows3", [1, 3, NU])
        end_f, end_i = n.sb("end_f", [1, 2, NU]), n.sb("end_i", [1, NU], I32)
        all3 = n.sb("all3", [P, 3, NU])
        v, ge, got, unit = n.sb("v", [P, 1]), n.sb("ge", [P, NU]), n.sb("got", [P, NU]), n.sb("unit", [P, 1])
        first, base, base0 = n.sb("first", [P, 1]), n.sb("base", [P, 1]), n.sb("base0", [P, 1])
        pair = n.sb("pair", [P, 2], I32)
        count = n.sb("count", [1, 2], I32)
        pb = n.ps("pb", [P, 3, GC])
        loaded, dve, spread, chunk, chunk_ready, written, marks = (n.sem(s) for s in (
            "loaded", "dve", "spread", "chunk", "chunk_ready", "written", "marks"))
        PER = 12
        with nc.Block() as block:
            @block.sync
            def _(eng):
                eng.dma_start(end_f[:, :, :], ends.rearrange("(o c) n -> o c n", o=1)).then_inc(loaded, 16)
                eng.dma_start(base0[:, :], everywhere(ends[0, 0:1], 1)).then_inc(loaded, 16)
                eng.dma_start(net.expand[H:2 * H, :], net.expand[0:H, :]).then_inc(loaded, 16)
                eng.wait_ge(loaded, 48)

            @block.vector
            def _(eng):
                eng.wait_ge(loaded, 48)
                steps = Steps(eng, dve)
                steps.done(eng.tensor_tensor(end_i[:, :], end_f[:, 1, :], end_f[:, 0, :], ALU.subtract))
                steps.settle()
                steps.done(eng.tensor_scalar(end_i[:, :], end_i[:, :], 7, None, ALU.logical_shift_right))
                steps.settle()
                steps.done(eng.tensor_scalar(rows3[:, 0, :], end_i[:, :], 1, None, ALU.add))
                steps.done(eng.memset(rows3[:, 2, :], 4.0 * NP))
                steps.settle()
                steps.done(eng.tensor_tensor(rows3[:, 2, 0:NU - 1], end_f[:, 0, 1:NU], end_f[:, 0, 0:NU - 1], ALU.subtract))
                steps.done(eng.tensor_tensor_scan(rows3[:, 1, :], rows3[:, 0, :], rows3[:, 0, :], 0.0, ALU.add, ALU.max))
                steps.settle()
                steps.done(eng.tensor_scalar(count[:, 0:1], rows3[:, 1, NU - 1:NU], -1.0, None, ALU.add))
                steps.done(eng.tensor_scalar(count[:, 1:2], rows3[:, 1, NU - 1:NU], float(P - 1 + R), None, ALU.add))
                steps.settle()
                steps.done(eng.tensor_scalar(net.last_i[:, :], count[:, 0:1], 2, None, ALU.logical_shift_right))
                steps.done(eng.tensor_scalar(count[:, 1:2], count[:, 1:2], 7, None, ALU.logical_shift_right))
                eng.wait_ge(spread, 1)
                steps.done(eng.tensor_copy(all3[:, :, :], pb[:, :, 0:NU]))
                steps.done(eng.tensor_scalar(v[:, :], net.spare[:, :], float(-NP), None, ALU.add))
                steps.settle()

            @block.tensor
            def _(eng):
                eng.wait_ge(dve, 8)
                for c in range(3):
                    mm = eng.matmul(pb[:, c, 0:NU], net.ones[0:1, :], rows3[:, c, :], start=True, stop=True)
                mm.then_inc(spread, 1)

        with nc.Block() as block:
            @block.sync
            def _(eng):
                rounds = eng.value_load(count[0:1, 1:2], min_val=2, max_val=VMAX // P)
                for c in turns(eng, rounds):
                    eng.wait_ge(chunk_ready, c + 1)
                    mark(eng, marks)
                    eng.dma_start(net.visits[bass.ds(c * (2 * P), 2 * P)].rearrange("(p a) -> p a", a=2), pair[:, :]).then_inc(written, 16)
                    eng.dma_start(net.visit_base[bass.ds(c * P, P)].rearrange("(p a) -> p a", a=1), base[:, :]).then_inc(written, 16)
                eng.wait_ge(written, rounds * 32)
                mark(eng, marks)

            @block.vector
            def _(eng):
                rounds = eng.value_load(count[0:1, 1:2], min_val=2, max_val=VMAX // P)
                for c in turns(eng, rounds):
                    steps = Steps(eng, chunk, c, PER)
                    steps.done(eng.tensor_scalar(ge[:, :], all3[:, 1, :], v[:, 0:1], None, ALU.is_le))
                    steps.settle()
                    steps.done(eng.tensor_reduce(unit[:, :], ge[:, :], AX, ALU.add))
                    steps.done(eng.tensor_tensor(got[:, :], ge[:, :], all3[:, 0, :], ALU.mult))
                    steps.settle()
                    steps.done(eng.tensor_reduce(first[:, :], got[:, :], AX, ALU.add))
                    steps.settle()
                    steps.done(eng.tensor_tensor(got[:, :], ge[:, :], all3[:, 2, :], ALU.mult))
                    steps.done(eng.tensor_tensor(first[:, :], v[:, :], first[:, :], ALU.subtract))
                    steps.settle()
                    eng.wait_ge(written, c * 32)
                    mark(eng, marks)
                    steps.done(eng.tensor_reduce(base[:, :], got[:, :], AX, ALU.add))
                    steps.settle()
                    steps.done(eng.tensor_tensor(base[:, :], base[:, :], base0[:, :], ALU.add))
                    steps.settle()
                    steps.done(eng.scalar_tensor_tensor(out=base[:, :], in0=first[:, :], scalar=float(P), in1=base[:, :],
                                                        op0=ALU.mult, op1=ALU.add))
                    steps.settle()
                    steps.done(eng.tensor_scalar(base[:, :], base[:, :], float(NP - P), None, ALU.min))
                    steps.done(eng.tensor_scalar(pair[:, 0:1], unit[:, :], float(NU - 1), None, ALU.min))
                    steps.settle()
                    eng.tensor_copy(pair[:, 1:2], base[:, :]).then_inc(chunk_ready, 1)
                    steps.done(eng.tensor_scalar(v[:, :], v[:, :], float(P), None, ALU.add))
                    steps.settle()
                    mark(eng, marks)
                    steps.end()

    n = net.scope("s1_")
    with n:
        dst_i = n.sb("dst_i", [P, NU * K4], I32)
        hi_i = n.sb("hi_i", [P, NU * K4], I32)
        lo_i = n.sb("lo_i", [P, NU * K4], I32)
        hi = n.sb("hi", [P, NU * K4])
        lo = n.sb("lo", [P, NU * K4])
        hot_lo = n.sb("hot_lo", [P, R, K4, P], BF16)
        hot_hi = n.sb("hot_hi", [P, R, K4, NT], BF16)
        deg = n.sb("deg", [P, NT])
        counts = n.ps("counts", [P, NT])
        loaded, dve = n.sem("loaded"), n.sem("dve")
        hot, used = n.sems("hot", R), n.sems("used", R)
        counted, rooted, zeroed = n.sem("counted"), n.sem("rooted"), n.sem("zeroed")
        zero, zeros, brought = n.sb("zero", [P, P], BF16), n.sb("zeros", [P, NT, D]), n.sem("brought")
        with nc.Block() as block:
            @block.sync
            def _(eng):
                eng.dma_start(dst_i[:, :], dram["dst_tiles"]).then_inc(loaded, 16)
                eng.dma_start(x_row[:, :, :], dram["x"].rearrange("(t p) d -> p t d", p=P)).then_inc(brought, 16)
                eng.wait_ge(zeroed, 2)
                for t in tabs:
                    eng.dma_start(t[0:NP, :].rearrange("(p t) d -> p t d", p=P), zeros[:, :, :]).then_inc(brought, 16)
                    eng.dma_start(t[NP:TR, :], zeros[:, 0, :]).then_inc(brought, 16)
                eng.wait_ge(brought, 16 + 32 * len(tabs))

            @block.gpsimd
            def _(eng):
                eng.memset(zero[:, :], 0.0).then_inc(zeroed, 1)
                eng.memset(zeros[:, :, :], 0.0).then_inc(zeroed, 1)

            @block.vector
            def _(eng):
                eng.wait_ge(loaded, 16)
                steps = Steps(eng, dve)
                steps.done(eng.tensor_scalar(hi_i[:, :], dst_i[:, :], 7, None, ALU.logical_shift_right))
                steps.done(eng.tensor_scalar(lo_i[:, :], dst_i[:, :], P - 1, None, ALU.bitwise_and))
                steps.settle()
                steps.done(eng.tensor_copy(hi[:, :], hi_i[:, :]))
                steps.done(eng.tensor_copy(lo[:, :], lo_i[:, :]))
                steps.settle()
                for i in turns(eng, NU // R):
                    for b in range(R):
                        u = i * R + b
                        eng.wait_ge(used[b], i)
                        eng.tensor_tensor(hot_lo[:, b], bc(net.iota[:, :].unsqueeze(1), [P, K4, P]),
                                          bc(lo[:, bass.ds(u * K4, K4)].unsqueeze(2), [P, K4, P]), ALU.is_equal).then_inc(hot[b], 1)
                        eng.tensor_tensor(hot_hi[:, b], bc(net.iota[:, 0:NT].unsqueeze(1), [P, K4, NT]),
                                          bc(hi[:, bass.ds(u * K4, K4)].unsqueeze(2), [P, K4, NT]), ALU.is_equal).then_inc(hot[b], 1)
                eng.wait_ge(counted, 1)
                steps.done(eng.tensor_scalar(deg[:, :], counts[:, :], 1.0, None, ALU.add))
                eng.wait_ge(rooted, 1)
                steps.done(eng.reciprocal(net.dinv[:, :], deg[:, :]))

            @block.scalar
            def _(eng):
                eng.wait_ge(dve, 5)
                eng.activation(deg[:, :], deg[:, :], ACT.Sqrt).then_inc(rooted, 1)

            @block.tensor
            def _(eng):
                eng.wait_ge(zeroed, 1)
                eng.matmul(counts[:, :], zero[:, :], zero[:, 0:NT], start=True, stop=False, skip_group_check=True)
                for i in turns(eng, NU // R):
                    for b in range(R):
                        eng.wait_ge(hot[b], i * 2 + 2)
                        for k in range(K4):
                            mm = eng.matmul(counts[:, :], hot_lo[:, b, k, :], hot_hi[:, b, k, :], start=False,
                                            stop=False, skip_group_check=True)
                        mm.then_inc(used[b], 1)
                eng.matmul(counts[:, :], zero[:, :], zero[:, 0:NT], start=False, stop=True, skip_group_check=True).then_inc(counted, 1)


def rows_of(table, lo, n=GC):
    return table[bass.ds(lo, n), :].rearrange("(t p) d -> p t d", p=P)


def part_rows(table, g, width):
    return table[bass.ds(g * GC, GC), :].rearrange("(t p) (c d) -> p t c d", p=P, d=width)


def project(net, name, weights, table, x_row, x_T=None, scale=None, keep=None, parts=None):
    nc, dram = net.nc, net.dram
    n = net.scope(name)
    with n:
        F = D * len(weights)
        FW = F if parts is None else F - D
        w = n.sb("w", [D, len(weights), D])
        stage = n.sb("stage", [P, 2, 4, D])
        xt = n.sb("xt", [P, 2, GC])
        prod = n.sb("prod", [P, 2, 4, F])
        three = n.sb("three", [P, 2, 4, 3, D], BF16)
        NS = 1 if parts is None else 2
        DK = 1 if keep is None else 2
        turned = [n.ps(f"turned{c}", [P, GC]) for c in range(2)]
        pp = [n.ps(f"pp{j}", [P, F]) for j in range(4)]
        NX = 1 if x_T is None else 2
        loaded, splits, moved, dve_kept, act_kept = (n.sem(s) for s in ("loaded", "splits", "moved", "dve_kept", "act_kept"))
        staged, turned_in, xt_in, made, stored = (n.sems(s, 2) for s in ("staged", "turned_in", "xt_in", "made", "stored"))
        with nc.Block() as block:
            @block.sync
            def _(eng):
                for c, name_ in enumerate(weights):
                    eng.dma_start(w[:, c, :], dram[name_]).then_inc(loaded, 16)
                for i, c, g in groups(eng):
                    eng.wait_ge(dve_kept, g * DK + DK)
                    mark(eng, moved)
                    eng.wait_ge(act_kept, g + 1)
                    mark(eng, moved)
                    if parts is not None:
                        eng.wait_ge(splits, g * SPLIT_STEPS + SPLIT_STEPS)
                        mark(eng, moved)
                    eng.dma_start(rows_of(table, g * GC)[:, :, 0:FW], prod[:, c, :, 0:FW]).then_inc(stored[c], 16)
                    if parts is not None:
                        eng.dma_start(parts[bass.ds(g * GC, GC), :].rearrange("(t p) c -> p t c", p=P),
                                      three[:, c, :, :, :].rearrange("p t c d -> p t (c d)")).then_inc(stored[c], 16)
                for c in range(2):
                    eng.wait_ge(stored[c], 16 * NS * ((NG + 1 - c) // 2))

            @block.gpsimd
            def _(eng):
                for i, c, g in groups(eng):
                    eng.wait_ge(turned_in[c], i)
                    mark(eng, moved)
                    eng.tensor_copy(stage[:, c, :, :], x_row[:, bass.ds(g * 4, 4), :]).then_inc(staged[c], 1)

            @block.tensor
            def _(eng):
                def turn(i, c, g):
                    eng.wait_ge(staged[c], i + 1)
                    eng.wait_ge(xt_in[c], i * NX)
                    for j in range(4):
                        mm = eng.transpose(turned[c][:, j * P:(j + 1) * P], stage[:, c, j, :], net.ident[:, :])
                    mm.then_inc(turned_in[c], 1)

                eng.wait_ge(loaded, 16 * len(weights))
                turn(0, 0, 0)
                for i, c, g, following in groups_ahead(eng):
                    for group in following:
                        turn(*group)
                    eng.wait_ge(xt_in[c], i * NX + NX)
                    eng.wait_ge(dve_kept, g * DK)
                    eng.wait_ge(act_kept, g)
                    for j in range(4):
                        mm = eng.matmul(pp[j][:, :], xt[:, c, j * P:(j + 1) * P], w[:, :, :].rearrange("p c d -> p (c d)"),
                                        start=True, stop=True)
                        if j == 1:
                            mm.then_inc(made[c], 1)
                    mm.then_inc(made[c], 1)

            @block.scalar
            def _(eng):
                def columns(i, c, g):
                    eng.wait_ge(turned_in[c], i + 1)
                    eng.wait_ge(made[c], i * 2)
                    mark(eng, moved)
                    eng.activation(xt[:, c, :], turned[c][:, :], ACT.Copy).then_inc(xt_in[c], 1)
                    if x_T is not None:
                        eng.activation(x_T[:, bass.ds(g * GC, GC)], turned[c][:, :], ACT.Copy).then_inc(xt_in[c], 1)

                columns(0, 0, 0)
                for i, c, g, following in groups_ahead(eng):
                    for group in following:
                        columns(*group)
                    eng.wait_ge(made[c], i * 2 + 2)
                    eng.wait_ge(stored[c], i * (16 * NS))
                    mark(eng, moved)
                    for j in range(2, 4):
                        if scale is None:
                            cp = eng.activation(prod[:, c, j, :], pp[j][:, :], ACT.Copy)
                        else:
                            cp = eng.activation(prod[:, c, j, :], pp[j][:, :], ACT.Copy, scale=scale[:, bass.ds(g * 4 + j, 1)])
                    cp.then_inc(act_kept, 1)

            @block.vector
            def _(eng):
                for i, c, g in groups(eng):
                    eng.wait_ge(made[c], i * 2 + 1)
                    eng.wait_ge(stored[c], i * (16 * NS))
                    mark(eng, moved)
                    for j in range(2):
                        if scale is None:
                            cp = eng.tensor_copy(prod[:, c, j, :], pp[j][:, :])
                        else:
                            cp = eng.tensor_scalar(prod[:, c, j, :], pp[j][:, :], scale[:, bass.ds(g * 4 + j, 1)], None, ALU.mult)
                    cp.then_inc(dve_kept, 1)
                    eng.wait_ge(dve_kept, g * DK + 1)
                    eng.wait_ge(act_kept, g + 1)
                    mark(eng, moved)
                    if keep is not None:
                        eng.tensor_copy(keep[:, bass.ds(g * 4, 4), :], prod[:, c, :, :]).then_inc(dve_kept, 1)
                    if parts is not None:
                        steps = Steps(eng, splits, g, SPLIT_STEPS)
                        split(eng, steps, prod[:, c, :, F - D:F], *(three[:, c, :, part, :] for part in range(3)))


def gather(eng, out, table, idx):
    return eng.indirect_dma_start(out=out, out_offset=None, in_=table,
                                  in_offset=bass.IndirectOffsetOnAxis(ap=idx, axis=0))


def visit_registers(net, eng):
    if eng.engine not in net.registers:
        net.registers[eng.engine] = [eng.alloc_register(f"visit{k}") for k in range(2 * R)]
    return net.registers[eng.engine]


def look_up(net, eng, regs, i):
    eng.load(regs, net.visits[bass.ds(i * (2 * R), 2 * R)].rearrange("(o a) -> o a", o=1))
    return [(eng.snap(regs[2 * b], min_val=0, max_val=NU - 1), eng.snap(regs[2 * b + 1], min_val=0, max_val=NP - P))
            for b in range(R)]


def last_turn(net, eng):
    return eng.value_load(net.last_i[0:1, 0:1], min_val=NU // R - 1, max_val=VMAX // R - 1)


def turn_count(net, eng):
    return last_turn(net, eng) + 1


def small_loads(net, eng, i, b, unit, idx, idx_in, got, base, base_in, base_used):
    eng.wait_ge(got[b], i * 64)
    eng.dma_start(idx[:, b, :], net.dram["src_tiles"][:, bass.ds(unit * K4, K4)]).then_inc(idx_in[b], 16)
    eng.wait_ge(base_used[b], i)
    mark(eng, net.marks)
    eng.dma_start(base[:, b:b + 1], bc(net.visit_base[bass.ds(i * R + b, 1)].rearrange("(o a) -> o a", o=1), [P, 1])).then_inc(base_in[b], 16)


def visit_loads(net, eng, i, b, unit, dst, base, base_in, base_used):
    eng.wait_ge(base_used[b], i)
    mark(eng, net.marks)
    eng.dma_start(dst[:, b, :], net.dst_cols[:, bass.ds(unit * K4, K4)]).then_inc(base_in[b], 16)
    eng.dma_start(base[:, b:b + 1], bc(net.visit_base[bass.ds(i * R + b, 1)].rearrange("(o a) -> o a", o=1), [P, 1])).then_inc(base_in[b], 16)


def source_loads(net, eng, i, b, unit, idx, idx_in, got):
    eng.wait_ge(got[b], i * 64)
    eng.dma_start(idx[:, b, :], net.dram["src_tiles"][:, bass.ds(unit * K4, K4)]).then_inc(idx_in[b], 16)


def hot_here(net, eng, hot, dst, base, b):
    return eng.scalar_tensor_tensor(out=hot[:, b], in0=bc(net.iota[:, :].unsqueeze(1), [P, K4, P]), scalar=base[:, b:b + 1],
                                    in1=bc(dst[:, b, :].unsqueeze(2), [P, K4, P]), op0=ALU.add, op1=ALU.is_equal)


def gather_unit(eng, marks, i, b, rows, table, idx, idx_in, got):
    eng.wait_ge(idx_in[b], i * 16 + 16)
    mark(eng, marks)
    for k in range(K4):
        gather(eng, rows[:, b, k, :], table, idx[:, b, k:k + 1]).then_inc(got[b], 16)


def build_hot(net, eng, hot, base, b, unit):
    return eng.scalar_tensor_tensor(out=hot[:, b], in0=bc(net.iota[:, :].unsqueeze(1), [P, K4, P]), scalar=base[:, b:b + 1],
                                    in1=bc(net.dst_f[:, bass.ds(unit * K4, K4)].unsqueeze(2), [P, K4, P]),
                                    op0=ALU.add, op1=ALU.is_equal)


def turn_hot(eng, i, b, hot, hot_in, ident, turned, turned_in, pt_in):
    eng.wait_ge(hot_in[b], i + 1)
    if b >= len(turned):
        eng.wait_ge(pt_in[b - len(turned)], i + 1)
    else:
        eng.wait_ge(pt_in[b + R - len(turned)], i)
    h = b % len(turned)
    for k in range(K4):
        mm = eng.transpose(turned[h][:, k, :], hot[:, b, k, :], ident)
    mm.then_inc(turned_in[b], 1)


def copy_turned(eng, marks, i, b, turned, turned_in, pt, pt_in, q_in):
    eng.wait_ge(q_in[b], i)
    eng.wait_ge(turned_in[b], i + 1)
    mark(eng, marks)
    eng.activation(pt[:, b], turned[b % len(turned)][:, :, :], ACT.Copy).then_inc(pt_in[b], 1)


def add_window(net, eng, i, b, base, adds, sums_free):
    if b:
        eng.wait_ge(sums_free[b - 1], i * len(adds) + len(adds))
    else:
        eng.wait_ge(sums_free[R - 1], i * len(adds))
    mark(eng, net.marks)
    for acc, sums in adds:
        at = acc[:, bass.ds(base, P)]
        eng.tensor_tensor(at, at, sums, ALU.add).then_inc(sums_free[b], 1)


def clear(net, name, acc):
    n = net.scope(name)
    with n, net.nc.Block() as block:
        @block.gpsimd
        def _(eng):
            for a in acc:
                eng.memset(a[:, :], 0.0)


def edges_gcn(net, hs, acc, dec_rows):
    nc, dram = net.nc, net.dram
    n = net.scope("l0_")
    with n:
        idx = n.sb("idx", [P, R, K4], I32)
        base, dst = n.sb("base", [P, R]), n.sb("dst", [P, R, K4])
        msg = n.sb("msg", [P, R, K4, D])
        hot = n.sb("hot", [P, R, K4, P])
        tb = n.sb("tb", [WB, R, UNIT], BF16)
        w3 = n.sb("w3", [3, P])
        cut3 = n.sb("cut3", [3, 3, P], BF16)
        wd1 = n.sb("wd1", [WB, P], BF16)
        wd2 = n.sb("wd2", [P, H])
        hid = n.sb("hid", [P, UNIT])
        dec = n.sb("dec", [P, NU * K4, H])
        sums = [n.ps(f"sums{b}", [P, P]) for b in range(R)]
        ph, pd = n.ps("ph", [P, UNIT]), n.ps("pd", [P, K4, H])
        idx_in, base_in, hot_in, summed, sums_free, tb_in, hid_in = (n.sems(s, R) for s in (
            "idx_in", "base_in", "hot_in", "summed", "sums_free", "tb_in", "hid_in"))
        zeroed, loaded, cut, placed, relu, pd_in, dec_in, dec_out = (n.sem(x) for x in (
            "zeroed", "loaded", "cut", "placed", "relu", "pd_in", "dec_in", "dec_out"))
        got = n.gather_sems("got", R)
        with nc.Block() as block:
            @block.gpsimd
            def _(eng):
                for w in (w3, wd2, wd1):
                    eng.memset(w[:, :], 0.0).then_inc(zeroed, 1)

            @block.sync
            def _(eng):
                eng.wait_ge(zeroed, 3)
                eng.dma_start(w3[0:1, 0:HID], dram["L3_gnn_Wd1"][0:1, :]).then_inc(loaded, 16)
                eng.dma_start(w3[2:3, 0:HID], dram["L3_gnn_Wd1"][1:2, :]).then_inc(loaded, 16)
                eng.dma_start(w3[1:2, 0:HID], dram["L3_gnn_bd1"].rearrange("(o d) -> o d", o=1)).then_inc(loaded, 16)
                eng.dma_start(w3[1:2, HID:HID + 1], dram["one"].rearrange("(o d) -> o d", o=1)).then_inc(loaded, 16)
                eng.dma_start(wd2[0:HID, :], dram["L3_gnn_Wd2"]).then_inc(loaded, 16)
                eng.dma_start(wd2[HID:HID + 1, :], dram["L3_gnn_bd2"].rearrange("(o d) -> o d", o=1)).then_inc(loaded, 16)
                eng.wait_ge(cut, 1 + SPLIT_STEPS)
                rows = [(0, 0), (0, 1), (0, 2), (0, 0), (0, 1), (0, 0)]
                rows += [(1, c) for c in range(3)] + [(2, c) for c in range(3)]
                for to, (of, c) in enumerate(rows):
                    eng.dma_start(wd1[to:to + 1, :], cut3[of:of + 1, c, :]).then_inc(placed, 16)
                eng.wait_ge(placed, 16 * WB)

            @block.vector
            def _(eng):
                eng.wait_ge(loaded, 16 * 6)
                steps = Steps(eng, cut)
                steps.done(eng.tensor_scalar(w3[:, :], w3[:, :], net.type_scale[0:3, 0:1], None, ALU.mult))
                steps.settle()
                split(eng, steps, w3[:, :], cut3[:, 0, :], cut3[:, 1, :], cut3[:, 2, :])

        with nc.Block() as block:
            @block.sync
            def _(eng):
                regs = visit_registers(net, eng)
                for i in turns(eng, turn_count(net, eng)):
                    visit = look_up(net, eng, regs, i)
                    for b in range(R):
                        source_loads(net, eng, i, b, visit[b][0], idx, idx_in, got)
                        visit_loads(net, eng, i, b, visit[b][0], dst, base, base_in, hot_in)
                        eng.wait_ge(hid_in[b], i)
                        mark(eng, net.marks)
                        eng.dma_start(tb[:, b, :], net.parts[0:WB, bass.ds(visit[b][0] * UNIT, UNIT)]).then_inc(tb_in[b], 16)
                eng.wait_ge(dec_in, turn_count(net, eng) * R)
                mark(eng, net.marks)
                eng.dma_start(dec_rows, dec[:, :, :].rearrange("p t h -> p (t h)")).then_inc(dec_out, 16)
                eng.wait_ge(dec_out, 16)

            @block.gpsimd
            def _(eng):
                for i in turns(eng, turn_count(net, eng)):
                    for b in range(R):
                        eng.wait_ge(summed[b], i)
                        gather_unit(eng, net.marks, i, b, msg, hs, idx, idx_in, got)

            @block.vector
            def _(eng):
                regs = visit_registers(net, eng)
                for i in turns(eng, turn_count(net, eng)):
                    visit = look_up(net, eng, regs, i)
                    for b in range(R):
                        eng.wait_ge(base_in[b], i * 32 + 32)
                        eng.wait_ge(summed[b], i)
                        hot_here(net, eng, hot, dst, base, b).then_inc(hot_in[b], 1)
                    for b in range(R):
                        eng.wait_ge(summed[b], i + 1)
                        add_window(net, eng, i, b, visit[b][1], [(acc, sums[b][:, :])], sums_free)

            @block.scalar
            def _(eng):
                regs = visit_registers(net, eng)
                for i in turns(eng, turn_count(net, eng)):
                    visit = look_up(net, eng, regs, i)
                    for b in range(R):
                        u = i * R + b
                        eng.wait_ge(hid_in[b], i + 1)
                        eng.wait_ge(pd_in, u)
                        mark(eng, net.marks)
                        eng.activation(hid[:, :], ph[:, :], ACT.Relu).then_inc(relu, 1)
                        eng.wait_ge(pd_in, u + 1)
                        eng.wait_ge(dec_in, u)
                        mark(eng, net.marks)
                        eng.activation(dec[:, bass.ds(visit[b][0] * K4, K4), :], pd[:, :, :], ACT.Copy).then_inc(dec_in, 1)

            @block.tensor
            def _(eng):
                for i in turns(eng, turn_count(net, eng)):
                    for b in range(R):
                        u = i * R + b
                        eng.wait_ge(tb_in[b], i * 16 + 16)
                        eng.wait_ge(relu, u)
                        eng.matmul(ph[:, :], wd1[:, :], tb[:, b, :], start=True, stop=True).then_inc(hid_in[b], 1)
                        eng.wait_ge(hot_in[b], i + 1)
                        eng.wait_ge(sums_free[b], i)
                        eng.wait_ge(got[b], i * 64 + 64)
                        for k in range(K4):
                            mm = eng.matmul(sums[b][:, :], msg[:, b, k, :], hot[:, b, k, :], start=(k == 0), stop=(k == K4 - 1))
                        mm.then_inc(summed[b], 1)
                        eng.wait_ge(relu, u + 1)
                        eng.wait_ge(dec_in, u)
                        for k in range(K4):
                            mm = eng.matmul(pd[:, k, :], hid[:, k * P:(k + 1) * P], wd2[:, :], start=True, stop=True)
                        mm.then_inc(pd_in, 1)


def nodes_gcn(net, acc, hs_row, x_row, table, parts):
    nc, dram = net.nc, net.dram
    n = net.scope("n0_")
    PER = 1 + 4 + 1 + LN_STEPS
    with n:
        bias = n.sb("bias", [P, D])
        st = n.sb("st", [P, 2, GC])
        y = n.sb("y", [P, 4, D])
        z = n.sb("z", [P, 4, D])
        rest = n.sb("rest", [P, 4, D])
        three = n.sb("three", [P, 2, 4, 3, D], BF16)
        stats, moments, std = n.sb("stats", [P, 4, 6]), n.sb("moments", [P, 4, 2]), n.sb("std", [P, 4])
        turned = [n.ps(f"turned{c}", [P, GC]) for c in range(2)]
        loaded, dve, rooted, marks, splits, rows_out = (n.sem(s) for s in ("loaded", "dve", "rooted", "marks", "splits", "rows_out"))
        staged, turned_in, used, stored = (n.sems(s, 2) for s in ("staged", "turned_in", "used", "stored"))
        with nc.Block() as block:
            @block.sync
            def _(eng):
                eng.dma_start(bias[:, :], everywhere(dram["L0_gnn_b"], D)).then_inc(loaded, 16)
                for i, c, g in groups(eng):
                    eng.wait_ge(dve, g * PER + PER)
                    mark(eng, marks)
                    eng.dma_start(rows_of(table, g * GC), x_row[:, bass.ds(g * 4, 4), :]).then_inc(rows_out, 16)
                    eng.wait_ge(splits, g * SPLIT_STEPS + SPLIT_STEPS)
                    mark(eng, marks)
                    eng.dma_start(part_rows(parts, g, D), three[:, c]).then_inc(stored[c], 16)
                for c in range(2):
                    eng.wait_ge(stored[c], 16 * ((NG + 1 - c) // 2))
                eng.wait_ge(rows_out, 16 * NG)

            @block.gpsimd
            def _(eng):
                for i, c, g in groups(eng):
                    eng.wait_ge(dve, g * PER + PER)
                    mark(eng, marks)
                    eng.wait_ge(stored[c], i * 16)
                    mark(eng, marks)
                    steps = Steps(eng, splits, g, SPLIT_STEPS)
                    split_of(eng, steps, x_row[:, bass.ds(g * 4, 4), :], rest[:, :, :], *(three[:, c, :, part, :] for part in range(3)), marks)
                    steps.settle()
                    mark(eng, marks)

            @block.tensor
            def _(eng):
                for i, c, g in groups(eng):
                    eng.wait_ge(staged[c], i + 1)
                    eng.wait_ge(used[c], i)
                    for j in range(4):
                        mm = eng.transpose(turned[c][:, j * P:(j + 1) * P], st[:, c, j * P:(j + 1) * P], net.ident[:, :])
                    mm.then_inc(turned_in[c], 1)

            @block.scalar
            def _(eng):
                def stage(i, c, g):
                    eng.wait_ge(turned_in[c], i)
                    mark(eng, marks)
                    eng.activation(st[:, c, :], acc[:, bass.ds(g * GC, GC)], ACT.Copy).then_inc(staged[c], 1)

                stage(0, 0, 0)
                for i, c, g, following in groups_ahead(eng):
                    for group in following:
                        stage(*group)
                    eng.wait_ge(dve, g * PER + 6 + 9)
                    eng.activation(std[:, :], std[:, :], ACT.Sqrt).then_inc(rooted, 1)

            @block.vector
            def _(eng):
                eng.wait_ge(loaded, 16)
                for i, c, g in groups(eng):
                    steps = Steps(eng, dve, g, PER)
                    mine = x_row[:, bass.ds(g * 4, 4), :]
                    eng.wait_ge(turned_in[c], i + 1)
                    mark(eng, marks)
                    steps.done(eng.tensor_tensor(y[:, :, :], turned[c][:, :].rearrange("p (t d) -> p t d", d=D),
                                                 hs_row[:, bass.ds(g * 4, 4), :], ALU.add))
                    steps.settle()
                    mark(eng, used[c])
                    for j in range(4):
                        steps.done(eng.scalar_tensor_tensor(out=z[:, j, :], in0=y[:, j, :], scalar=net.dinv[:, bass.ds(g * 4 + j, 1)],
                                                            in1=bias[:, :], op0=ALU.mult, op1=ALU.add))
                    steps.settle()
                    mark(eng, marks)
                    steps.done(eng.scalar_tensor_tensor(out=y[:, :, :], in0=z[:, :, :], scalar=0.0, in1=mine, op0=ALU.max, op1=ALU.add))
                    steps.settle()
                    layer_norm(eng, steps, y, stats, moments, std, mine, marks, rooted, g + 1, 1e-5)
                    mark(eng, marks)
                    steps.end()


def edges_gated(net, x1, x1_parts, acc, tabs):
    nc, dram = net.nc, net.dram
    n = net.scope("l1_")
    IDX = 6
    with n:
        idx = n.sb("idx", [P, R, K4], I32)
        base = n.sb("base", [P, R])
        src_all = n.sb("src_all", [P, R, UNIT], I32)
        xs, xd, ea = (n.sb(s, [P, R, K4, D]) for s in ("xs", "xd", "ea"))
        hot = n.sb("hot", [P, R, K4, P])
        pt = n.sb("pt", [P, R, K4, P], BF16)
        slab = n.sb("slab", [P, R, 3, D], BF16)
        same = n.sb("same", [P, R, K4, P])
        before = n.sb("before", [P, K4, P])
        again = n.sb("again", [P, K4])
        off = n.sb("off", [P, K4])
        to_i = n.sb("to_i", [P, R, K4], I32)
        total = n.sb("total", [P, R, K4, D])
        turned = [n.ps(f"turned{b}", [P, K4, P]) for b in range(2)]
        q = [n.ps(f"q{b}", [P, K4, D]) for b in range(2)]
        pres = [n.ps(f"pres{b}", [P, K4, D]) for b in range(2)]
        sums = [n.ps(f"sums{b}", [P, P]) for b in range(2)]
        got = n.gather_sems("got", R)
        idx_in, base_in, ea_in, hot_in, slab_in, turned_in, pt_in, q_in, gated, summed, sums_free, total_in, to_in = (
            n.sems(s, R) for s in ("idx_in", "base_in", "ea_in", "hot_in", "slab_in", "turned_in", "pt_in", "q_in", "gated",
                                   "summed", "sums_free", "total_in", "to_in"))
        pre_in = n.sems("pre_in", 2)
        tab_added = n.gather_sems("tab_added", K4)
        marks, dve = net.marks, n.sem("dve")
        with nc.Block() as block:
            @block.sync
            def _(eng):
                regs = visit_registers(net, eng)
                for i in turns(eng, turn_count(net, eng)):
                    visit = look_up(net, eng, regs, i)
                    for b in range(R):
                        unit, at = visit[b]
                        small_loads(net, eng, i, b, unit, idx, idx_in, got, base, base_in, hot_in)
                        eng.wait_ge(q_in[b], i)
                        mark(eng, marks)
                        eng.dma_start(slab[:, b, :, :], x1_parts[bass.ds(at, P), :].rearrange("p (c d) -> p c d", d=D)).then_inc(slab_in[b], 16)
                        eng.wait_ge(summed[b], i)
                        mark(eng, marks)
                        eng.dma_start(ea[:, b], dram["ea"][bass.ds(unit * UNIT, UNIT), :].rearrange(
                            "(p k) d -> p k d", k=K4)).then_inc(ea_in[b], 16)
                        eng.dma_start(src_all[:, b, :], bc(dram["src_row"][bass.ds(unit * UNIT, UNIT)].rearrange(
                            "(o e) -> o e", o=1), [P, UNIT])).then_inc(ea_in[b], 16)

            @block.gpsimd
            def _(eng):
                n_turns = turn_count(net, eng)
                for i in turns(eng, n_turns):
                    for b in range(R):
                        eng.wait_ge(summed[b], i)
                        gather_unit(eng, marks, i, b, xs, x1, idx, idx_in, got)
                    for b in range(R):
                        eng.wait_ge(total_in[b], i + 1)
                        eng.wait_ge(to_in[b], i + 1)
                        for k in range(K4):
                            eng.wait_ge(tab_added[k], (i * R + b) * 16)
                            mark(eng, marks)
                            eng.indirect_dma_start(out=tabs[k], out_offset=bass.IndirectOffsetOnAxis(ap=to_i[:, b, k:k + 1], axis=0),
                                                   in_=total[:, b, k, :], in_offset=None, compute_op=ALU.add).then_inc(tab_added[k], 16)
                for k in range(K4):
                    eng.wait_ge(tab_added[k], n_turns * (R * 16))
                mark(eng, marks)

            @block.vector
            def _(eng):
                def add(i, b):
                    eng.wait_ge(summed[b], i + 1)
                    add_window(net, eng, i, b, visit[b][1], [(acc, sums[b % 2][:, :])], sums_free)

                regs = visit_registers(net, eng)
                for i in turns(eng, turn_count(net, eng)):
                    visit = look_up(net, eng, regs, i)
                    for b in range(R):
                        eng.wait_ge(base_in[b], i * 16 + 16)
                        eng.wait_ge(summed[b], i)
                        build_hot(net, eng, hot, base, b, visit[b][0]).then_inc(hot_in[b], 1)
                    for b in range(R):
                        unit = visit[b][0]
                        src = net.src_f[:, bass.ds(unit * K4, K4)]
                        steps = Steps(eng, dve, i * R + b, IDX)
                        eng.wait_ge(ea_in[b], i * 32 + 32)
                        mark(eng, marks)
                        steps.done(eng.tensor_tensor(same[:, b], src_all[:, b, :].rearrange("p (q k) -> p k q", k=K4),
                                                     bc(src.unsqueeze(2), [P, K4, P]), ALU.is_equal))
                        steps.settle()
                        steps.done(eng.tensor_tensor(before[:, :, :], same[:, b], bc(net.lower[:, :].unsqueeze(1), [P, K4, P]), ALU.mult))
                        steps.done(eng.tensor_scalar(off[:, :], src, -1.0, net.spare[:, 0:1], ALU.mult, ALU.add))
                        steps.settle()
                        steps.done(eng.tensor_reduce(again[:, :], before[:, :, :], AX, ALU.max))
                        steps.settle()
                        steps.done(eng.tensor_tensor(off[:, :], off[:, :], again[:, :], ALU.mult))
                        for k in range(K4):
                            eng.wait_ge(tab_added[k], i * (16 * R))
                        steps.settle()
                        mark(eng, marks)
                        steps.done(eng.tensor_tensor(off[:, :], off[:, :], src, ALU.add))
                        steps.settle()
                        mark(eng, marks)
                        eng.tensor_copy(to_i[:, b, :], off[:, :]).then_inc(to_in[b], 1)
                        eng.wait_ge(q_in[b], i + 1)
                        eng.tensor_tensor(xd[:, b], q[b % 2][:, :, :], ea[:, b], ALU.mult).then_inc(gated[b], 1)
                        eng.wait_ge(got[b], i * 64 + 64)
                        eng.tensor_tensor(xs[:, b], xs[:, b], ea[:, b], ALU.mult).then_inc(gated[b], 1)
                        steps.end()
                        if b:
                            add(i, b - 1)
                    add(i, R - 1)

            @block.scalar
            def _(eng):
                for i in turns(eng, turn_count(net, eng)):
                    for b in range(R):
                        copy_turned(eng, marks, i, b, turned, turned_in, pt, pt_in, q_in)
                    for b in range(R):
                        h = b % 2
                        eng.wait_ge(pre_in[h], i * (R // 2) + b // 2 + 1)
                        for k in range(K4):
                            eng.wait_ge(tab_added[k], i * (16 * R))
                        mark(eng, marks)
                        eng.activation(total[:, b], pres[h][:, :, :], ACT.Copy).then_inc(total_in[b], 1)

            @block.tensor
            def _(eng):
                def hand_out(i, b):
                    eng.wait_ge(pt_in[b], i + 1)
                    eng.wait_ge(slab_in[b], i * 16 + 16)
                    eng.wait_ge(gated[(b + 2) % R], i * 2 + (2 if b >= 2 else 0))
                    for k in range(K4):
                        for c in range(3):
                            mm = eng.matmul(q[b % 2][:, k, :], pt[:, b, k, :], slab[:, b, c, :], start=(c == 0), stop=(c == 2))
                    mm.then_inc(q_in[b], 1)

                def sum_up(i, b):
                    h = b % 2
                    eng.wait_ge(gated[b], i * 2 + 2)
                    eng.wait_ge(sums_free[(b + 2) % R], i + (1 if b >= 2 else 0))
                    eng.wait_ge(total_in[(b + 2) % R], i + (1 if b >= 2 else 0))
                    for k in range(K4):
                        mm = eng.matmul(pres[h][:, k, :], same[:, b, k, :], xd[:, b, k, :], start=True, stop=True)
                    mm.then_inc(pre_in[h], 1)
                    for k in range(K4):
                        mm = eng.matmul(sums[h][:, :], xs[:, b, k, :], hot[:, b, k, :], start=(k == 0), stop=(k == K4 - 1))
                    mm.then_inc(summed[b], 1)

                for i in turns(eng, turn_count(net, eng)):
                    for b in range(R):
                        turn_hot(eng, i, b, hot, hot_in, net.ident[:, :], turned, turned_in, pt_in)
                    hand_out(i, 0)
                    for b in range(R):
                        if b + 1 < R:
                            hand_out(i, b + 1)
                        sum_up(i, b)


def nodes_gated(net, acc, tabs, x_row):
    nc, dram = net.nc, net.dram
    n = net.scope("n1_")
    PER = 1 + LN_STEPS
    with n:
        st = n.sb("st", [P, 2, GC])
        parts = n.sb("parts", [P, 2, K4, 4, D])
        z = n.sb("z", [P, 2, 4, D])
        y = n.sb("y", [P, 4, D])
        stats, moments, std = n.sb("stats", [P, 4, 6]), n.sb("moments", [P, 4, 2]), n.sb("std", [P, 4])
        turned = [n.ps(f"turned{c}", [P, GC]) for c in range(2)]
        dve, rooted, marks, pool = (n.sem(s) for s in ("dve", "rooted", "marks", "pool"))
        loaded, staged, turned_in, z_in, used = (n.sems(s, 2) for s in ("loaded", "staged", "turned_in", "z_in", "used"))
        with nc.Block() as block:
            @block.sync
            def _(eng):
                for i, c, g in groups(eng):
                    eng.wait_ge(z_in[c], i)
                    mark(eng, marks)
                    for k in range(K4):
                        eng.dma_start(parts[:, c, k], rows_of(tabs[k], g * GC)).then_inc(loaded[c], 16)

            @block.gpsimd
            def _(eng):
                for i, c, g in groups(eng):
                    steps = Steps(eng, pool, g, 3)
                    eng.wait_ge(loaded[c], i * (16 * K4) + 16 * K4)
                    mark(eng, marks)
                    steps.done(eng.tensor_tensor(parts[:, c, 0], parts[:, c, 0], parts[:, c, 1], ALU.add))
                    steps.done(eng.tensor_tensor(parts[:, c, 2], parts[:, c, 2], parts[:, c, 3], ALU.add))
                    steps.settle()
                    mark(eng, marks)
                    steps.done(eng.tensor_tensor(parts[:, c, 0], parts[:, c, 0], parts[:, c, 2], ALU.add))
                    eng.wait_ge(used[c], i)
                    steps.settle()
                    mark(eng, marks)
                    eng.tensor_tensor(z[:, c], parts[:, c, 0], x_row[:, bass.ds(g * 4, 4), :], ALU.add).then_inc(z_in[c], 1)

            @block.tensor
            def _(eng):
                for i, c, g in groups(eng):
                    eng.wait_ge(staged[c], i + 1)
                    eng.wait_ge(used[c], i)
                    for j in range(4):
                        mm = eng.transpose(turned[c][:, j * P:(j + 1) * P], st[:, c, j * P:(j + 1) * P], net.ident[:, :])
                    mm.then_inc(turned_in[c], 1)

            @block.scalar
            def _(eng):
                def stage(i, c, g):
                    eng.wait_ge(turned_in[c], i)
                    mark(eng, marks)
                    eng.activation(st[:, c, :], acc[:, bass.ds(g * GC, GC)], ACT.Copy).then_inc(staged[c], 1)

                stage(0, 0, 0)
                for i, c, g, following in groups_ahead(eng):
                    for group in following:
                        stage(*group)
                    eng.wait_ge(dve, g * PER + 1 + 9)
                    eng.activation(std[:, :], std[:, :], ACT.Sqrt).then_inc(rooted, 1)

            @block.vector
            def _(eng):
                for i, c, g in groups(eng):
                    steps = Steps(eng, dve, g, PER)
                    eng.wait_ge(turned_in[c], i + 1)
                    eng.wait_ge(z_in[c], i + 1)
                    steps.done(eng.tensor_tensor(y[:, :, :], turned[c][:, :].rearrange("p (t d) -> p t d", d=D), z[:, c], ALU.add))
                    steps.settle()
                    mark(eng, used[c])
                    layer_norm(eng, steps, y, stats, moments, std, x_row[:, bass.ds(g * 4, 4), :], marks, rooted, g + 1, 1e-5)
                    mark(eng, marks)
                    steps.end()


def edges_attention(net, kv, q_parts, acc, acc_z):
    nc = net.nc
    n = net.scope("l2_")
    PER = 3
    with n:
        idx = n.sb("idx", [P, R, K4], I32)
        base, dst = n.sb("base", [P, R]), n.sb("dst", [P, R, K4])
        kvs = n.sb("kvs", [P, R, K4, 2 * D])
        qk = n.sb("qk", [P, K4, D])
        hot = n.sb("hot", [P, R, K4, P])
        pt = n.sb("pt", [P, R, K4, P], BF16)
        slab = n.sb("slab", [P, R, 3, D], BF16)
        s = n.sb("s", [P, R, K4, H])
        msg = n.sb("msg", [P, R, K4, D])
        turned = [n.ps(f"turned{b}", [P, K4, P]) for b in range(2)]
        q = [n.ps(f"q{b}", [P, K4, D]) for b in range(2)]
        both = [n.ps(f"both{b}", [P, 2, P]) for b in range(R)]
        sums, zs = [t[:, 0, :] for t in both], [t[0:H, 1, :] for t in both]
        got = n.gather_sems("got", R)
        idx_in, base_in, hot_in, slab_in, turned_in, pt_in, q_in, scored, weighed, ready, summed, sums_free = (n.sems(x, R) for x in (
            "idx_in", "base_in", "hot_in", "slab_in", "turned_in", "pt_in", "q_in", "scored", "weighed", "ready", "summed", "sums_free"))
        marks, dve = net.marks, n.sem("dve")
        with nc.Block() as block:
            @block.sync
            def _(eng):
                regs = visit_registers(net, eng)
                for i in turns(eng, turn_count(net, eng)):
                    visit = look_up(net, eng, regs, i)
                    for b in range(R):
                        unit, at = visit[b]
                        source_loads(net, eng, i, b, unit, idx, idx_in, got)
                        visit_loads(net, eng, i, b, unit, dst, base, base_in, hot_in)
                        eng.wait_ge(q_in[b], i)
                        mark(eng, marks)
                        eng.dma_start(slab[:, b, :, :], q_parts[bass.ds(at, P), :].rearrange("p (c d) -> p c d", d=D)).then_inc(slab_in[b], 16)

            @block.gpsimd
            def _(eng):
                for i in turns(eng, turn_count(net, eng)):
                    for b in range(R):
                        eng.wait_ge(ready[b], i)
                        gather_unit(eng, marks, i, b, kvs, kv, idx, idx_in, got)

            @block.vector
            def _(eng):
                def score(i, b):
                    steps = Steps(eng, dve, i * R + b, PER)
                    eng.wait_ge(q_in[b], i + 1)
                    eng.wait_ge(got[b], i * 64 + 64)
                    steps.done(eng.tensor_tensor(qk[:, :, :], q[b % 2][:, :, :], kvs[:, b, :, 0:D], ALU.mult))
                    steps.settle()
                    steps.done(eng.tensor_reduce(s[:, b], qk[:, :, :].rearrange("p k (h c) -> p k h c", h=H), AX, ALU.add))
                    steps.settle()
                    steps.done(eng.tensor_scalar(s[:, b], s[:, b], 1.0 / DH ** 0.5, 5.0, ALU.mult, ALU.min))
                    steps.settle()
                    eng.tensor_scalar(s[:, b], s[:, b], -5.0, None, ALU.max).then_inc(scored[b], 1)
                    steps.end()

                def weigh(i, b):
                    eng.wait_ge(weighed[b], i + 1)
                    eng.tensor_tensor(msg[:, b].rearrange("p k (h c) -> p k h c", h=H),
                                      kvs[:, b, :, D:2 * D].rearrange("p k (h c) -> p k h c", h=H),
                                      bc(s[:, b].unsqueeze(3), [P, K4, H, DH]), ALU.mult).then_inc(ready[b], 1)

                def add(i, b):
                    eng.wait_ge(summed[b], i + 1)
                    add_window(net, eng, i, b, visit[b][1], [(acc, sums[b]), (acc_z, zs[b])], sums_free)

                def build(i, b):
                    eng.wait_ge(base_in[b], i * 32 + 32)
                    eng.wait_ge(summed[b], i)
                    hot_here(net, eng, hot, dst, base, b).then_inc(hot_in[b], 1)

                regs = visit_registers(net, eng)
                for b in range(R):
                    build(0, b)
                for i, final in rolling(eng, last_turn(net, eng)):
                    visit = look_up(net, eng, regs, i)
                    for b in range(R + 2):
                        if b < R:
                            score(i, b)
                        if 1 <= b <= R:
                            weigh(i, b - 1)
                        if b >= 2:
                            add(i, b - 2)
                            for visit_later in later(i, b - 2, R, final):
                                build(*visit_later)
                    mark(eng, marks)

            @block.scalar
            def _(eng):
                for b in range(3):
                    copy_turned(eng, marks, 0, b, turned, turned_in, pt, pt_in, q_in)
                for i, final in rolling(eng, last_turn(net, eng)):
                    for b in range(R):
                        eng.wait_ge(scored[b], i + 1)
                        eng.activation(s[:, b], s[:, b], ACT.Exp).then_inc(weighed[b], 1)
                        for visit in later(i, b, 3, final):
                            copy_turned(eng, marks, *visit, turned, turned_in, pt, pt_in, q_in)

            @block.tensor
            def _(eng):
                def hand_out(i, b):
                    eng.wait_ge(pt_in[b], i + 1)
                    eng.wait_ge(slab_in[b], i * 16 + 16)
                    eng.wait_ge(scored[(b + 2) % R], i + (1 if b >= 2 else 0))
                    for k in range(K4):
                        for c in range(3):
                            mm = eng.matmul(q[b % 2][:, k, :], pt[:, b, k, :], slab[:, b, c, :], start=(c == 0), stop=(c == 2))
                    mm.then_inc(q_in[b], 1)

                def sum_up(i, b):
                    eng.wait_ge(sums_free[b], i * 2)
                    eng.wait_ge(weighed[b], i + 1)
                    for k in range(K4):
                        eng.matmul(zs[b], s[:, b, k, :], hot[:, b, k, :], start=(k == 0), stop=(k == K4 - 1))
                    eng.wait_ge(ready[b], i + 1)
                    for k in range(K4):
                        mm = eng.matmul(sums[b], msg[:, b, k, :], hot[:, b, k, :], start=(k == 0), stop=(k == K4 - 1))
                    mm.then_inc(summed[b], 1)

                for b in range(3):
                    turn_hot(eng, 0, b, hot, hot_in, net.ident[:, :], turned, turned_in, pt_in)
                for b in range(2):
                    hand_out(0, b)
                for i, final in rolling(eng, last_turn(net, eng)):
                    for b in range(R):
                        for visit in later(i, b, 2, final):
                            hand_out(*visit)
                        for visit in later(i, b, 3, final):
                            turn_hot(eng, *visit, hot, hot_in, net.ident[:, :], turned, turned_in, pt_in)
                        sum_up(i, b)


def reciprocals(net, name, acc_z, to, groups_of_heads, least, added):
    nc = net.nc
    n = net.scope(name)
    W = H * NP // P
    with n:
        spread = n.sb("spread", [P, groups_of_heads, W])
        cells = net.table(name + "cells", (groups_of_heads, H, NP))
        moved, dve = n.sem("moved"), n.sem("dve")
        with nc.Block() as block:
            @block.sync
            def _(eng):
                flat = cells.rearrange("t h n -> t (h n)")
                for t in range(groups_of_heads):
                    eng.dma_start(cells[t], acc_z[t * H:(t + 1) * H, :]).then_inc(moved, 16)
                eng.wait_ge(moved, 16 * groups_of_heads)
                for t in range(groups_of_heads):
                    eng.dma_start(spread[:, t, :], flat[t].rearrange("(p w) -> p w", p=P)).then_inc(moved, 16)
                eng.wait_ge(dve, groups_of_heads + 1)
                eng.dma_start(flat[0].rearrange("(p w) -> p w", p=P), spread[:, 0, :]).then_inc(moved, 16)
                eng.wait_ge(moved, 32 * groups_of_heads + 16)
                eng.dma_start(to[0:H, :], cells[0]).then_inc(moved, 16)
                eng.wait_ge(moved, 32 * groups_of_heads + 32)

            @block.vector
            def _(eng):
                steps = Steps(eng, dve)
                eng.wait_ge(moved, 32 * groups_of_heads)
                for t in range(1, groups_of_heads):
                    steps.done(eng.tensor_tensor(spread[:, 0, :], spread[:, 0, :], spread[:, t, :], ALU.add))
                    steps.settle()
                if least is not None:
                    steps.done(eng.tensor_scalar(spread[:, 0, :], spread[:, 0, :], least, None, ALU.max))
                else:
                    steps.done(eng.tensor_scalar(spread[:, 0, :], spread[:, 0, :], added, None, ALU.add))
                steps.settle()
                steps.done(eng.reciprocal(spread[:, 0, :], spread[:, 0, :]))


def nodes_attention(net, acc, acc_z, x_row, x_T):
    nc, dram = net.nc, net.dram
    reciprocals(net, "r2_", acc_z, acc_z, 1, None, 1e-6)
    n = net.scope("n2_")
    with n:
        hx = n.sb("hx", [P, NP])
        wo, w1, w2 = n.sb("wo", [D, D]), n.sb("w1", [D, 2, P]), n.sb("w2", [P, 2, D])
        bo, b1, b2 = n.sb("bo", [P, 1]), n.sb("b1", [P, 2]), n.sb("b2", [P, 1])
        bn = n.sb("bn", [P, 4])
        h, h1 = n.sb("h", [P, 2, GC]), n.sb("h1", [P, 2, GC])
        stats, mv, coef, std = n.sb("stats", [P, NG, 6]), n.sb("mv", [P, 2]), n.sb("coef", [P, 2]), n.sb("std", [P, 1])
        pz = [n.ps(f"pz{c}", [P, GC]) for c in range(2)]
        po = [n.ps(f"po{c}", [P, GC]) for c in range(2)]
        p1 = [n.ps(f"p1{f}", [P, GC]) for f in range(2)]
        marks = n.sem("marks")

        def batch_coefficients(name, gain, bias):
            dve, rooted = n.sem(name + "dve"), n.sem(name + "rooted")
            with nc.Block() as block:
                @block.scalar
                def _(eng):
                    eng.wait_ge(dve, 2)
                    eng.activation(std[:, :], std[:, :], ACT.Sqrt).then_inc(rooted, 1)

                @block.vector
                def _(eng):
                    steps = Steps(eng, dve)
                    steps.done(eng.bn_aggr(mv[:, :], stats[:, :, :]))
                    steps.settle()
                    steps.done(eng.tensor_scalar(std[:, :], mv[:, 1:2], 1e-5, None, ALU.add))
                    eng.wait_ge(rooted, 1)
                    steps.done(eng.reciprocal(std[:, :], std[:, :]))
                    steps.settle()
                    steps.done(eng.tensor_tensor(coef[:, 0:1], std[:, :], gain, ALU.mult))
                    steps.settle()
                    steps.done(eng.tensor_tensor(std[:, :], mv[:, 0:1], coef[:, 0:1], ALU.mult))
                    steps.settle()
                    steps.done(eng.tensor_tensor(coef[:, 1:2], bias, std[:, :], ALU.subtract))

        z = n.sb("z", [H, 2, GC])
        loaded, counted = n.sem("loaded"), n.sem("counted")
        z_in, spread, normed, made, used = (n.sems(s, 2) for s in ("z_in", "spread", "normed", "made", "used"))
        with nc.Block() as block:
            @block.sync
            def _(eng):
                eng.dma_start(wo[:, :], dram["L2_gnn_Wo"]).then_inc(loaded, 16)
                eng.dma_start(w1[:, :, :], dram["L2_gnn_W1"].rearrange("d (f o) -> d f o", f=2)).then_inc(loaded, 16)
                eng.dma_start(w2[:, :, :], dram["L2_gnn_W2"].rearrange("(f o) d -> o f d", f=2)).then_inc(loaded, 16)
                eng.dma_start(bo[:, :], cols(dram["L2_gnn_bo"])).then_inc(loaded, 16)
                for f in range(2):
                    eng.dma_start(b1[:, f:f + 1], cols(dram["L2_gnn_b1"][f * P:(f + 1) * P])).then_inc(loaded, 16)
                eng.dma_start(b2[:, :], cols(dram["L2_gnn_b2"])).then_inc(loaded, 16)
                for c, name in enumerate(("bn1_g", "bn1_b", "bn2_g", "bn2_b")):
                    eng.dma_start(bn[:, c:c + 1], cols(dram["L2_gnn_" + name])).then_inc(loaded, 16)
                eng.wait_ge(loaded, 16 * 11)

            @block.vector
            def _(eng):
                eng.wait_ge(loaded, 16 * 11)

                def normalise(i, c, g):
                    eng.wait_ge(spread[c], i + 1)
                    eng.wait_ge(made[c], i)
                    eng.tensor_tensor(h[:, c, :], acc[:, bass.ds(g * GC, GC)], pz[c][:, :], ALU.mult).then_inc(normed[c], 1)

                normalise(0, 0, 0)
                for i, c, g, following in groups_ahead(eng):
                    for group in following:
                        normalise(*group)
                    width = GC if following else LASTN
                    eng.wait_ge(made[c], i + 1)
                    eng.scalar_tensor_tensor(out=hx[:, bass.ds(g * GC, GC)], in0=po[c][:, :], scalar=bo[:, 0:1],
                                             in1=x_T[:, bass.ds(g * GC, GC)], op0=ALU.add, op1=ALU.add).then_inc(used[c], 1)
                    eng.wait_ge(used[c], i + 1)
                    mark(eng, marks)
                    eng.bn_stats(stats[:, bass.ds(g, 1), :].rearrange("p a s -> p (a s)"), hx[:, bass.ds(g * GC, width)]).then_inc(counted, 1)
                eng.wait_ge(counted, NG)

            @block.scalar
            def _(eng):
                for i, c, g in groups(eng):
                    eng.wait_ge(spread[c], i)
                    mark(eng, marks)
                    eng.activation(z[:, c, :], acc_z[0:H, bass.ds(g * GC, GC)], ACT.Copy).then_inc(z_in[c], 1)

            @block.tensor
            def _(eng):
                def spread_out(i, c, g):
                    eng.wait_ge(z_in[c], i + 1)
                    eng.wait_ge(normed[c], i)
                    eng.matmul(pz[c][:, :], net.expand[0:H, :], z[:, c, :], start=True, stop=True).then_inc(spread[c], 1)

                eng.wait_ge(loaded, 16 * 11)
                spread_out(0, 0, 0)
                for i, c, g, following in groups_ahead(eng):
                    for group in following:
                        spread_out(*group)
                    eng.wait_ge(normed[c], i + 1)
                    eng.wait_ge(used[c], i)
                    eng.matmul(po[c][:, :], wo[:, :], h[:, c, :], start=True, stop=True).then_inc(made[c], 1)
        batch_coefficients("a_", bn[:, 0:1], bn[:, 1:2])

        hid, relu, counted2 = n.sem("hid"), n.sem("relu"), n.sem("counted2")
        scaled, made2, used2 = (n.sems(s, 2) for s in ("scaled", "made2", "used2"))
        with nc.Block() as block:
            @block.vector
            def _(eng):
                def scale(i, c, g):
                    eng.wait_ge(used2[c], i)
                    eng.tensor_scalar(h[:, c, :], hx[:, bass.ds(g * GC, GC)], coef[:, 0:1], coef[:, 1:2], ALU.mult, ALU.add).then_inc(scaled[c], 1)

                scale(0, 0, 0)
                for i, c, g, following in groups_ahead(eng):
                    for group in following:
                        scale(*group)
                    width = GC if following else LASTN
                    eng.wait_ge(scaled[c], i + 1)
                    eng.wait_ge(made2[c], i + 1)
                    eng.scalar_tensor_tensor(out=hx[:, bass.ds(g * GC, GC)], in0=po[c][:, :], scalar=b2[:, 0:1],
                                             in1=h[:, c, :], op0=ALU.add, op1=ALU.add).then_inc(used2[c], 1)
                    eng.wait_ge(used2[c], i + 1)
                    mark(eng, marks)
                    eng.bn_stats(stats[:, bass.ds(g, 1), :].rearrange("p a s -> p (a s)"), hx[:, bass.ds(g * GC, width)]).then_inc(counted2, 1)
                eng.wait_ge(counted2, NG)

            @block.scalar
            def _(eng):
                for g in turns(eng, NG):
                    for f in range(2):
                        eng.wait_ge(hid, g * 2 + f + 1)
                        eng.activation(h1[:, f, :], p1[f][:, :], ACT.Relu, bias=b1[:, f:f + 1]).then_inc(relu, 1)

            @block.tensor
            def _(eng):
                for i, c, g in groups(eng):
                    eng.wait_ge(scaled[c], i + 1)
                    for f in range(2):
                        eng.matmul(p1[f][:, :], w1[:, f, :], h[:, c, :], start=True, stop=True).then_inc(hid, 1)
                    eng.wait_ge(used2[c], i)
                    for f in range(2):
                        eng.wait_ge(relu, g * 2 + f + 1)
                        mm = eng.matmul(po[c][:, :], w2[:, f, :], h1[:, f, :], start=(f == 0), stop=(f == 1))
                    mm.then_inc(made2[c], 1)
        batch_coefficients("b_", bn[:, 2:3], bn[:, 3:4])

        PER = 1 + LN_STEPS
        y = h1[:, 0, :].rearrange("p (t d) -> p t d", d=D)
        rs, rm, rstd = n.sb("rs", [P, 4, 6]), n.sb("rm", [P, 4, 2]), n.sb("rstd", [P, 4])
        dve, rooted = n.sem("dve3"), n.sem("rooted")
        scaled, turned, used = (n.sems(s, 2) for s in ("scaled3", "turned3", "used3"))
        with nc.Block() as block:
            @block.vector
            def _(eng):
                for i, c, g in groups(eng):
                    mine = x_row[:, bass.ds(g * 4, 4), :]
                    steps = Steps(eng, dve, g, PER)
                    eng.wait_ge(turned[c], i + 1)
                    steps.done(eng.tensor_tensor(y, po[c][:, :].rearrange("p (t d) -> p t d", d=D), mine, ALU.add))
                    steps.settle()
                    mark(eng, used[c])
                    layer_norm(eng, steps, y, rs, rm, rstd, mine, marks, rooted, g + 1, 1e-5)
                    mark(eng, marks)
                    steps.end()

            @block.scalar
            def _(eng):
                def scale(i, c, g):
                    eng.wait_ge(turned[c], i)
                    mark(eng, marks)
                    eng.activation(h[:, c, :], hx[:, bass.ds(g * GC, GC)], ACT.Identity, bias=coef[:, 1:2], scale=coef[:, 0:1]).then_inc(scaled[c], 1)

                scale(0, 0, 0)
                for i, c, g, following in groups_ahead(eng):
                    for group in following:
                        scale(*group)
                    eng.wait_ge(dve, g * PER + 1 + 9)
                    eng.activation(rstd[:, :], rstd[:, :], ACT.Sqrt).then_inc(rooted, 1)

            @block.tensor
            def _(eng):
                for i, c, g in groups(eng):
                    eng.wait_ge(scaled[c], i + 1)
                    eng.wait_ge(used[c], i)
                    for j in range(4):
                        mm = eng.transpose(po[c][:, j * P:(j + 1) * P], h[:, c, j * P:(j + 1) * P], net.ident[:, :])
                    mm.then_inc(turned[c], 1)


def hyperbolic(net, x_row, kvm, m_parts):
    nc, dram = net.nc, net.dram
    n = net.scope("hy_")
    CT = NT // 4
    with n:
        xx = n.sb("xx", [P, NT, D])
        m = n.sb("m", [P, 2, CT, D])
        three = n.sb("three", [P, 2, CT, 3, D], BF16)
        norm, y, th, f = (n.sb(s, [P, NT]) for s in ("norm", "y", "th", "f"))
        c, most = n.sb("c", [P, 2]), n.sb("most", [P, 1])
        loaded, dve, act, splits, marks = (n.sem(s) for s in ("loaded", "dve", "act", "splits", "marks"))
        stored = n.sems("stored", 2)

        def chunks(eng):
            for i in turns(eng, 2):
                yield i, 0, i * 2
                yield i, 1, i * 2 + 1

        chunk_rows = lambda table, q: table[bass.ds(q * (CT * P), CT * P), :].rearrange("(t p) d -> p t d", p=P)
        with nc.Block() as block:
            @block.sync
            def _(eng):
                eng.dma_start(c[:, 0:1], everywhere(dram["L3_gnn_c_mag"], 1)).then_inc(loaded, 16)
                for i, buf, q in chunks(eng):
                    eng.wait_ge(splits, q * SPLIT_STEPS + 1)
                    mark(eng, marks)
                    eng.dma_start(chunk_rows(kvm, q)[:, :, 2 * D:3 * D], xx[:, bass.ds(q * CT, CT), :]).then_inc(stored[buf], 16)
                    eng.wait_ge(splits, q * SPLIT_STEPS + SPLIT_STEPS)
                    mark(eng, marks)
                    eng.dma_start(chunk_rows(m_parts, q), three[:, buf].rearrange("p t c d -> p t (c d)")).then_inc(stored[buf], 16)
                for buf in range(2):
                    eng.wait_ge(stored[buf], 32 * 2)

            @block.scalar
            def _(eng):
                eng.activation(xx[:, :, :], x_row[:, :, :], ACT.Square).then_inc(act, 1)
                eng.wait_ge(dve, 5)
                eng.activation(norm[:, :], norm[:, :], ACT.Sqrt).then_inc(act, 1)
                eng.activation(c[:, 1:2], c[:, 0:1], ACT.Sqrt).then_inc(act, 1)
                eng.wait_ge(dve, 6)
                eng.activation(th[:, :], y[:, :], ACT.Tanh).then_inc(act, 1)

            @block.vector
            def _(eng):
                eng.wait_ge(loaded, 16)
                eng.wait_ge(act, 1)
                steps = Steps(eng, dve)
                steps.done(eng.tensor_reduce(norm[:, :], xx[:, :, :], AX, ALU.add))
                steps.settle()
                steps.done(eng.tensor_scalar(norm[:, :], norm[:, :], 1e-30, None, ALU.max))
                steps.done(eng.tensor_scalar(c[:, 1:2], c[:, 0:1], -1.0, None, ALU.mult))
                steps.settle()
                steps.done(eng.tensor_tensor(c[:, 0:1], c[:, 0:1], c[:, 1:2], ALU.max))
                steps.settle()
                steps.done(eng.tensor_scalar(c[:, 0:1], c[:, 0:1], 1e-15, None, ALU.max))
                eng.wait_ge(act, 3)
                steps.done(eng.tensor_scalar(y[:, :], norm[:, :], c[:, 1:2], None, ALU.mult))
                steps.settle()
                eng.wait_ge(act, 4)
                steps.done(eng.reciprocal(f[:, :], y[:, :]))
                steps.done(eng.reciprocal(most[:, :], c[:, 1:2]))
                steps.settle()
                steps.done(eng.tensor_tensor(f[:, :], f[:, :], th[:, :], ALU.mult))
                steps.done(eng.tensor_scalar(most[:, :], most[:, :], 1.0 - 1e-5, None, ALU.mult))
                steps.settle()
                steps.done(eng.tensor_tensor(norm[:, :], norm[:, :], f[:, :], ALU.mult))
                steps.settle()
                steps.done(eng.reciprocal(norm[:, :], norm[:, :]))
                steps.settle()
                steps.done(eng.tensor_scalar(norm[:, :], norm[:, :], most[:, 0:1], 1.0, ALU.mult, ALU.min))
                steps.settle()
                steps.done(eng.tensor_tensor(f[:, :], f[:, :], norm[:, :], ALU.mult))
                steps.settle()
                steps.done(eng.tensor_tensor(xx[:, :, :], x_row[:, :, :], bc(f[:, :].unsqueeze(2), [P, NT, D]), ALU.mult))
                steps.settle()
                for i, buf, q in chunks(eng):
                    steps = Steps(eng, splits, q, SPLIT_STEPS)
                    eng.wait_ge(stored[buf], i * 32)
                    mark(eng, marks)
                    split_of(eng, steps, xx[:, bass.ds(q * CT, CT), :], m[:, buf], *(three[:, buf, :, part, :] for part in range(3)), marks)


def edges_relational(net, kvm, q3_parts, m_parts, met, v_rows):
    nc, dram = net.nc, net.dram
    n = net.scope("l3_")
    with n:
        idx = n.sb("idx", [P, R, K4], I32)
        base, dst = n.sb("base", [P, R]), n.sb("dst", [P, R, K4])
        ks = n.sb("ks", [P, R, K4, 3 * D])
        qk = n.sb("qk", [P, K4, D])
        hot = n.sb("hot", [P, R, K4, P], BF16)
        pt = n.sb("pt", [P, R, K4, P], BF16)
        slab = n.sb("slab", [P, R, 3, 2 * D], BF16)
        te = n.sb("te", [TE, R, UNIT])
        tb = n.sb("tb", [6, R, UNIT], BF16)
        wk = n.sb("wk", [TE, D])
        rel = n.sb("rel", [2, D])
        cut2 = n.sb("cut2", [2, 3, D], BF16)
        wq = n.sb("wq", [6, D], BF16)
        shifted = n.sb("shifted", [P, R, K4])
        within = n.sb("within", [P, K4])
        new = n.sb("new", [P, K4, H + 1])
        turned = [n.ps(f"turned{b}", [P, K4, P], BF16) for b in range(2)]
        q = [n.ps(f"q{b}", [P, K4, 2 * D]) for b in range(2)]
        kadd = [n.ps(f"kadd{b}", [P, K4, D]) for b in range(2)]
        got = n.gather_sems("got", R)
        idx_in, base_in, hot_in, slab_in, turned_in, pt_in, q_in, te_in, v_out, used, squared, shift_in, keyed = (n.sems(x, R) for x in (
            "idx_in", "base_in", "hot_in", "slab_in", "turned_in", "pt_in", "q_in", "te_in", "v_out", "used", "squared", "shift_in", "keyed"))
        zeroed, loaded, cut, placed, dve, k_in = (n.sem(x) for x in ("zeroed", "loaded", "cut", "placed", "dve", "k_in"))
        marks = net.marks
        PER = 5
        with nc.Block() as block:
            @block.gpsimd
            def _(eng):
                eng.memset(met[:, :, :], 0.0).then_inc(zeroed, 1)

            @block.sync
            def _(eng):
                eng.dma_start(wk[0:32, :], dram["L3_gnn_Wt"]).then_inc(loaded, 16)
                eng.dma_start(wk[32:33, :], dram["L3_gnn_bt"].rearrange("(o d) -> o d", o=1)).then_inc(loaded, 16)
                for t in range(2):
                    eng.dma_start(wk[34 - t:35 - t, :], dram["L3_gnn_rel_k"][t:t + 1, :]).then_inc(loaded, 16)
                eng.dma_start(rel[:, :], dram["L3_gnn_rel_q"]).then_inc(loaded, 16)
                eng.wait_ge(cut, SPLIT_STEPS)
                for c in range(3):
                    eng.dma_start(wq[c:c + 1, :], cut2[1:2, c, :]).then_inc(placed, 16)
                    eng.dma_start(wq[3 + c:4 + c, :], cut2[0:1, c, :]).then_inc(placed, 16)
                eng.wait_ge(placed, 16 * 6)

            @block.vector
            def _(eng):
                eng.wait_ge(loaded, 16 * 5)
                steps = Steps(eng, cut)
                split(eng, steps, rel[:, :], cut2[:, 0, :], cut2[:, 1, :], cut2[:, 2, :])

        with nc.Block() as block:
            @block.sync
            def _(eng):
                regs = visit_registers(net, eng)
                for i in turns(eng, turn_count(net, eng)):
                    visit = look_up(net, eng, regs, i)
                    for b in range(R):
                        unit, at = visit[b]
                        source_loads(net, eng, i, b, unit, idx, idx_in, got)
                        visit_loads(net, eng, i, b, unit, dst, base, base_in, shift_in)
                        eng.wait_ge(used[b], i)
                        mark(eng, marks)
                        eng.dma_start(slab[:, b, :, 0:D], q3_parts[bass.ds(at, P), :].rearrange("p (c d) -> p c d", d=D)).then_inc(slab_in[b], 16)
                        eng.dma_start(slab[:, b, :, D:2 * D], m_parts[bass.ds(at, P), :].rearrange("p (c d) -> p c d", d=D)).then_inc(slab_in[b], 16)
                        eng.dma_start(te[0:33, b, :], dram["te"][:, bass.ds(unit * UNIT, UNIT)]).then_inc(te_in[b], 16)
                        eng.dma_start(te[33:35, b, :], net.type_rows[:, bass.ds(unit * UNIT, UNIT)]).then_inc(te_in[b], 16)
                        eng.dma_start(tb[:, b, :], net.parts[TB - 6:TB, bass.ds(unit * UNIT, UNIT)]).then_inc(te_in[b], 16)

            @block.gpsimd
            def _(eng):
                for i in turns(eng, turn_count(net, eng)):
                    for b in range(R):
                        eng.wait_ge(used[b], i)
                        eng.wait_ge(v_out[b], i * 16)
                        gather_unit(eng, marks, i, b, ks, kvm, idx, idx_in, got)

            @block.vector
            def _(eng):
                def build(i, b):
                    eng.wait_ge(base_in[b], i * 32 + 32)
                    eng.tensor_scalar(shifted[:, b, :], dst[:, b, :], base[:, b:b + 1], None, ALU.subtract).then_inc(shift_in[b], 1)
                    eng.wait_ge(pt_in[b], i)
                    eng.wait_ge(shift_in[b], i + 1)
                    eng.tensor_tensor(hot[:, b], bc(net.iota[:, :].unsqueeze(1), [P, K4, P]),
                                      bc(shifted[:, b, :].unsqueeze(2), [P, K4, P]), ALU.is_equal).then_inc(hot_in[b], 1)

                def meet(i, b, unit):
                    u4 = bass.ds(unit * K4, K4)
                    steps = Steps(eng, dve, i * R + b, PER)
                    mk = ks[:, b, :, 2 * D:3 * D]
                    steps.done(eng.scalar_tensor_tensor(out=within[:, :], in0=shifted[:, b, :], scalar=float(1 - P), in1=shifted[:, b, :],
                                                        op0=ALU.add, op1=ALU.mult))
                    eng.wait_ge(q_in[b], i + 1)
                    eng.wait_ge(got[b], i * 64 + 64)
                    eng.tensor_tensor(mk, mk, q[b % 2][:, :, D:2 * D], ALU.subtract).then_inc(squared[b], 1)
                    eng.wait_ge(k_in, i * R + b + 1)
                    mark(eng, marks)
                    eng.tensor_tensor(ks[:, b, :, 0:D], ks[:, b, :, 0:D], kadd[b % 2][:, :, :], ALU.add).then_inc(keyed[b], 1)
                    eng.wait_ge(keyed[b], i + 1)
                    steps.done(eng.tensor_tensor(qk[:, :, :], q[b % 2][:, :, 0:D], ks[:, b, :, 0:D], ALU.mult))
                    steps.settle()
                    steps.done(eng.tensor_reduce(new[:, :, 0:H], qk[:, :, :].rearrange("p k (h c) -> p k h c", h=H), AX, ALU.add))
                    eng.wait_ge(squared[b], i * 2 + 2)
                    steps.done(eng.tensor_reduce(new[:, :, H:H + 1], mk.unsqueeze(2), AX, ALU.add))
                    steps.settle()
                    steps.done(eng.scalar_tensor_tensor(out=new[:, :, :], in0=bc(within[:, :].unsqueeze(2), [P, K4, H + 1]), scalar=0.0,
                                                        in1=new[:, :, :], op0=ALU.is_le, op1=ALU.mult))
                    steps.settle()
                    eng.tensor_tensor(met[:, u4, :], met[:, u4, :], new[:, :, :], ALU.add).then_inc(used[b], 1)
                    eng.wait_ge(used[b], i + 1)
                    steps.end()

                regs = visit_registers(net, eng)
                for b in range(3):
                    build(0, b)
                for i, final in rolling(eng, last_turn(net, eng)):
                    visit = look_up(net, eng, regs, i)
                    for b in range(R):
                        meet(i, b, visit[b][0])
                        for visit_later in later(i, b, 3, final):
                            build(*visit_later)
                mark(eng, marks)

            @block.scalar
            def _(eng):
                regs = visit_registers(net, eng)
                last = last_turn(net, eng)
                for b in range(2):
                    copy_turned(eng, marks, 0, b, turned, turned_in, pt, pt_in, q_in)
                for i, final in rolling(eng, last):
                    visit = look_up(net, eng, regs, i)
                    for b in range(R):
                        unit = visit[b][0]
                        for visit_later in later(i, b, 2, final):
                            copy_turned(eng, marks, *visit_later, turned, turned_in, pt, pt_in, q_in)
                        mk = ks[:, b, :, 2 * D:3 * D]
                        eng.wait_ge(squared[b], i * 2 + 1)
                        eng.activation(mk, mk, ACT.Square).then_inc(squared[b], 1)
                        eng.dma_start(v_rows[bass.ds(unit * UNIT, UNIT), :].rearrange("(p k) d -> p k d", k=K4),
                                      ks[:, b, :, D:2 * D]).then_inc(v_out[b], 16)
                for b in range(R):
                    eng.wait_ge(v_out[b], (last + 1) * 16)
                mark(eng, marks)

            @block.tensor
            def _(eng):
                def hand_out(i, b):
                    eng.wait_ge(pt_in[b], i + 1)
                    eng.wait_ge(slab_in[b], i * 32 + 32)
                    eng.wait_ge(used[(b + 2) % R], i + (1 if b >= 2 else 0))
                    for k in range(K4):
                        for c in range(3):
                            eng.matmul(q[b % 2][:, k, :], pt[:, b, k, :], slab[:, b, c, :], start=(c == 0), stop=False, skip_group_check=True)
                        mm = eng.matmul(q[b % 2][:, k, 0:D], tb[:, b, k * P:(k + 1) * P], wq[:, :], start=False, stop=True, skip_group_check=True)
                    mm.then_inc(q_in[b], 1)

                def key_sums(i, b):
                    eng.wait_ge(te_in[b], i * 48 + 48)
                    eng.wait_ge(keyed[(b + 2) % R], i + (1 if b >= 2 else 0))
                    for k in range(K4):
                        mm = eng.matmul(kadd[b % 2][:, k, :], te[:, b, k * P:(k + 1) * P], wk[:, :], start=True, stop=True)
                    mm.then_inc(k_in, 1)

                for b in range(2):
                    turn_hot(eng, 0, b, hot, hot_in, net.ident_b[:, :], turned, turned_in, pt_in)
                key_sums(0, 0)
                hand_out(0, 0)
                for i, final in rolling(eng, last_turn(net, eng)):
                    for b in range(R):
                        for visit in later(i, b, 2, final):
                            turn_hot(eng, *visit, hot, hot_in, net.ident_b[:, :], turned, turned_in, pt_in)
                        for visit in later(i, b, 1, final):
                            key_sums(*visit)
                            hand_out(*visit)


def logits(net, met, dot, dec, dec_rows):
    nc, dram = net.nc, net.dram
    n = net.scope("lg_")
    with n:
        small = n.sb("small", [P, 6, H])
        far = n.sb("far", [P, NU * K4, H])
        dist = n.sb("dist", [P, NU * K4, 1])
        loaded, dve, act = n.sem("loaded"), n.sem("dve"), n.sem("act")
        every = [P, NU * K4, H]
        with nc.Block() as block:
            @block.sync
            def _(eng):
                for c, name in enumerate(("decay_scale", "logit_alpha", "hyp_beta")):
                    eng.dma_start(small[:, c, :], everywhere(dram["L3_gnn_" + name], H)).then_inc(loaded, 16)
                eng.dma_start(dec[:, :, :].rearrange("p t h -> p (t h)"), dec_rows).then_inc(loaded, 16)
                eng.wait_ge(loaded, 64)

            @block.scalar
            def _(eng):
                eng.wait_ge(loaded, 64)
                eng.activation(dec[:, :, :], dec[:, :, :], ACT.Tanh).then_inc(act, 1)
                eng.activation(small[:, 3, :], small[:, 1, :], ACT.Exp, scale=-1.0).then_inc(act, 1)
                eng.wait_ge(dve, 1)
                eng.activation(dec[:, :, :], dec[:, :, :], ACT.Exp).then_inc(act, 1)
                eng.activation(dist[:, :, :], met[:, :, H:H + 1], ACT.Sqrt).then_inc(act, 1)

            @block.vector
            def _(eng):
                steps = Steps(eng, dve)
                eng.wait_ge(loaded, 64)
                eng.wait_ge(act, 2)
                steps.done(eng.tensor_tensor(dec[:, :, :], dec[:, :, :], bc(small[:, 0, :].unsqueeze(1), every), ALU.mult))
                steps.done(eng.tensor_scalar(small[:, 3, :], small[:, 3, :], 1.0, None, ALU.add))
                steps.settle()
                steps.done(eng.reciprocal(small[:, 4, :], small[:, 3, :]))
                steps.settle()
                steps.done(eng.tensor_scalar(small[:, 5, :], small[:, 4, :], -1.0, 1.0, ALU.mult, ALU.add))
                steps.done(eng.tensor_scalar(small[:, 3, :], small[:, 4, :], 1.0 / DH ** 0.5, None, ALU.mult))
                steps.settle()
                steps.done(eng.tensor_tensor(small[:, 5, :], small[:, 5, :], small[:, 2, :], ALU.mult))
                steps.done(eng.tensor_tensor(dot[:, :, :], met[:, :, 0:H], bc(small[:, 3, :].unsqueeze(1), every), ALU.mult))
                steps.settle()
                eng.wait_ge(act, 4)
                steps.done(eng.tensor_tensor(far[:, :, :], bc(dist[:, :, :], every), bc(small[:, 5, :].unsqueeze(1), every), ALU.mult))
                steps.settle()
                steps.done(eng.tensor_tensor(dot[:, :, :], dot[:, :, :], far[:, :, :], ALU.subtract))
                steps.settle()
                steps.done(eng.tensor_tensor(dot[:, :, :], dot[:, :, :], dec[:, :, :], ALU.mult))


def segment_softmax(net, dot):
    nc, dram = net.nc, net.dram
    n = net.scope("sm_")
    last = CE - 1
    with n:
        lt = n.sb("lt", [P, CE])
        pen = n.sb("pen", [P, CE + 1])
        run = n.sb("run", [P, CE])
        best = n.sb("best", [P, CE])
        stage = n.sb("stage", [P, K4, P])
        edge_dst = n.sb("edge_dst", [P, 2])
        pair = n.sb("pair", [P, 2])
        carry = n.sb("carry", [H, 3, CH])
        start = n.sb("start", [P, 1])
        turned = n.ps("turned", [P, K4, P])
        loaded, staged, turned_s, placed, marks, dve = (n.sem(s) for s in ("loaded", "staged", "turned_s", "placed", "marks", "dve"))
        cells = net.table("cells", (2, P, 2))
        carried = net.table("carried", (2, CH, H))
        chunks = net.dst_rows.rearrange("(c e) -> c e", c=CH)
        view = dot[:, :, :].rearrange("p (c j k) h -> p c j k h", c=CH, k=K4)
        with nc.Block() as block:
            @block.gpsimd
            def _(eng):
                eng.memset(edge_dst[:, :], -1.0).then_inc(marks, 1)

            @block.sync
            def _(eng):
                for c in range(CH):
                    eng.dma_start(best[c * H:(c + 1) * H, :], bc(chunks[c:c + 1, :], [H, CE])).then_inc(loaded, 16)
                eng.wait_ge(marks, 1)
                for c in range(1, CH):
                    eng.dma_start(edge_dst[c * H:(c + 1) * H, 0:1], bc(chunks[c - 1:c, last:CE], [H, 1])).then_inc(loaded, 16)
                for c in range(CH - 1):
                    eng.dma_start(edge_dst[c * H:(c + 1) * H, 1:2], bc(chunks[c + 1:c + 2, 0:1], [H, 1])).then_inc(loaded, 16)
                eng.wait_ge(loaded, 16 * (3 * CH - 2))

            @block.vector
            def _(eng):
                for j in turns(eng, CU):
                    eng.wait_ge(turned_s, j)
                    mark(eng, staged)
                    for k in range(K4):
                        eng.tensor_copy(stage[:, k, :].rearrange("p (c a h) -> p c a h", a=1, h=H),
                                        view[:, :, bass.ds(j, 1), k, :]).then_inc(staged, 1)
                    eng.wait_ge(turned_s, j + 1)
                    mark(eng, placed)
                    eng.tensor_copy(lt[:, bass.ds(j * UNIT, UNIT)].rearrange("p (q k) -> p k q", k=K4), turned[:, :, :]).then_inc(placed, 1)

            @block.tensor
            def _(eng):
                for j in turns(eng, CU):
                    eng.wait_ge(placed, j * 2)
                    eng.wait_ge(staged, j * 5 + 5)
                    for k in range(K4):
                        mm = eng.transpose(turned[:, k, :], stage[:, k, :], net.ident[:, :])
                    mm.then_inc(turned_s, 1)

        with nc.Block() as block:
            @block.vector
            def _(eng):
                steps = Steps(eng, dve)
                d = best
                steps.done(eng.tensor_tensor(pen[:, 1:CE], d[:, 1:CE], d[:, 0:CE - 1], ALU.not_equal))
                steps.done(eng.tensor_tensor(pen[:, 0:1], d[:, 0:1], edge_dst[:, 0:1], ALU.not_equal))
                steps.done(eng.tensor_tensor(pen[:, CE:CE + 1], d[:, last:CE], edge_dst[:, 1:2], ALU.not_equal))
                steps.done(eng.tensor_tensor(start[:, :], d[:, 0:1], d[:, last:CE], ALU.not_equal))
                steps.settle()
                steps.done(eng.tensor_scalar(pen[:, :], pen[:, :], -BIG, None, ALU.mult))
                steps.done(eng.tensor_scalar(start[:, :], start[:, :], -BIG, None, ALU.mult))
                steps.settle()
                steps.done(eng.tensor_tensor_scan(run[:, :], pen[:, 0:CE], lt[:, :], -BIG, ALU.add, ALU.max))
                steps.done(eng.tensor_tensor(pair[:, 0:1], start[:, :], pen[:, 0:1], ALU.add))
                steps.settle()
                steps.done(eng.tensor_copy(pair[:, 1:2], run[:, last:CE]))

        def carry_over(name, at, backward):
            wrote, scanned = n.sem(name + "wrote"), n.sem(name + "scanned")
            with nc.Block() as block:
                @block.sync
                def _(eng):
                    eng.dma_start(cells[at], pair[:, :]).then_inc(wrote, 16)
                    eng.wait_ge(wrote, 16)
                    for w in range(2):
                        eng.dma_start(carry[:, w, :], cells[at, :, w:w + 1].rearrange("(c h) o -> h (c o)", h=H), allow_slow_non_contiguous=True).then_inc(wrote, 16)
                    eng.wait_ge(scanned, 2)
                    eng.dma_start(carried[at].rearrange("c h -> h c"), carry[:, 2, :], allow_slow_non_contiguous=True).then_inc(wrote, 16)
                    eng.wait_ge(wrote, 64)
                    lo, hi = (0, P - H) if backward else (H, P)
                    rows = carried[at].rearrange("c h -> (c h)").rearrange("(p o) -> p o", o=1)
                    eng.dma_start(start[lo:hi, :], rows[H:P, :] if backward else rows[0:P - H, :]).then_inc(wrote, 16)
                    eng.wait_ge(wrote, 80)

                @block.vector
                def _(eng):
                    eng.memset(start[:, :], -BIG).then_inc(scanned, 1)
                    eng.wait_ge(wrote, 48)
                    s = slice(None, None, -1) if backward else slice(None)
                    eng.tensor_tensor_scan(carry[:, 2, s], carry[:, 0, s], carry[:, 1, s], -BIG, ALU.add, ALU.max).then_inc(scanned, 1)

        carry_over("f_", 0, False)
        dve2 = n.sem("dve2")
        with nc.Block() as block:
            @block.vector
            def _(eng):
                steps = Steps(eng, dve2)
                steps.done(eng.tensor_tensor_scan(run[:, :], pen[:, 0:CE], lt[:, :], start[:, 0:1], ALU.add, ALU.max))
                steps.settle()
                steps.done(eng.tensor_tensor_scan(best[:, ::-1], pen[:, 1:CE + 1][:, ::-1], run[:, ::-1], -BIG, ALU.add, ALU.max))
                steps.done(eng.tensor_tensor(pair[:, 0:1], pair[:, 0:1], pen[:, 0:1], ALU.subtract))
                steps.settle()
                steps.done(eng.tensor_tensor(pair[:, 0:1], pair[:, 0:1], pen[:, CE:CE + 1], ALU.add))
                steps.done(eng.tensor_copy(pair[:, 1:2], best[:, 0:1]))
        carry_over("b_", 1, True)
        dve3, act = n.sem("dve3"), n.sem("act")
        with nc.Block() as block:
            @block.vector
            def _(eng):
                steps = Steps(eng, dve3)
                steps.done(eng.tensor_tensor_scan(best[:, ::-1], pen[:, 1:CE + 1][:, ::-1], run[:, ::-1], start[:, 0:1], ALU.add, ALU.max))
                steps.settle()
                steps.done(eng.tensor_tensor(lt[:, :], lt[:, :], best[:, :], ALU.subtract))

            @block.scalar
            def _(eng):
                eng.wait_ge(dve3, 2)
                eng.activation(lt[:, :], lt[:, :], ACT.Exp).then_inc(act, 1)

        staged, turned_s, placed = n.sem("staged2"), n.sem("turned2"), n.sem("placed2")
        with nc.Block() as block:
            @block.vector
            def _(eng):
                for j in turns(eng, CU):
                    eng.wait_ge(turned_s, j)
                    mark(eng, staged)
                    eng.tensor_copy(stage[:, :, :], lt[:, bass.ds(j * UNIT, UNIT)].rearrange("p (q k) -> p k q", k=K4)).then_inc(staged, 1)
                    eng.wait_ge(turned_s, j + 1)
                    mark(eng, placed)
                    for k in range(K4):
                        eng.tensor_copy(view[:, :, bass.ds(j, 1), k, :],
                                        turned[:, k, :].rearrange("p (c a h) -> p c a h", a=1, h=H)).then_inc(placed, 1)

            @block.tensor
            def _(eng):
                for j in turns(eng, CU):
                    eng.wait_ge(placed, j * 5)
                    eng.wait_ge(staged, j * 2 + 2)
                    for k in range(K4):
                        mm = eng.transpose(turned[:, k, :], stage[:, k, :], net.ident[:, :])
                    mm.then_inc(turned_s, 1)


def edges_weighted(net, ex, v_rows, acc, acc_z):
    nc = net.nc
    n = net.scope("l4_")
    with n:
        base, dst = n.sb("base", [P, R]), n.sb("dst", [P, R, K4])
        v = n.sb("v", [P, R, K4, D])
        hot = n.sb("hot", [P, R, K4, P])
        e = n.sb("e", [P, R, K4, 2, H])
        sums = [n.ps(f"sums{b}", [P, P]) for b in range(R)]
        zs = [n.ps(f"zs{b}", [2 * H, P]) for b in range(R)]
        out, out_z = n.sb("out", [P, R, P]), n.sb("out_z", [2 * H, R, P])
        base_in, v_in, hot_in, e_in, ready, summed, sums_out, added = (n.sems(x, R) for x in (
            "base_in", "v_in", "hot_in", "e_in", "ready", "summed", "sums_out", "added"))
        marks = net.marks
        with nc.Block() as block:
            @block.sync
            def _(eng):
                regs = visit_registers(net, eng)
                for i in turns(eng, turn_count(net, eng)):
                    visit = look_up(net, eng, regs, i)
                    for b in range(R):
                        visit_loads(net, eng, i, b, visit[b][0], dst, base, base_in, hot_in)
                        eng.wait_ge(summed[b], i)
                        mark(eng, marks)
                        eng.dma_start(v[:, b], v_rows[bass.ds(visit[b][0] * UNIT, UNIT), :].rearrange(
                            "(p k) d -> p k d", k=K4)).then_inc(v_in[b], 16)

            @block.vector
            def _(eng):
                def build(i, b):
                    eng.wait_ge(base_in[b], i * 32 + 32)
                    eng.wait_ge(summed[b], i)
                    hot_here(net, eng, hot, dst, base, b).then_inc(hot_in[b], 1)

                def weigh(i, b, unit):
                    u4 = bass.ds(unit * K4, K4)
                    eng.wait_ge(summed[b], i)
                    mark(eng, marks)
                    eng.tensor_tensor(e[:, b, :, 1, :], ex[:, u4, :], bc(net.type_f[:, u4].unsqueeze(2), [P, K4, H]), ALU.mult).then_inc(e_in[b], 1)
                    eng.wait_ge(v_in[b], i * 16 + 16)
                    eng.tensor_tensor(v[:, b].rearrange("p k (h c) -> p k h c", h=H),
                                      v[:, b].rearrange("p k (h c) -> p k h c", h=H),
                                      bc(ex[:, u4, :].unsqueeze(3), [P, K4, H, DH]), ALU.mult).then_inc(ready[b], 1)
                    eng.wait_ge(e_in[b], i * 2 + 1)
                    eng.tensor_tensor(e[:, b, :, 0, :], ex[:, u4, :], e[:, b, :, 1, :], ALU.subtract).then_inc(e_in[b], 1)

                regs = visit_registers(net, eng)
                for b in range(3):
                    build(0, b)
                for i, final in rolling(eng, last_turn(net, eng)):
                    visit = look_up(net, eng, regs, i)
                    for b in range(R):
                        weigh(i, b, visit[b][0])
                        for visit_later in later(i, b, 3, final):
                            build(*visit_later)
                    mark(eng, marks)

            @block.gpsimd
            def _(eng):
                regs = visit_registers(net, eng)
                for i in turns(eng, turn_count(net, eng)):
                    visit = look_up(net, eng, regs, i)
                    for b in range(R):
                        eng.wait_ge(sums_out[b], i * 2 + 2)
                        add_window(net, eng, i, b, visit[b][1], [(acc, out[:, b, :]), (acc_z, out_z[:, b, :])], added)

            @block.scalar
            def _(eng):
                for i in turns(eng, turn_count(net, eng)):
                    for b in range(R):
                        eng.wait_ge(summed[b], i + 1)
                        eng.wait_ge(added[b], i * 2)
                        eng.activation(out[:, b, :], sums[b][:, :], ACT.Copy).then_inc(sums_out[b], 1)
                        eng.activation(out_z[:, b, :], zs[b][:, :], ACT.Copy).then_inc(sums_out[b], 1)

            @block.tensor
            def _(eng):
                for i in turns(eng, turn_count(net, eng)):
                    for b in range(R):
                        eng.wait_ge(hot_in[b], i + 1)
                        eng.wait_ge(sums_out[b], i * 2)
                        eng.wait_ge(ready[b], i + 1)
                        mark(eng, marks)
                        for k in range(K4):
                            mm = eng.matmul(sums[b][:, :], v[:, b, k, :], hot[:, b, k, :], start=(k == 0), stop=(k == K4 - 1))
                        eng.wait_ge(e_in[b], i * 2 + 2)
                        mark(eng, marks)
                        for k in range(K4):
                            mm = eng.matmul(zs[b][:, :], e[:, b, k, :, :].rearrange("p t h -> p (t h)"), hot[:, b, k, :], start=(k == 0), stop=(k == K4 - 1))
                        mm.then_inc(summed[b], 1)


def nodes_relational(net, acc, acc_z, x_row, out):
    nc, dram = net.nc, net.dram
    n = net.scope("n3_")
    A = 3 + LN_STEPS + 2
    B = 1 + LN_STEPS + 2 + LN_STEPS
    with n:
        shares = n.sb("shares", [H, NP])
        reciprocals(net, "r3_", acc_z, shares, 2, 1e-30, None)
        wo, wf1, wf2 = n.sb("wo", [D, D]), n.sb("wf1", [D, 4, P]), n.sb("wf2", [P, 4, D])
        rows = n.sb("rows", [P, 6, D])
        bf1 = n.sb("bf1", [P, 4])
        rel_v = n.sb("rel_v", [2 * H, D])
        z, share = n.sb("z", [2 * H, 2, GC]), n.sb("share", [H, 2, GC])
        with_bo, with_be2, with_bf2 = (n.sb(s, [P, 2, 4, D]) for s in ("with_bo", "with_be2", "with_bf2"))
        agg, x4t, h = n.sb("agg", [P, GC]), n.sb("x4t", [P, GC]), n.sb("h", [P, 4, GC])
        y, y2, x4, x5 = n.sb("y", [P, 4, D]), n.sb("y2", [P, 4, D]), n.sb("x4", [P, 2, 4, D]), n.sb("x5", [P, 4, D])
        stats, moments, std = n.sb("stats", [P, 4, 6]), n.sb("moments", [P, 4, 2]), n.sb("std", [P, 4])
        pz, pr, po, pe = n.ps("pz", [P, GC]), n.ps("pr", [P, GC]), n.ps("po", [P, 4, D]), n.ps("pe", [P, 4, D])
        pf = [n.ps(f"pf{f}", [P, GC]) for f in range(4)]
        pt = pz
        masked, loaded, before, after, spread, made, turned, x4t_in, hid, gelu, fed, marks, stored = (n.sem(s) for s in (
            "masked", "loaded", "before", "after", "spread", "made", "turned", "x4t_in", "hid", "gelu", "fed", "marks", "stored"))
        rooted, rooted_after = n.sem("rooted"), n.sem("rooted_after")
        z_in, sums_in, bf2_in, done = n.sem("z_in"), n.sem("sums_in"), n.sem("bf2_in"), n.sems("done", 2)
        NL = 6 + 3 + 4 + 2
        row = lambda c: bc(rows[:, c, :].unsqueeze(1), [P, 4, D])
        with nc.Block() as block:
            @block.sync
            def _(eng):
                eng.dma_start(wo[:, :], dram["L3_gnn_Wo"]).then_inc(loaded, 16)
                eng.dma_start(wf1[:, :, :], dram["L3_gnn_Wf1"].rearrange("d (f o) -> d f o", f=4)).then_inc(loaded, 16)
                eng.dma_start(wf2[:, :, :], dram["L3_gnn_Wf2"].rearrange("(f o) d -> o f d", f=4)).then_inc(loaded, 16)
                for f in range(4):
                    eng.dma_start(bf1[:, f:f + 1], cols(dram["L3_gnn_bf1"][f * P:(f + 1) * P])).then_inc(loaded, 16)
                for c, name in enumerate(("bo", "g1", "be1", "g2", "be2", "bf2")):
                    eng.dma_start(rows[:, c, :], everywhere(dram["L3_gnn_" + name], D)).then_inc(loaded, 16)
                for t in range(2):
                    eng.dma_start(rel_v[t * H:(t + 1) * H, :], bc(dram["L3_gnn_rel_v"][t:t + 1, :], [H, D])).then_inc(loaded, 16)
                for g in turns(eng, NG - 1):
                    eng.wait_ge(after, g * B + B)
                    mark(eng, marks)
                    eng.dma_start(rows_of(out, g * GC), x_row[:, bass.ds(g * 4, 4), :]).then_inc(stored, 16)
                eng.wait_ge(after, NG * B)
                full = N // P
                assert full == (NG - 1) * 4
                eng.dma_start(out[full * P:N, :], x_row[0:N - full * P, full, :]).then_inc(stored, 16)
                eng.wait_ge(stored, 16 * NG)

            @block.gpsimd
            def _(eng):
                def prepare(i, c, g):
                    mine = x_row[:, bass.ds(g * 4, 4), :]
                    eng.wait_ge(spread, g)
                    mark(eng, marks)
                    eng.tensor_copy(z[:, c, :], acc_z[:, bass.ds(g * GC, GC)]).then_inc(z_in, 1)
                    eng.tensor_copy(share[:, c, :], shares[:, bass.ds(g * GC, GC)]).then_inc(z_in, 1)
                    eng.wait_ge(done[c], i)
                    mark(eng, marks)
                    eng.tensor_tensor(with_bo[:, c], mine, row(0), ALU.add).then_inc(sums_in, 1)
                    eng.tensor_tensor(with_be2[:, c], mine, row(4), ALU.add).then_inc(sums_in, 1)

                eng.wait_ge(loaded, 16 * NL)
                prepare(0, 0, 0)
                for i, c, g, following in groups_ahead(eng):
                    for group in following:
                        prepare(*group)
                    eng.wait_ge(before, g * A + A)
                    mark(eng, marks)
                    eng.tensor_tensor(with_bf2[:, c], x4[:, c], row(5), ALU.add).then_inc(bf2_in, 1)

            @block.vector
            def _(eng):
                def come_up(i, c, g):
                    steps = Steps(eng, before, g, A)
                    eng.wait_ge(spread, g + 1)
                    steps.done(eng.tensor_tensor(agg[:, :], acc[:, bass.ds(g * GC, GC)], pr[:, :], ALU.add))
                    steps.settle()
                    steps.done(eng.tensor_tensor(agg[:, :], agg[:, :], pz[:, :], ALU.mult))
                    eng.wait_ge(sums_in, g * 2 + 2)
                    eng.wait_ge(made, g + 1)
                    steps.done(eng.tensor_tensor(y[:, :, :], po[:, :, :], with_bo[:, c], ALU.add))
                    steps.settle()
                    layer_norm(eng, steps, y, stats, moments, std, x4[:, c], marks, rooted, g + 1, 1e-5)
                    steps.done(eng.tensor_tensor(x4[:, c], x4[:, c], row(1), ALU.mult))
                    steps.settle()
                    steps.done(eng.tensor_tensor(x4[:, c], x4[:, c], row(2), ALU.add))
                    steps.settle()
                    steps.end()

                eng.wait_ge(loaded, 16 * NL)
                eng.tensor_tensor(rel_v[:, :], rel_v[:, :], net.expand[:, :], ALU.mult).then_inc(masked, 1)
                come_up(0, 0, 0)
                for i, c, g, following in groups_ahead(eng):
                    for group in following:
                        come_up(*group)
                    steps = Steps(eng, after, g, B)
                    eng.wait_ge(bf2_in, g + 1)
                    eng.wait_ge(fed, g + 1)
                    steps.done(eng.tensor_tensor(y2[:, :, :], pe[:, :, :], with_bf2[:, c], ALU.add))
                    steps.settle()
                    layer_norm(eng, steps, y2, stats, moments, std, x5, marks, rooted_after, g * 2 + 1, 1e-5)
                    steps.done(eng.tensor_tensor(x5[:, :, :], x5[:, :, :], row(3), ALU.mult))
                    steps.settle()
                    steps.done(eng.tensor_tensor(y2[:, :, :], x5[:, :, :], with_be2[:, c], ALU.add))
                    steps.settle()
                    mark(eng, done[c])
                    layer_norm(eng, steps, y2, stats, moments, std, x_row[:, bass.ds(g * 4, 4), :], marks, rooted_after, g * 2 + 2, 1e-5)
                    mark(eng, marks)
                    steps.end()

            @block.scalar
            def _(eng):
                def come_up(i, c, g):
                    eng.wait_ge(before, g * A + 3 + 9)
                    eng.activation(std[:, :], std[:, :], ACT.Sqrt).then_inc(rooted, 1)
                    eng.wait_ge(turned, g + 1)
                    eng.activation(x4t[:, :], pt[:, :], ACT.Copy).then_inc(x4t_in, 1)

                come_up(0, 0, 0)
                for i, c, g, following in groups_ahead(eng):
                    for f in range(4):
                        eng.wait_ge(hid, g * 4 + f + 1)
                        eng.activation(h[:, f, :], pf[f][:, :], ACT.Gelu, bias=bf1[:, f:f + 1]).then_inc(gelu, 1)
                    for group in following:
                        come_up(*group)
                    eng.wait_ge(after, g * B + 1 + 9)
                    eng.activation(std[:, :], std[:, :], ACT.Sqrt).then_inc(rooted_after, 1)
                    eng.wait_ge(after, g * B + 3 + LN_STEPS + 9)
                    eng.activation(std[:, :], std[:, :], ACT.Sqrt).then_inc(rooted_after, 1)

            @block.tensor
            def _(eng):
                def come_up(i, c, g):
                    eng.wait_ge(z_in, g * 2 + 2)
                    eng.wait_ge(x4t_in, g)
                    eng.wait_ge(before, g * A)
                    eng.matmul(pz[:, :], net.expand[0:H, :], share[:, c, :], start=True, stop=True)
                    eng.matmul(pr[:, :], rel_v[:, :], z[:, c, :], start=True, stop=True).then_inc(spread, 1)
                    eng.wait_ge(before, g * A + 2)
                    for j in range(4):
                        mm = eng.matmul(po[:, j, :], agg[:, j * P:(j + 1) * P], wo[:, :], start=True, stop=True)
                    mm.then_inc(made, 1)

                def turn(i, c, g):
                    eng.wait_ge(before, g * A + A)
                    for j in range(4):
                        mm = eng.transpose(pt[:, j * P:(j + 1) * P], x4[:, c, j, :], net.ident[:, :])
                    mm.then_inc(turned, 1)

                eng.wait_ge(masked, 1)
                come_up(0, 0, 0)
                turn(0, 0, 0)
                for i, c, g, following in groups_ahead(eng):
                    eng.wait_ge(x4t_in, g + 1)
                    for f in range(4):
                        eng.matmul(pf[f][:, :], wf1[:, f, :], x4t[:, :], start=True, stop=True).then_inc(hid, 1)
                    for group in following:
                        come_up(*group)
                    eng.wait_ge(gelu, g * 4 + 4)
                    eng.wait_ge(after, g * B)
                    for j in range(4):
                        for f in range(4):
                            mm = eng.matmul(pe[:, j, :], h[:, f, j * P:(j + 1) * P], wf2[:, f, :], start=(f == 0), stop=(f == 3))
                    mm.then_inc(fed, 1)
                    for group in following:
                        turn(*group)


def graph_network(nc, dram, out):
    net = Net(nc, ExitStack(), dram)
    with net:
        net.marks = net.lasting.enter_context(nc.semaphore("marks"))
        x_row = net.sb("x_row", [P, NT, D])
        tabs = [net.table(f"tab{k}", (TR, D)) for k in range(K4)]
        setup(net, x_row, tabs)
        hs, x1 = net.table("hs", (NP, D)), net.table("x1", (NP, D))
        x1_parts, q_parts = net.table("x1_parts", (NP, 3 * D), BF16), net.table("q_parts", (NP, 3 * D), BF16)
        kv, kvm = net.table("kv", (NP, 2 * D)), net.table("kvm", (NP, 3 * D))
        q3_parts, m_parts = net.table("q3_parts", (NP, 3 * D), BF16), net.table("m_parts", (NP, 3 * D), BF16)
        v_rows = net.table("v_rows", (EP, D))
        dec_rows = net.table("dec_rows", (P, NU * K4 * H))

        layer = net.scope("a_")
        with layer:
            acc, hs_row = layer.sb("acc", [P, NP]), layer.sb("hs_row", [P, NT, D])
            clear(net, "c0_", [acc])
            project(net, "p0_", ["L0_gnn_W"], hs, x_row, scale=net.dinv, keep=hs_row)
            edges_gcn(net, hs, acc, dec_rows)
            nodes_gcn(net, acc, hs_row, x_row, x1, x1_parts)

        layer = net.scope("b_")
        with layer:
            acc = layer.sb("acc", [P, NP])
            clear(net, "c1_", [acc])
            edges_gated(net, x1, x1_parts, acc, tabs)
            nodes_gated(net, acc, tabs, x_row)

        layer = net.scope("c_")
        with layer:
            acc, acc_z, x_T = layer.sb("acc", [P, NP]), layer.sb("acc_z", [H, NP]), layer.sb("x_T", [P, NP])
            clear(net, "c2_", [acc, acc_z])
            project(net, "p2_", ["L2_gnn_Wk", "L2_gnn_Wv", "L2_gnn_Wq"], kv, x_row, x_T=x_T, parts=q_parts)
            edges_attention(net, kv, q_parts, acc, acc_z)
            nodes_attention(net, acc, acc_z, x_row, x_T)

        project(net, "p3_", ["L3_gnn_Wk", "L3_gnn_Wv", "L3_gnn_Wq"], kvm, x_row, parts=q3_parts)
        hyperbolic(net, x_row, kvm, m_parts)
        layer = net.scope("d_")
        with layer:
            dot = layer.sb("dot", [P, NU * K4, H])
            first = net.scope("e_")
            with first:
                dec, met = first.sb("dec", [P, NU * K4, H]), first.sb("met", [P, NU * K4, H + 1])
                edges_relational(net, kvm, q3_parts, m_parts, met, v_rows)
                logits(net, met, dot, dec, dec_rows)
            segment_softmax(net, dot)
            acc, acc_z = layer.sb("acc", [P, NP]), layer.sb("acc_z", [2 * H, NP])
            clear(net, "c3_", [acc, acc_z])
            edges_weighted(net, dot, v_rows, acc, acc_z)
            nodes_relational(net, acc, acc_z, x_row, out)


def kernel(**inputs):
    import concourse.bacc as bacc
    from concourse.bass_utils import run_bass_kernel_spmd

    a = {k: np.asarray(v) for k, v in inputs.items()}
    tail = EP - E
    tiled = lambda v: np.ascontiguousarray(v.reshape(NU, P, K4).transpose(1, 0, 2).reshape(P, NU * K4))
    by_tile = lambda v: np.ascontiguousarray(v.reshape(NU, P, K4, -1).transpose(3, 0, 2, 1).reshape(-1, EP))
    src = np.pad(a["src"], (0, tail), constant_values=N)
    dst = np.pad(a["dst"], (0, tail), constant_values=N)
    te = by_tile(np.pad(a["edge_attr_32"], ((0, tail), (0, 0))))
    types = np.pad(a["edge_type_2"], (0, tail))
    arrays = {
        "x": np.pad(a["x"], ((0, NP - N), (0, 0))),
        "src_row": src, "dst_row": dst, "src_tiles": tiled(src), "dst_tiles": tiled(dst),
        "type_tiles": tiled(types), "type_row": by_tile(types)[0], "weight_row": by_tile(np.pad(a["edge_weight"], (0, tail)))[0],
        "ea": np.pad(a["edge_attr_128"], ((0, tail), (0, 0))),
        "te": np.concatenate([te, np.ones((1, EP), np.float32)]),
        "one": np.ones((1,), np.float32),
    }
    for name, shape in WEIGHTS.items():
        arrays[name] = a[name].reshape(shape)
    nc = bacc.Bacc("TRN2", target_bir_lowering=False, num_devices=1)
    dram = {k: nc.dram_tensor(f"in_{k}", v.shape, mybir.dt.from_np(v.dtype), kind="ExternalInput").ap() for k, v in arrays.items()}
    out = nc.dram_tensor("out", (N, D), F32, kind="ExternalOutput").ap()
    graph_network(nc, dram, out)
    r = run_bass_kernel_spmd(nc, [{f"in_{k}": v for k, v in arrays.items()}], core_ids=[0])
    return r.results[0]["out"]
```
